# Optimizing a Trainium2 kernel written in Bass

```python
import numpy as np
import jax
import jax.numpy as jnp

def _softmax(x, axis=-1):
    return jax.nn.softmax(x, axis=axis)

def _gelu(x):
    return jax.nn.gelu(x, approximate=True)

def _silu(x):
    return jax.nn.silu(x)

def _sigmoid(x):
    return jax.nn.sigmoid(x)

def _layernorm(x, axis=-1, eps=1e-05):
    m = jnp.mean(x, axis=axis, keepdims=True)
    v = jnp.var(x, axis=axis, keepdims=True)
    return (x - m) / jnp.sqrt(v + eps)

def _scatter_add(tgt, idx, src, axis=0):
    return tgt.at[idx].add(src)

def _segment_sum(src, seg, n):
    return jax.ops.segment_sum(src, seg, n)
kernel_name = 'mk_flamingo_gated_d1_seqx_r4_52eeda'

def setup_inputs(seed: int=0):
    np.random.seed(seed)
    _w = jnp.asarray

    def _rec_inputs():
        import jax
        import jax.numpy as jnp
        _rk = jax.random.key(seed)
        x = -0.0003929 + 0.9999 * jax.random.normal(jax.random.fold_in(_rk, 1), (16, 256, 256), jnp.float32)
        _lenS = 256 - jax.random.randint(jax.random.fold_in(_rk, 7), (16,), 0, max(1, 256 // 4) + 1, jnp.int32)
        _lenS2 = 256 - jax.random.randint(jax.random.fold_in(_rk, 8), (16,), 0, max(1, 256 // 4) + 1, jnp.int32)
        _ctx_768P = jax.random.normal(jax.random.fold_in(_rk, 11), (16, 16, 192), jnp.float32)
        _ctx_768c = jax.random.dirichlet(jax.random.fold_in(_rk, 511), 0.3 * jnp.ones((16,), jnp.float32), (16, 256))
        _ctx_768t = jnp.einsum('bsk,bkd->bsd', _ctx_768c, _ctx_768P)
        _ctx_768t = _ctx_768t * jax.lax.rsqrt(jnp.mean(jnp.square(_ctx_768t)) + 1e-12) * 0.953939
        ctx_768 = -7.36909e-05 + 0.999899 * (_ctx_768t + 0.3 * jax.random.normal(jax.random.fold_in(_rk, 611), (16, 256, 192), jnp.float32))
        _g = jax.random.normal(jax.random.fold_in(_rk, 9001), (2, 1), jnp.float32)
        _g = jnp.sign(_g) * jnp.maximum(jnp.abs(_g), 1.0) + (_g == 0) * 1.0
        g_xattn = _g[0]
        g_ffn = _g[1]
        return (x, ctx_768, g_xattn, g_ffn)
    x, ctx_768, g_xattn, g_ffn = _rec_inputs()

    def _L0_xattn_setup():
        import jax, jax.numpy as jnp
        import numpy as np
        EPS = 1e-08
        key = jax.random.key(seed)
        kv, kt, k1, k2, k3, k4 = jax.random.split(key, 6)
        B, S = (16, 256)
        VD, TD, H = (256, 192, 128)
        visual_features = jax.random.normal(kv, (B, S, VD), dtype=jnp.float32)
        text_features = jax.random.normal(kt, (B, S, TD), dtype=jnp.float32)
        Wv = jax.random.normal(k1, (H, VD), dtype=jnp.float32) * (1.0 / np.sqrt(VD))
        bv = jax.random.normal(k2, (H,), dtype=jnp.float32) * 0.01
        Wt = jax.random.normal(k3, (H, TD), dtype=jnp.float32) * (1.0 / np.sqrt(TD))
        bt = jax.random.normal(k4, (H,), dtype=jnp.float32) * 0.01
        return {'visual_features': visual_features, 'text_features': text_features, 'Wv': Wv, 'bv': bv, 'Wt': Wt, 'bt': bt}
    _L0_xattn_all = _L0_xattn_setup()
    _L0_xattn_in = {k: v for k, v in _L0_xattn_all.items() if k in ('Wv', 'bv', 'Wt', 'bt')}
    del _L0_xattn_all

    def _L0_ffn_setup():
        import jax, jax.numpy as jnp
        import numpy as np
        B, S, D = (4, 1024, 256)
        H = 1024
        RH = 256
        E = 16
        K = 2
        NS = 1

        def _swiglu(x, w1, w2, w3):
            return jax.nn.silu(x @ w1) * (x @ w2) @ w3
        key = jax.random.key(seed)
        ks = jax.random.split(key, 9)
        s = 0.02
        return {'x': jax.random.normal(ks[0], (B, S, D), dtype=jnp.float32), 'router_w': jax.random.normal(ks[1], (D, E), dtype=jnp.float32) * s, 'expert_bias': jnp.zeros((E,), dtype=jnp.float32), 'shared_w1': jax.random.normal(ks[2], (NS, D, H), dtype=jnp.float32) * s, 'shared_w2': jax.random.normal(ks[3], (NS, D, H), dtype=jnp.float32) * s, 'shared_w3': jax.random.normal(ks[4], (NS, H, D), dtype=jnp.float32) * s, 'routed_w1': jax.random.normal(ks[5], (E, D, RH), dtype=jnp.float32) * s, 'routed_w2': jax.random.normal(ks[6], (E, D, RH), dtype=jnp.float32) * s, 'routed_w3': jax.random.normal(ks[7], (E, RH, D), dtype=jnp.float32) * s}
    _L0_ffn_all = _L0_ffn_setup()
    _L0_ffn_in = {k: v for k, v in _L0_ffn_all.items() if k in ('router_w', 'expert_bias', 'shared_w1', 'shared_w2', 'shared_w3', 'routed_w1', 'routed_w2', 'routed_w3')}
    del _L0_ffn_all
    return {'x': x, 'ctx_768': ctx_768, 'g_xattn': g_xattn, 'g_ffn': g_ffn, 'L0_xattn_Wv': _L0_xattn_in['Wv'], 'L0_xattn_bv': _L0_xattn_in['bv'], 'L0_xattn_Wt': _L0_xattn_in['Wt'], 'L0_xattn_bt': _L0_xattn_in['bt'], 'L0_ffn_router_w': _L0_ffn_in['router_w'], 'L0_ffn_expert_bias': _L0_ffn_in['expert_bias'], 'L0_ffn_shared_w1': _L0_ffn_in['shared_w1'], 'L0_ffn_shared_w2': _L0_ffn_in['shared_w2'], 'L0_ffn_shared_w3': _L0_ffn_in['shared_w3'], 'L0_ffn_routed_w1': _L0_ffn_in['routed_w1'], 'L0_ffn_routed_w2': _L0_ffn_in['routed_w2'], 'L0_ffn_routed_w3': _L0_ffn_in['routed_w3']}

def reference(x, ctx_768, g_xattn, g_ffn, L0_xattn_Wv, L0_xattn_bv, L0_xattn_Wt, L0_xattn_bt, L0_ffn_router_w, L0_ffn_expert_bias, L0_ffn_shared_w1, L0_ffn_shared_w2, L0_ffn_shared_w3, L0_ffn_routed_w1, L0_ffn_routed_w2, L0_ffn_routed_w3):
    import jax
    import jax.numpy as jnp

    def _L0_xattn_ref(visual_features, text_features, Wv, bv, Wt, bt):
        import jax, jax.numpy as jnp
        import numpy as np
        EPS = 1e-08
        v = jnp.einsum('bsd,hd->bsh', visual_features, Wv) + bv
        t = jnp.einsum('bsd,hd->bsh', text_features, Wt) + bt
        dots = jnp.einsum('bih,bjh->bij', v, t)
        vn = jnp.linalg.norm(v, axis=-1)
        tn = jnp.linalg.norm(t, axis=-1)
        denom = jnp.maximum(vn[:, :, None] * tn[:, None, :], EPS)
        return dots / denom

    def _L0_ffn_ref(x, router_w, expert_bias, shared_w1, shared_w2, shared_w3, routed_w1, routed_w2, routed_w3):
        import jax, jax.numpy as jnp
        import numpy as np
        B, S, D = (4, 1024, 256)
        H = 1024
        RH = 256
        E = 16
        K = 2
        NS = 1

        def _swiglu(x, w1, w2, w3):
            return jax.nn.silu(x @ w1) * (x @ w2) @ w3
        shared_out = jnp.sum(jax.vmap(lambda w1, w2, w3: _swiglu(x, w1, w2, w3))(shared_w1, shared_w2, shared_w3), axis=0)
        scores = jax.nn.sigmoid(x @ router_w)
        sel_scores = scores + expert_bias
        _, top_idx = jax.lax.top_k(sel_scores, K)
        top_scores = jnp.take_along_axis(scores, top_idx, axis=-1)
        gates = jnp.sum(jax.nn.one_hot(top_idx, E, dtype=scores.dtype) * top_scores[..., None], axis=-2)
        xf = x.reshape(-1, D)
        gf = gates.reshape(-1, E).T

        def body(acc, ws):
            w1, w2, w3, g = ws
            return (acc + _swiglu(xf, w1, w2, w3) * g[:, None], None)
        routed_out, _ = jax.lax.scan(body, jnp.zeros_like(xf), (routed_w1, routed_w2, routed_w3, gf))
        return shared_out + routed_out.reshape(x.shape)
    x = x + jnp.tanh(g_xattn[0]) * _L0_xattn_ref(_layernorm(x, axis=-1), ctx_768, L0_xattn_Wv, L0_xattn_bv, L0_xattn_Wt, L0_xattn_bt)
    x = x + jnp.tanh(g_ffn[0]) * _L0_ffn_ref(_layernorm(x, axis=-1), L0_ffn_router_w, L0_ffn_expert_bias, L0_ffn_shared_w1, L0_ffn_shared_w2, L0_ffn_shared_w3, L0_ffn_routed_w1, L0_ffn_routed_w2, L0_ffn_routed_w3)
    return x

_drawn_inputs = setup_inputs


def setup_inputs(seed=0):
    import zlib

    import numpy as np

    out = dict(_drawn_inputs(seed))
    spreads = {'L0_ffn_expert_bias': (0.0, 0.548)}
    factors = {'L0_xattn_bv': 8.0,
     'L0_xattn_bt': 45.38,
     'L0_ffn_router_w': 6.001,
     'L0_ffn_routed_w1': 4.494,
     'L0_ffn_routed_w2': 4.444,
     'L0_ffn_routed_w3': 4.441,
     'L0_ffn_shared_w1': 3.619,
     'L0_ffn_shared_w2': 3.582,
     'L0_ffn_shared_w3': 3.586}
    for name, (base, spread) in spreads.items():
        noise = np.random.default_rng([zlib.crc32(name.encode()), seed]).standard_normal(out[name].shape)
        drawn = base * np.exp(spread * noise) if base else spread * noise
        out[name] = jnp.asarray(drawn.astype(out[name].dtype))
    for name, factor in factors.items():
        out[name] = (out[name] * factor).astype(out[name].dtype)
    return out
```

```python
import concourse.bass as bass
from concourse import mybir
from contextlib import ExitStack

P = 128


def flamingo_block(nc, x, ctx_t, g_xattn, g_ffn, wv_t, bv, wt_t, bt, router_w, expert_bias,
                   shared_w1, shared_w2, shared_w3, routed_w1, routed_w2, routed_w3, out):
    F32, F16, I32, U32 = mybir.dt.float32, mybir.dt.float16, mybir.dt.int32, mybir.dt.uint32
    ALU = mybir.AluOpType
    ACT = mybir.ActivationFunctionType
    AX = mybir.AxisListType
    ds = bass.ds

    B, S, D = x.shape
    TOK = B * S
    NT = TOK // P
    CW = 512
    TPC = CW // P
    NC = TOK // CW
    KD = D // P
    TD = ctx_t.shape[0]
    KT = TD // 2
    H = wv_t.shape[1]
    E = router_w.shape[1]
    SH = shared_w1.shape[2]
    J = SH // P
    RH = routed_w1.shape[2]
    NBLK = 2 * TOK // P + E
    WE = 2 * KD * RH + (RH // P) * D
    WH = WE // 2
    W3E = 2 * KD * RH
    WSH = 2 * KD * SH + J * D
    W3S = 2 * KD * SH
    WSCALE = 64.0
    LN_EPS = 1e-5
    INV_EPS = 1e8
    TINY = 1e-30

    x_tiles = x.rearrange("b s d -> (b s) d").rearrange("(t p) d -> p t d", p=P)
    out_tiles = out.rearrange("b s d -> (b s) d").rearrange("(t p) d -> p t d", p=P)

    xrow = nc.dram_tensor("xrow", (TOK, D), F32, kind="Internal").ap()
    xtd = nc.dram_tensor("xtd", (NC * P, 2 * KD * CW), F16, kind="Internal").ap()
    slot_token = nc.dram_tensor("slot_token", (P * NBLK, 1), I32, kind="Internal").ap()
    yrow = nc.dram_tensor("yrow", (NBLK * P, D), F32, kind="Internal").ap()
    xrow_tiles = xrow.rearrange("(t p) d -> p t d", p=P)

    ctx = ExitStack()
    with ctx:
        def sb(name, shape, dt):
            return ctx.enter_context(nc.sbuf_tensor(name, shape, dt))

        def sem(name):
            return ctx.enter_context(nc.semaphore(name))

        X = sb("X", [P, NT, D], F32)
        WR = sb("WR", [P, E * 2 * WE], F16)
        WS = sb("WS", [P, 2, WSH], F16)
        XTC = sb("XTC", [P, 2, 2, KD, CW], F16)
        GS = sb("GS", [P, 2, 2, CW], F16)
        SIL = sb("SIL", [P, 2, CW], F32)
        G = sb("G", [P, 2, CW], F32)
        STAGE = sb("STAGE", [P, 2, WE], F32)
        ROWS = sb("ROWS", [P, 8, D], F32)
        XG = ROWS[:, 0:4, :]
        YS = ROWS[:, 4:8, :]
        YG = ROWS[:, :, :].rearrange("p (t k) d -> p t k d", k=2)
        XTB = sb("XTB", [P, 2, 2, KD, P], F16)
        GT = sb("GT", [P, 2, 2, RH // P, P], F16)
        ident = sb("ident", [P, P], F32)
        before = sb("before", [P, P], F32)
        ones = sb("ones", [P, P], F32)
        wv = sb("wv", [P, KD, H], F32)
        wt = sb("wt", [KT, 2, H], F32)
        rw = sb("rw", [P, KD, E], F32)
        bvc = sb("bvc", [P, 1], F32)
        btc = sb("btc", [P, 1], F32)
        bias16 = sb("bias16", [P, E], F32)
        gates_in = sb("gates_in", [P, 2], F32)
        tg = sb("tg", [P, 2], F32)
        tgs = sb("tgs", [P, 1], F32)
        st = sb("st", [P, NT, 6], F32)
        mean1 = sb("mean1", [P, NT], F32)
        var1 = sb("var1", [P, NT], F32)
        rstd1 = sb("rstd1", [P, NT], F32)
        tmp1 = sb("tmp1", [P, NT], F32)
        tn = sb("tn", [P, NT], F32)
        rt = sb("rt", [P, NT], F32)
        vn = sb("vn", [P, TPC], F32)
        rv = sb("rv", [P, TPC], F32)
        st2 = sb("st2", [P, TPC, 6], F32)
        mv2 = sb("mv2", [P, TPC, 2], F32)
        ve2 = sb("ve2", [P, TPC], F32)
        sd2 = sb("sd2", [P, TPC], F32)
        rs2 = sb("rs2", [P, TPC], F32)
        posi = sb("posi", [P, 2, NT], I32)
        sloti = sb("sloti", [P, 2, NT], I32)
        gate = sb("gate", [P, 2, NT], F32)
        tokid = sb("tokid", [P, NT], I32)
        blk_word = sb("blk_word", [1, NBLK // 4], I32)
        blk_iota = sb("blk_iota", [1, NBLK], F32)
        rev = sb("rev", [P, E], F32)
        idx = sb("idx", [P, NBLK], I32)
        zero_idx = sb("zero_idx", [P, NBLK], I32)
        ixs = sb("ixs", [P, 4, 2], I32)
        tks = sb("tks", [P, 4], I32)
        ixb = sb("ixb", [P, 4], I32)
        ixc = sb("ixc", [P, 4, 2], I32)

        arena_at = [0]

        def arena(shape):
            n = 2
            for s in shape:
                n *= s
            a = WR[:, arena_at[0]:arena_at[0] + n].bitcast(F32)
            arena_at[0] += n
            assert arena_at[0] <= E * 2 * WE
            if len(shape) == 2:
                a = a.rearrange("p (a b) -> p a b", a=shape[0])
            return a

        route_at = arena_at[0]
        CTX = arena([2, TOK])
        TT = arena([TOK])
        SHST = arena([WSH])
        SQT = arena([2, CW])
        XL = arena([TPC, D])
        XT = arena([KD, CW])
        VT = arena([CW])
        SQV = arena([CW])
        M = arena([TPC, D])
        A = arena([2, D])
        DG = arena([TPC, P])
        stage_f = STAGE[:, :, :].rearrange("p a b -> p (a b)")
        XL2 = stage_f[:, 0:TPC * D].rearrange("p (a b) -> p a b", a=TPC)
        X2T = stage_f[:, TPC * D:TPC * D + KD * CW].rearrange("p (a b) -> p a b", a=KD)
        XHL = stage_f[:, TPC * D + KD * CW:TPC * D + 2 * KD * CW].bitcast(F16)\
            .rearrange("p (a k n) -> p a k n", a=2, k=KD)
        arena_at[0] = route_at
        SCS = arena([NT, E])
        SEL = arena([NT, E])
        EQ = arena([NT, E])
        RE = arena([NT, E])
        OH0 = arena([NT, E])
        OH1 = arena([NT, E])
        OHS = arena([NT, E])
        TOTS = arena([NT, E])
        INCA = arena([NT // 2 + NT, E])
        INCB = arena([NT // 2 + NT, E])
        PA = arena([NT, E])
        PB = arena([NT, E])
        CMP = arena([NBLK, E])
        assert arena_at[0] <= 2 * 2 * TOK
        OH = [OH0, OH1]
        m1 = sb("m1", [P, NT], F32)
        rm = sb("rm", [P, NT], F32)
        gsum = sb("gsum", [P, NT], F32)
        nf = sb("nf", [P, E], F32)
        ni = sb("ni", [P, E], I32)
        bi = sb("bi", [P, E], I32)
        bf = sb("bf", [P, E], F32)
        ea = sb("ea", [P, E // 2 + E], F32)
        eb = sb("eb", [P, E // 2 + E], F32)
        base_row = sb("base_row", [P, E], F32)
        lowi = sb("lowi", [P, 2, NT], I32)
        highi = sb("highi", [P, 2, NT], I32)
        bef = sb("bef", [1, NBLK + 4], F32)
        word = sb("word", [1, 2, NBLK // 4], F32)

        bank = [ctx.enter_context(nc.psum_tensor(f"bank{i}", [P, CW], F32)) for i in range(8)]

        ld_small = sem("ld_small")
        ld_ctx = [sem(f"ld_ctx{i}") for i in range(4)]
        ld_x = [sem(f"ld_x{i}") for i in range(4)]
        ld_shared = sem("ld_shared")
        ld_bias = sem("ld_bias")
        table_zeroed = sem("table_zeroed")
        pool_apart = sem("pool_apart")
        dve_apart = sem("dve_apart")
        c_mem = sem("c_mem")
        c_ready = sem("c_ready")
        ws_hi = sem("ws_hi")
        ws_lo = sem("ws_lo")
        tanh_done = sem("tanh_done")
        tgs_done = sem("tgs_done")
        t_mm = sem("t_mm")
        t_sq = sem("t_sq")
        t_norm = sem("t_norm")
        t_sqrt = sem("t_sqrt")
        rt_ready = sem("rt_ready")
        ve1_ready = sem("ve1_ready")
        sd1_ready = sem("sd1_ready")
        s1 = sem("s1")
        xln = sem("xln")
        t1 = sem("t1")
        xt = sem("xt")
        v_mm = sem("v_mm")
        v_sq = sem("v_sq")
        dg = sem("dg")
        rb = sem("rb")
        n_mm = sem("n_mm")
        vn_sq = sem("vn_sq")
        rv_own = sem("rv_own")
        rv_ready = sem("rv_ready")
        m_ready = sem("m_ready")
        dot = sem("dot")
        cos_done = sem("cos_done")
        s2 = sem("s2")
        s2_aggr = sem("s2_aggr")
        s2_rs = sem("s2_rs")
        ve2_ready = sem("ve2_ready")
        sd2_ready = sem("sd2_ready")
        xl2 = sem("xl2")
        t2 = sem("t2")
        x2t = sem("x2t")
        hl2 = sem("hl2")
        r_mm = sem("r_mm")
        st_rows = sem("st_rows")
        st_xt = sem("st_xt")
        sig = sem("sig")
        r = sem("r")
        ohs_ready = sem("ohs_ready")
        rank = sem("rank")
        routed_ok = sem("routed_ok")
        pad_zero = sem("pad_zero")
        ix_copy = sem("ix_copy")
        scat = [sem(f"scat{i}") for i in range(4)]
        ld_idx = sem("ld_idx")
        ld_xtc = [sem(f"ld_xtc{i}") for i in range(2)]
        s_h = sem("s_h")
        s_sil = sem("s_sil")
        s_g = sem("s_g")
        s_ghi = sem("s_ghi")
        s_glo = sem("s_glo")
        s_y = sem("s_y")
        s_base = sem("s_base")
        ld_stage = [sem(f"ld_stage{i}") for i in range(2)]
        w_hi = sem("w_hi")
        w_lo = sem("w_lo")
        xg = [sem(f"xg{i}") for i in range(4)]
        b_ix = sem("b_ix")
        b_tx = sem("b_tx")
        b_xhi = sem("b_xhi")
        b_xlo = sem("b_xlo")
        b_h = sem("b_h")
        b_sil = sem("b_sil")
        b_g = sem("b_g")
        b_tg = sem("b_tg")
        b_ghi = sem("b_ghi")
        b_glo = sem("b_glo")
        b_y = sem("b_y")
        b_yev = sem("b_yev")
        st_y = [sem(f"st_y{i}") for i in range(4)]
        c_ix = sem("c_ix")
        yg = [sem(f"yg{i}") for i in range(4)]
        cmb = sem("cmb")
        st_out = sem("st_out")

        NSMALL = 7 * 16
        WP = WSH // NC
        LAST = NC - 1
        NCA = NC // 2
        NSA = NCA * J

        block = ctx.enter_context(nc.Block())

        @block.sync
        def _(sp):
            sp.dma_start(wt[:, :, :], wt_t.rearrange("(k p) h -> p k h", p=KT)).then_inc(ld_small, 16)
            sp.dma_start(btc[:, :], bt.rearrange("(p o) -> p o", o=1)).then_inc(ld_small, 16)
            ctx_k = ctx_t.rearrange("(k p) n -> p k n", p=KT)
            q = TOK // 4
            for i in range(4):
                sp.dma_start(CTX[0:KT, :, i * q:(i + 1) * q], ctx_k[:, :, i * q:(i + 1) * q]).then_inc(ld_ctx[i], 16)
                sp.dma_start(X[:, i * (NT // 4):(i + 1) * (NT // 4), :],
                             x_tiles[:, i * (NT // 4):(i + 1) * (NT // 4), :]).then_inc(ld_x[i], 16)
                if i == 0:
                    sp.dma_start(bvc[:, :], bv.rearrange("(p o) -> p o", o=1)).then_inc(ld_small, 16)
                    sp.dma_start(wv[:, :, :], wv_t.rearrange("(k p) h -> p k h", p=P)).then_inc(ld_small, 16)
                    sp.dma_start(rw[:, :, :], router_w.rearrange("(k p) e -> p k e", p=P)).then_inc(ld_small, 16)
                    sp.dma_start(gates_in[:, 0:1], g_xattn.partition_broadcast(P)).then_inc(ld_small, 16)
                    sp.dma_start(gates_in[:, 1:2], g_ffn.partition_broadcast(P)).then_inc(ld_small, 16)
                    sp.dma_start(bias16[:, :], expert_bias.partition_broadcast(P)).then_inc(ld_bias, 16)
            for w, at in ((shared_w1, 0), (shared_w2, KD * SH)):
                sp.dma_start(SHST[:, at:at + KD * SH].rearrange("p (k n) -> p k n", k=KD),
                             w[0].rearrange("(k p) n -> p k n", p=P)).then_inc(ld_shared, 16)
            sp.dma_start(SHST[:, W3S:WSH].rearrange("p (j n) -> p j n", j=J),
                         shared_w3[0].rearrange("(j p) n -> p j n", p=P)).then_inc(ld_shared, 16)
            sp.wait_ge(c_ready, 1)
            sp.dma_start(slot_token.rearrange("(p b) o -> p (b o)", p=P), zero_idx[:, :]).then_inc(table_zeroed, 16)
            with sp.Fori(0, NC) as c:
                sp.wait_ge(xl2, c + 1)
                sp.dma_start(xrow_tiles[:, ds(c * TPC, TPC), :], XL2).then_inc(st_rows, 16)
                sp.wait_ge(hl2, c + 1)
                sp.dma_start(xtd[ds(c * P, P), :], XHL.rearrange("p a k n -> p (a k n)")).then_inc(st_xt, 16)
            sp.wait_ge(st_rows, NC * 16)
            sp.wait_ge(st_xt, NC * 16)
            for u in range(2):
                sp.dma_start(XTC[:, u, :, :, :].rearrange("p a k n -> p (a k n)"),
                             xtd[u * P:(u + 1) * P, :]).then_inc(ld_xtc[u], 16)

            def stage(e, u):
                at = STAGE[:, u, 0:W3E].rearrange("p (k w n) -> p k w n", k=KD, w=2)
                for w, m in enumerate((routed_w1, routed_w2)):
                    sp.dma_start(at[:, :, w, :], m[ds(e, 1), :, :].rearrange("e (k p) n -> p (e k) n", p=P))\
                        .then_inc(ld_stage[u], 16)
                sp.dma_start(STAGE[:, u, W3E:WE].rearrange("p (k n) -> p k n", n=D),
                             routed_w3[ds(e, 1), :, :].rearrange("e (k p) n -> p (e k) n", p=P))\
                    .then_inc(ld_stage[u], 16)

            sp.wait_ge(r_mm, NC)
            for u in range(2):
                stage(u, u)
            with sp.Fori(1, E // 2) as i:
                for u in range(2):
                    sp.wait_ge(w_lo, i * 4 + (2 * u - 2))
                    stage(i * 2 + u, u)
            with sp.Fori(0, NBLK // 4) as i:
                for u in range(4):
                    sp.wait_ge(b_yev, i * 4 + (u + 1))
                    sp.dma_start(yrow[ds(i * (4 * P) + u * P, P), :], YS[:, u, :]).then_inc(st_y[u], 16)
            for u in range(2):
                sp.wait_ge(s_h, (NCA + 1 + u) * J)
                sp.dma_start(XTC[:, u, :, :, :].rearrange("p a k n -> p (a k n)"),
                             xtd[(NC - 2 + u) * P:(NC - 1 + u) * P, :]).then_inc(ld_xtc[u], 16)
            with sp.Fori(0, NC) as c:
                sp.wait_ge(s_base, c + 1)
                sp.wait_ge(cmb, c * (2 * TPC) + 2 * TPC)
                sp.dma_start(out_tiles[:, ds(c * TPC, TPC), :], X[:, ds(c * TPC, TPC), :]).then_inc(st_out, 16)
            sp.wait_ge(st_out, NC * 16)
            for u in range(4):
                sp.wait_ge(st_y[u], NBLK // 4 * 16)

        @block.gpsimd
        def _(pool):
            pool.memset(ident[:, :], 0.0).then_inc(c_mem, 1)
            pool.memset(before[:, :], 1.0).then_inc(c_mem, 1)
            pool.memset(ones[:, :], 1.0)
            pool.memset(zero_idx[:, :], 0)
            pool.iota(tokid[:, :], pattern=[[P, NT]], base=0, channel_multiplier=1)
            pool.wait_ge(c_mem, 2)
            pool.affine_select(out=ident[:, :], in_=ident[:, :], compare_op=ALU.not_equal, fill=1.0,
                               base=0, pattern=[[-1, P]], channel_multiplier=1)
            pool.affine_select(out=before[:, :], in_=before[:, :], compare_op=ALU.is_ge, fill=0.0,
                               base=-1, pattern=[[1, P]], channel_multiplier=-1).then_inc(c_ready, 1)
            pool.iota(blk_iota[:, :], pattern=[[1, NBLK]], base=0, channel_multiplier=0,
                      allow_small_or_imprecise_dtypes=True)
            pool.iota(rev[:, :], pattern=[[-1, E]], base=E, channel_multiplier=0,
                      allow_small_or_imprecise_dtypes=True).then_inc(c_ready, 1)
            def diagonal(c, first=False):
                if first:
                    pool.wait_ge(rt_ready, 1)
                else:
                    pool.wait_ge(rb, c)
                pool.tensor_tensor(DG, ident[:, :].unsqueeze(1).to_broadcast([P, TPC, P]),
                                   rt[:, ds(c * TPC, TPC)].unsqueeze(2).to_broadcast([P, TPC, P]),
                                   ALU.mult).then_inc(dg, 1)

            def cut(c):
                pool.wait_ge(x2t, c * 2 + 2)
                pool.sem_inc(pool_apart, 1)
                pool.tensor_tensor(XHL[:, 1], X2T, XHL[:, 0], ALU.subtract).then_inc(hl2, 1)

            diagonal(0, True)
            diagonal(1)
            diagonal(2)
            cut(0)
            with pool.Fori(1, NC - 2) as c:
                diagonal(c + 2)
                cut(c)
            cut(NC - 2)
            cut(NC - 1)

            pool.wait_ge(routed_ok, 1)
            pool.wait_ge(table_zeroed, 16)

            def scatter(i, u, first=False):
                t = i * 4 + u
                if not first:
                    pool.wait_ge(scat[u], i * 32)
                pool.sem_inc(pool_apart, 1)
                pool.tensor_copy(ixs[:, u, :], sloti[:, :, ds(t, 1)].rearrange("p a b -> p (a b)"))
                pool.tensor_copy(tks[:, u:u + 1], tokid[:, ds(t, 1)]).then_inc(ix_copy, 1)
                pool.wait_ge(ix_copy, t + 1)
                pool.sem_inc(pool_apart, 1)
                for k in range(2):
                    pool.indirect_dma_start(out=slot_token, in_=tks[:, u:u + 1], in_offset=None,
                                            out_offset=bass.IndirectOffsetOnAxis(
                                                ap=ixs[:, u, k:k + 1].bitcast(U32), axis=0))\
                        .then_inc(scat[u], 16)

            for u in range(4):
                scatter(0, u, True)
            with pool.Fori(1, NT // 4) as i:
                for u in range(4):
                    scatter(i, u)
            for u in range(4):
                pool.wait_ge(scat[u], NT // 4 * 32)
            pool.dma_start(idx[:, :], slot_token.rearrange("(p b) o -> p (b o)", p=P)).then_inc(ld_idx, 16)
            pool.wait_ge(ld_idx, 16)
            pool.wait_ge(st_rows, NC * 16)

            def fetch(i, u, first=False):
                b = i * 4 + u
                if not first:
                    pool.wait_ge(b_tx, i * 4 + (u - 3))
                pool.sem_inc(pool_apart, 1)
                pool.tensor_copy(ixb[:, u:u + 1], idx[:, ds(b, 1)]).then_inc(b_ix, 1)
                pool.wait_ge(b_ix, b + 1)
                pool.sem_inc(pool_apart, 1)
                pool.indirect_dma_start(out=XG[:, u, :], out_offset=None, in_=xrow,
                                        in_offset=bass.IndirectOffsetOnAxis(
                                            ap=ixb[:, u:u + 1].bitcast(U32), axis=0)).then_inc(xg[u], 16)

            for u in range(4):
                fetch(0, u, True)
            with pool.Fori(1, NBLK // 4) as i:
                for u in range(4):
                    fetch(i, u)

            pool.wait_ge(b_tx, NBLK)
            for u in range(4):
                pool.wait_ge(st_y[u], NBLK // 4 * 16)

            def bring(i, u, first=False):
                t = i * 4 + u
                if not first:
                    pool.wait_ge(cmb, i * 8 + (2 * u - 6))
                pool.sem_inc(pool_apart, 1)
                pool.tensor_copy(ixc[:, u, :], posi[:, :, ds(t, 1)].rearrange("p a b -> p (a b)")).then_inc(c_ix, 1)
                pool.wait_ge(c_ix, t + 1)
                pool.sem_inc(pool_apart, 1)
                for k in range(2):
                    pool.indirect_dma_start(out=YG[:, u, k, :], out_offset=None, in_=yrow,
                                            in_offset=bass.IndirectOffsetOnAxis(
                                                ap=ixc[:, u, k:k + 1].bitcast(U32), axis=0))\
                        .then_inc(yg[u], 16)

            for u in range(4):
                bring(0, u, True)
            with pool.Fori(1, NT // 4) as i:
                for u in range(4):
                    bring(i, u)

        @block.scalar
        def _(act):
            act.wait_ge(ld_small, NSMALL)
            act.activation(tg[:, :], gates_in[:, :], ACT.Tanh).then_inc(tanh_done, 1)
            act.preload_act_table(ACT.Sqrt)
            for c in range(NC):
                u = c % 2
                act.wait_ge(t_mm, c + 1)
                act.activation(TT[:, c * CW:(c + 1) * CW], bank[u][:, :], ACT.Identity, bias=btc[:, :])
                if c >= 2:
                    act.wait_ge(t_norm, c - 1)
                act.activation(SQT[:, u, :], bank[u][:, :], ACT.Square, bias=btc[:, :]).then_inc(t_sq, 1)
            act.wait_ge(t_norm, NC)
            act.activation(tn[:, :], bank[2][:, 0:NT], ACT.Sqrt).then_inc(t_sqrt, 1)
            act.wait_ge(ve1_ready, 1)
            act.activation(tmp1[:, :], var1[:, :], ACT.Sqrt).then_inc(sd1_ready, 1)

            def lead(c, first=False):
                for u in range(2):
                    act.wait_ge(t1, c * 2 + (u + 1))
                    if u == 0 and not first:
                        act.wait_ge(v_mm, c)
                    act.activation(XT[:, :, u * D:(u + 1) * D],
                                   bank[3 + u][:, :].rearrange("p (k n) -> p k n", k=KD), ACT.Copy).then_inc(xt, 1)

            def lead_v(c, first=False):
                act.wait_ge(v_mm, c + 1)
                if not first:
                    act.wait_ge(dot, c * 2)
                act.activation(VT, bank[5][:, :], ACT.Identity, bias=bvc[:, :])
                if not first:
                    act.wait_ge(n_mm, c)
                act.activation(SQV, bank[5][:, :], ACT.Square, bias=bvc[:, :]).then_inc(v_sq, 1)

            def lead_norm(c, first=False):
                act.wait_ge(n_mm, c + 1)
                if not first:
                    act.wait_ge(rv_ready, c)
                act.activation(vn[:, :], bank[2][:, 0:TPC], ACT.Sqrt).then_inc(vn_sq, 1)

            def scales(c, first=False):
                act.wait_ge(rv_ready, c + 1)
                act.wait_ge(rb, c + 1)
                for u in range(2):
                    if not first:
                        act.wait_ge(cos_done, c * 2 + (u - 1))
                    for i in range(2):
                        last = act.activation(M[:, 2 * u + i, :], bank[6][:, u * D:(u + 1) * D], ACT.Copy,
                                              scale=rv[:, 2 * u + i:2 * u + i + 1])
                    last.then_inc(m_ready, 1)

            def lag(c, first=False):
                for u in range(2):
                    act.wait_ge(t2, c * 2 + (u + 1))
                    if u == 0 and not first:
                        act.wait_ge(r_mm, c)
                        act.wait_ge(hl2, c)
                        act.wait_ge(st_xt, c * 16)
                    half = bank[3 + u][:, :].rearrange("p (k n) -> p k n", k=KD)
                    act.activation(X2T[:, :, u * D:(u + 1) * D], half, ACT.Copy)
                    act.activation(XHL[:, 0, :, u * D:(u + 1) * D], half, ACT.Copy).then_inc(x2t, 1)

            def weights_hi(c):
                act.activation(WS[:, 0, ds(c * WP, WP)], SHST[:, ds(c * WP, WP)], ACT.Copy, scale=WSCALE)\
                    .then_inc(ws_hi, 1)

            def deviation(c):
                act.wait_ge(ve2_ready, c + 1)
                act.activation(sd2[:, :], ve2[:, :], ACT.Sqrt).then_inc(sd2_ready, 1)

            lead(0, True)
            lead_v(0, True)
            lead_norm(0, True)
            scales(0, True)
            lead(1)
            lead_v(1)
            deviation(0)
            lead_norm(1)
            act.wait_ge(ld_shared, 48)
            scales(1)
            weights_hi(0)
            lead(2)
            lag(0, True)
            weights_hi(1)
            lead_v(2)
            deviation(1)
            lead_norm(2)
            with act.Fori(2, LAST) as c:
                scales(c)
                lead(c + 1)
                lag(c - 1)
                lead_v(c + 1)
                deviation(c)
                weights_hi(c)
                lead_norm(c + 1)
            scales(LAST)
            lag(LAST - 1)
            weights_hi(LAST)
            deviation(LAST)
            lag(LAST)

            act.wait_ge(r_mm, NC)
            act.activation(SCS.rearrange("p a b -> p (a b)"), bank[7][:, :], ACT.Sigmoid).then_inc(sig, 1)
            act.preload_act_table(ACT.Silu)

            def step(n, j, first=False, fill=False, e=None, u=0):
                a = j % 2
                act.wait_ge(s_h, n + 1)
                if not first:
                    act.wait_ge(s_g, n - 1)
                act.activation(SIL[:, a, :], bank[2 * a][:, :], ACT.Silu, scale=1.0 / WSCALE).then_inc(s_sil, 1)
                if e is not None:
                    if j % 2 == 0:
                        act.wait_ge(ld_stage[e[1]], e[2])
                    at = e[0] * (2 * WE) + (j % 2) * WH
                    act.activation(WR[:, ds(at, WH)], STAGE[:, e[1], (j % 2) * WH:(j % 2 + 1) * WH], ACT.Copy,
                                   scale=WSCALE).then_inc(w_hi, 1)
                act.wait_ge(s_g, n + 1)
                if not first:
                    act.wait_ge(s_y, n - 1)
                act.activation(GS[:, a, 0, :], G[:, a, :], ACT.Copy).then_inc(s_ghi, 1)

            def shared_a(i, first=False):
                for u in range(2):
                    for j in range(J):
                        k = u * J + j
                        e = (i * J + k // 2, (k // 2) % 2, i * (4 * 48) + (k // 4 + 1) * 48)
                        step(i * (2 * J) + k, j, first and k < 2, e=e)
                    act.dma_start(XTC[:, u, :, :, :].rearrange("p a k n -> p (a k n)"),
                                  xtd[ds(i * (2 * P) + (u + 2) * P, P), :]).then_inc(ld_xtc[u], 16)

            act.wait_ge(routed_ok, 1)
            shared_a(0, True)
            with act.Fori(1, NCA // 2) as i:
                shared_a(i)

            def x_hi(b, u, first=False):
                act.wait_ge(b_tx, b + 1)
                if not first:
                    act.wait_ge(b_h, b - 1)
                act.activation(XTB[:, u, 0], bank[2][:, 0:KD * P].rearrange("p (k n) -> p k n", k=KD), ACT.Copy)\
                    .then_inc(b_xhi, 1)

            def r_silu(b, u, first=False):
                act.wait_ge(b_h, b + 1)
                if not first:
                    act.wait_ge(b_g, b - 1)
                act.activation(SIL[:, u, 0:RH], bank[u][:, 0:RH], ACT.Silu, scale=1.0 / WSCALE).then_inc(b_sil, 1)

            def g_hi(b, u, first=False):
                act.wait_ge(b_tg, b + 1)
                if not first:
                    act.wait_ge(b_y, b - 1)
                act.activation(GT[:, u, 0], bank[3][:, 0:RH].rearrange("p (k n) -> p k n", k=RH // P), ACT.Copy)\
                    .then_inc(b_ghi, 1)

            act.wait_ge(s_g, NSA)
            x_hi(0, 0, True)
            x_hi(1, 1, True)
            for b in range(4):
                r_silu(b, b % 2, b < 2)
                if b >= 1:
                    g_hi(b - 1, (b - 1) % 2, b - 1 < 2)
                x_hi(b + 2, b % 2)
            with act.Fori(1, NBLK // 4 - 1) as i:
                for k in range(4):
                    b = i * 4 + k
                    r_silu(b, k % 2)
                    g_hi(b - 1, (k + 1) % 2)
                    x_hi(b + 2, k % 2)
            for b in range(NBLK - 4, NBLK):
                r_silu(b, b % 2)
                g_hi(b - 1, (b - 1) % 2)
                if b + 2 < NBLK:
                    x_hi(b + 2, b % 2)
            g_hi(NBLK - 1, 1)

            act.wait_ge(b_g, NBLK)
            with act.Fori(NCA // 2, NC // 2) as i:
                for k in range(2 * J):
                    step(i * (2 * J) + k, k % J)

        @block.vector
        def _(dve):
            dve.wait_ge(tanh_done, 1)
            dve.tensor_scalar(tgs[:, :], tg[:, 1:2], 1.0 / WSCALE, None, ALU.mult).then_inc(tgs_done, 1)
            for g in range(4):
                dve.wait_ge(ld_x[g], 16)
                with dve.Fori(g * (NT // 4), (g + 1) * (NT // 4)) as t:
                    dve.bn_stats(st[:, t, :], X[:, t, :]).then_inc(s1, 1)
            dve.wait_ge(s1, NT)
            dve.tensor_tensor(mean1[:, :], st[:, :, 1], st[:, :, 4], ALU.add)
            dve.tensor_tensor(gsum[:, :], st[:, :, 1], st[:, :, 4], ALU.subtract)
            dve.tensor_tensor(var1[:, :], st[:, :, 2], st[:, :, 5], ALU.add).then_inc(s1, 1)
            dve.wait_ge(s1, NT + 1)
            dve.tensor_scalar(mean1[:, :], mean1[:, :], 0.5, None, ALU.mult)
            dve.tensor_scalar(gsum[:, :], gsum[:, :], 0.5, None, ALU.mult)
            dve.tensor_scalar(var1[:, :], var1[:, :], 1.0 / D, LN_EPS, ALU.mult, ALU.add).then_inc(s1, 1)
            dve.wait_ge(s1, NT + 2)
            dve.tensor_tensor(rstd1[:, :], gsum[:, :], gsum[:, :], ALU.mult).then_inc(s1, 1)
            dve.wait_ge(s1, NT + 3)
            dve.tensor_tensor(var1[:, :], var1[:, :], rstd1[:, :], ALU.add).then_inc(ve1_ready, 1)
            dve.wait_ge(sd1_ready, 1)
            dve.reciprocal(rstd1[:, :], tmp1[:, :]).then_inc(s1, 1)
            dve.wait_ge(s1, NT + 4)

            def normalise(c, first=False):
                if not first:
                    dve.wait_ge(t1, c * 2)
                for k in range(TPC):
                    t = c * TPC + k
                    last = dve.tensor_scalar(XL[:, k, :], X[:, ds(t, 1), :].rearrange("p a n -> p (a n)"),
                                             mean1[:, ds(t, 1)], rstd1[:, ds(t, 1)], ALU.subtract, ALU.mult)
                last.then_inc(xln, 1)

            def inverse_norm(c, first=False):
                dve.wait_ge(vn_sq, c + 1)
                if not first:
                    dve.wait_ge(m_ready, c * 2)
                dve.tensor_scalar(vn[:, :], vn[:, :], TINY, None, ALU.max).then_inc(rv_own, 1)
                dve.wait_ge(rv_own, c + 1)
                dve.reciprocal(rv[:, :], vn[:, :]).then_inc(rv_ready, 1)

            def attend(c, first=False):
                for u in range(2):
                    own = c * 8 + 4 * u
                    dve.wait_ge(dot, c * 2 + (u + 1))
                    dve.wait_ge(m_ready, c * 2 + (u + 1))
                    for i in range(2):
                        last = dve.scalar_tensor_tensor(out=A[:, i, :], in0=M[:, 2 * u + i, :], scalar=INV_EPS,
                                                        in1=bank[u][:, i * D:(i + 1) * D],
                                                        op0=ALU.min, op1=ALU.mult)
                    last.then_inc(cos_done, 1)
                    dve.wait_ge(cos_done, c * 2 + (u + 1))
                    xs = [X[:, ds(c * TPC + (2 * u + i), 1), :].rearrange("p a n -> p (a n)") for i in range(2)]
                    for i in range(2):
                        dve.scalar_tensor_tensor(out=xs[i], in0=A[:, i, :], scalar=tg[:, 0:1], in1=xs[i],
                                                 op0=ALU.mult, op1=ALU.add).then_inc(s2, 1)
                    for i in range(2):
                        dve.wait_ge(s2, own + (i + 1))
                        dve.sem_inc(dve_apart, 1)
                        dve.bn_stats(st2[:, 2 * u + i, :], xs[i]).then_inc(s2, 1)
                    for i in range(2):
                        dve.wait_ge(s2, own + (3 + i))
                        dve.sem_inc(dve_apart, 1)
                        last = dve.bn_aggr(mv2[:, 2 * u + i, :], st2[:, 2 * u + i, :])
                last.then_inc(s2_aggr, 1)
                dve.wait_ge(s2_aggr, c + 1)
                dve.tensor_scalar(ve2[:, :], mv2[:, :, 1], LN_EPS, None, ALU.add).then_inc(ve2_ready, 1)

            def normalise2(c, first=False):
                dve.wait_ge(sd2_ready, c + 1)
                dve.reciprocal(rs2[:, :], sd2[:, :]).then_inc(s2_rs, 1)
                dve.wait_ge(s2_rs, c + 1)
                if not first:
                    dve.wait_ge(t2, c * 2)
                    dve.wait_ge(st_rows, c * 16)
                for k in range(TPC):
                    last = dve.tensor_scalar(XL2[:, k, :],
                                             X[:, ds(c * TPC + k, 1), :].rearrange("p a n -> p (a n)"),
                                             mv2[:, k, 0:1], rs2[:, k:k + 1], ALU.subtract, ALU.mult)
                last.then_inc(xl2, 1)

            def weights_lo(c):
                dve.wait_ge(ws_hi, c + 1)
                dve.scalar_tensor_tensor(out=WS[:, 1, ds(c * WP, WP)], in0=SHST[:, ds(c * WP, WP)], scalar=WSCALE,
                                         in1=WS[:, 0, ds(c * WP, WP)], op0=ALU.mult, op1=ALU.subtract)\
                    .then_inc(ws_lo, 1)

            normalise(0, True)
            dve.wait_ge(t_sqrt, 1)
            dve.tensor_scalar(tn[:, :], tn[:, :], TINY, None, ALU.max).then_inc(s1, 1)
            dve.wait_ge(s1, NT + 5)
            dve.reciprocal(rt[:, :], tn[:, :]).then_inc(rt_ready, 1)
            inverse_norm(0, True)
            normalise(1)
            attend(0, True)
            normalise2(0, True)
            inverse_norm(1)
            with dve.Fori(1, LAST) as c:
                normalise(c + 1)
                attend(c)
                weights_lo(c - 1)
                normalise2(c)
                inverse_norm(c + 1)
            attend(LAST)
            weights_lo(LAST - 1)
            normalise2(LAST)

            own = [0]

            def link(ins):
                own[0] += 1
                ins.then_inc(r, 1)
                dve.wait_ge(r, own[0])

            def over_tiles(a):
                return a.unsqueeze(1).to_broadcast([P, NT, E])

            def over_experts(a):
                return a.unsqueeze(2).to_broadcast([P, NT, E])

            dve.wait_ge(sig, 1)
            dve.wait_ge(ld_bias, 16)
            dve.wait_ge(c_ready, 2)
            PADT = NT // 2
            PADE = E // 2
            dve.memset(INCA[:, 0:PADT, :], 0.0)
            dve.memset(INCB[:, 0:PADT, :], 0.0)
            dve.memset(ea[:, 0:PADE], 0.0)
            dve.memset(bef[:, :], 0.0)
            link(dve.memset(eb[:, 0:PADE], 0.0))
            link(dve.tensor_tensor(SEL, SCS, over_tiles(bias16[:, :]), ALU.add))
            for k in range(2):
                link(dve.tensor_reduce(m1[:, :], SEL, AX.X, ALU.max))
                link(dve.tensor_tensor(EQ, SEL, over_experts(m1[:, :]), ALU.is_equal))
                link(dve.tensor_tensor(RE, EQ, over_tiles(rev[:, :]), ALU.mult))
                link(dve.tensor_reduce(rm[:, :], RE, AX.X, ALU.max))
                link(dve.tensor_tensor(OH[k], over_experts(rm[:, :]), over_tiles(rev[:, :]), ALU.is_equal))
                if k == 0:
                    link(dve.scalar_tensor_tensor(out=SEL, in0=OH[k], scalar=-1e30, in1=SEL,
                                                  op0=ALU.mult, op1=ALU.add))
            dve.tensor_tensor(OHS, OH[0], OH[1], ALU.add).then_inc(ohs_ready, 1)
            for k in range(2):
                link(dve.tensor_tensor(EQ, OH[k], SCS, ALU.mult))
                link(dve.tensor_reduce(gsum[:, :], EQ, AX.X, ALU.add))
                link(dve.tensor_scalar(gate[:, k, :], gsum[:, :], tgs[:, :], None, ALU.mult))
            weights_lo(LAST)
            dve.wait_ge(rank, 2)
            dve.tensor_copy(TOTS.rearrange("p a b -> p (a b)"), bank[7][:, :])
            link(dve.tensor_copy(INCA[:, PADT:PADT + NT, :].rearrange("p a b -> p (a b)"), bank[7][:, :]))
            src, dst = INCA, INCB
            step = 1
            while step < NT:
                link(dve.tensor_tensor(dst[:, PADT:PADT + NT, :], src[:, PADT:PADT + NT, :],
                                       src[:, PADT - step:PADT - step + NT, :], ALU.add))
                src, dst = dst, src
                step *= 2
            inc = src[:, PADT:PADT + NT, :]
            link(dve.tensor_scalar(ni[:, :], src[:, PADT + NT - 1, :], float(P - 1), None, ALU.add))
            link(dve.tensor_scalar(bi[:, :], ni[:, :], 7, None, ALU.arith_shift_right))
            dve.tensor_copy(bf[:, :], bi[:, :])
            link(dve.tensor_copy(ea[:, PADE:PADE + E], bi[:, :]))
            es, ed = ea, eb
            step = 1
            while step < E:
                link(dve.tensor_tensor(ed[:, PADE:PADE + E], es[:, PADE:PADE + E],
                                       es[:, PADE - step:PADE - step + E], ALU.add))
                es, ed = ed, es
                step *= 2
            ends = es[:, PADE:PADE + E]
            link(dve.tensor_tensor(nf[:, :], ends, bf[:, :], ALU.subtract))
            link(dve.tensor_scalar(base_row[:, :], nf[:, :], float(P), None, ALU.mult))
            link(dve.tensor_tensor(PA, inc, TOTS, ALU.subtract))
            link(dve.tensor_tensor(PB, PA, over_tiles(base_row[:, :]), ALU.add))
            link(dve.tensor_tensor(PA.rearrange("p a b -> p (a b)"), PB.rearrange("p a b -> p (a b)"),
                                   bank[6][:, :], ALU.add))
            for k in range(2):
                link(dve.tensor_tensor(EQ, OH[k], PA, ALU.mult))
                link(dve.tensor_reduce(gsum[:, :], EQ, AX.X, ALU.add))
                link(dve.tensor_copy(posi[:, k, :], gsum[:, :]))
            dve.tensor_scalar(lowi[:, :, :], posi[:, :, :], P - 1, None, ALU.bitwise_and)
            link(dve.tensor_scalar(highi[:, :, :], posi[:, :, :], 7, None, ALU.arith_shift_right))
            link(dve.scalar_tensor_tensor(out=sloti[:, :, :], in0=lowi[:, :, :], scalar=float(NBLK),
                                          in1=highi[:, :, :], op0=ALU.mult, op1=ALU.add))
            link(dve.tensor_tensor(CMP[0:1], ends[0:1].unsqueeze(1).to_broadcast([1, NBLK, E]),
                                   blk_iota[:, :].unsqueeze(2).to_broadcast([1, NBLK, E]), ALU.is_le))
            link(dve.tensor_reduce(bef[:, 2:2 + NBLK], CMP[0:1], AX.X, ALU.add))
            link(dve.tensor_scalar(bef[:, 2:2 + NBLK], bef[:, 2:2 + NBLK], float(E - 1), None, ALU.min))
            four = bef[:, :].rearrange("o (i k) -> o k i", k=4)
            own_blocks = [four[:, k, 0:NBLK // 4] for k in range(4)] + [four[:, k, 1:1 + NBLK // 4] for k in range(2)]
            acc = own_blocks[5]
            for k in (4, 3, 2, 1):
                link(dve.scalar_tensor_tensor(out=word[:, k % 2, :], in0=acc, scalar=float(E),
                                              in1=own_blocks[k], op0=ALU.mult, op1=ALU.add))
                acc = word[:, k % 2, :]
            dve.scalar_tensor_tensor(out=blk_word[:, :], in0=acc, scalar=float(E), in1=own_blocks[0],
                                     op0=ALU.mult, op1=ALU.add).then_inc(routed_ok, 1)

            def step_s(n, j, first=False, e=None, tile=None, slot=0, count=None, chunks=None):
                a = j % 2
                dve.wait_ge(s_sil, n + 1)
                if not first:
                    dve.wait_ge(s_ghi, n - 1)
                dve.scalar_tensor_tensor(out=G[:, a, :], in0=bank[2 * a + 1][:, :], scalar=1.0 / WSCALE,
                                         in1=SIL[:, a, :], op0=ALU.mult, op1=ALU.mult).then_inc(s_g, 1)
                if e is not None:
                    at = e[0] * (2 * WE) + (j % 2) * WH
                    dve.wait_ge(w_hi, n + 1)
                    dve.scalar_tensor_tensor(out=WR[:, ds(at + WE, WH)],
                                             in0=STAGE[:, e[1], (j % 2) * WH:(j % 2 + 1) * WH], scalar=WSCALE,
                                             in1=WR[:, ds(at, WH)], op0=ALU.mult, op1=ALU.subtract)\
                        .then_inc(w_lo, 1)
                if tile is not None:
                    dve.wait_ge(yg[slot], count)
                    dve.wait_ge(s_base, chunks)
                    xs = X[:, ds(tile, 1), :].rearrange("p a n -> p (a n)")
                    for k in range(2):
                        if k == 1:
                            dve.wait_ge(cmb, tile * 2 + 1)
                        dve.scalar_tensor_tensor(out=xs, in0=YG[:, slot, k, :], scalar=gate[:, k, ds(tile, 1)],
                                                 in1=xs, op0=ALU.mult, op1=ALU.add).then_inc(cmb, 1)
                dve.wait_ge(s_ghi, n + 1)
                dve.tensor_tensor(GS[:, a, 1, :], G[:, a, :], GS[:, a, 0, :], ALU.subtract).then_inc(s_glo, 1)

            def add_shared(c, combined=None):
                dve.wait_ge(s_y, c * J + J)
                if combined is not None:
                    dve.wait_ge(cmb, combined)
                for k in range(TPC):
                    xs = X[:, ds(c * TPC + k, 1), :].rearrange("p a n -> p (a n)")
                    last = dve.scalar_tensor_tensor(out=xs, in0=bank[4 + k // 2][:, (k % 2) * D:(k % 2 + 1) * D],
                                                    scalar=tgs[:, :], in1=xs, op0=ALU.mult, op1=ALU.add)
                last.then_inc(s_base, 1)

            def shared_a(i, first=False):
                for u in range(2):
                    for j in range(J):
                        k = u * J + j
                        step_s(i * (2 * J) + k, j, first and k < 2, e=(i * J + k // 2, (k // 2) % 2))
                    add_shared(i * 2 + u)

            shared_a(0, True)
            with dve.Fori(1, NCA // 2) as i:
                shared_a(i)

            def x_lo(b, u):
                dve.wait_ge(b_xhi, b + 1)
                dve.tensor_tensor(XTB[:, u, 1], bank[2][:, 0:KD * P].rearrange("p (k n) -> p k n", k=KD),
                                  XTB[:, u, 0], ALU.subtract).then_inc(b_xlo, 1)

            def gated(b, u, first=False):
                dve.wait_ge(b_sil, b + 1)
                if not first:
                    dve.wait_ge(b_tg, b - 1)
                dve.scalar_tensor_tensor(out=G[:, u, 0:RH], in0=bank[u][:, RH:2 * RH], scalar=1.0 / WSCALE,
                                         in1=SIL[:, u, 0:RH], op0=ALU.mult, op1=ALU.mult).then_inc(b_g, 1)

            def g_lo(b, u):
                dve.wait_ge(b_ghi, b + 1)
                dve.tensor_tensor(GT[:, u, 1], bank[3][:, 0:RH].rearrange("p (k n) -> p k n", k=RH // P),
                                  GT[:, u, 0], ALU.subtract).then_inc(b_glo, 1)

            def rows(b, i, u, first=False):
                dve.wait_ge(b_y, b + 1)
                if not first:
                    dve.wait_ge(st_y[u], i * 16)
                dve.tensor_copy(YS[:, u, :], bank[4][:, 0:D]).then_inc(b_yev, 1)

            dve.wait_ge(s_y, NSA)
            x_lo(0, 0)
            x_lo(1, 1)
            for b in range(4):
                gated(b, b % 2, b < 2)
                if b >= 1:
                    g_lo(b - 1, (b - 1) % 2)
                x_lo(b + 2, b % 2)
                if b >= 2:
                    rows(b - 2, 0, b - 2, True)
            gated(4, 0)
            g_lo(3, 1)
            x_lo(6, 0)
            rows(2, 0, 2, True)
            gated(5, 1)
            g_lo(4, 0)
            x_lo(7, 1)
            rows(3, 0, 3, True)
            with dve.Fori(1, NBLK // 4 - 1) as i:
                for k in range(4):
                    b = i * 4 + (k + 2)
                    gated(b, k % 2)
                    g_lo(b - 1, (k + 1) % 2)
                    x_lo(b + 2, k % 2)
                    rows(b - 2, i, k)
            for b in range(NBLK - 2, NBLK):
                gated(b, b % 2)
                g_lo(b - 1, (b - 1) % 2)
                rows(b - 2, (b - 2) // 4, (b - 2) % 4)
            g_lo(NBLK - 1, 1)
            rows(NBLK - 2, NBLK // 4 - 1, 2)
            rows(NBLK - 1, NBLK // 4 - 1, 3)

            with dve.Fori(NCA // 2, NC // 2) as i:
                for u in range(2):
                    for j in range(J):
                        k = u * J + j
                        step_s(i * (2 * J) + k, j, tile=i * (2 * J) + (k - NSA), slot=k % 4,
                               count=i * (4 * 32) + (k // 4 + 1 - NSA // 4) * 32, chunks=i * 2 + u)
                    add_shared(i * 2 + u, combined=i * (4 * J) + ((u + 1) * 2 * J - 2 * NSA))

        @block.tensor
        def _(pe):
            pe.wait_ge(ld_small, NSMALL)
            pe.wait_ge(c_ready, 1)

            def t_norms(c):
                u = c % 2
                pe.wait_ge(t_sq, c + 1)
                for k in range(TPC):
                    last = pe.matmul(bank[2][:, c * TPC + k:c * TPC + k + 1], SQT[:, u, k * P:(k + 1) * P],
                                     ones[:, 0:1], start=True, stop=True)
                last.then_inc(t_norm, 1)

            for c in range(NC):
                u = c % 2
                if u == 0:
                    pe.wait_ge(ld_ctx[c // 2], 16)
                if c >= 2:
                    pe.wait_ge(t_sq, c - 1)
                for k in range(2):
                    last = pe.matmul(bank[u][:, :], wt[:, k, :], CTX[0:KT, k, c * CW:(c + 1) * CW],
                                     start=(k == 0), stop=(k == 1))
                last.then_inc(t_mm, 1)
                if c >= 1:
                    t_norms(c - 1)
            t_norms(NC - 1)

            def transpose1(c, first=False, after_t2=True):
                pe.wait_ge(xln, c + 1)
                for u in range(2):
                    if not first:
                        if after_t2:
                            pe.wait_ge(x2t, c * 2 + (u - 5))
                        else:
                            pe.wait_ge(xt, c * 2 + (u - 1))
                    for k in range(KD):
                        for i in range(2):
                            last = pe.transpose(bank[3 + u][:, k * D + i * P:k * D + (i + 1) * P],
                                                XL[:, 2 * u + i, k * P:(k + 1) * P], ident[:, :])
                    last.then_inc(t1, 1)

            def values(c, first=False):
                pe.wait_ge(xt, c * 2 + 2)
                if not first:
                    pe.wait_ge(v_sq, c)
                for k in range(KD):
                    last = pe.matmul(bank[5][:, :], wv[:, k, :], XT[:, k, :], start=(k == 0), stop=(k == KD - 1))
                last.then_inc(v_mm, 1)

            def row_norms(c, first=False):
                pe.wait_ge(dg, c + 1)
                if not first:
                    pe.wait_ge(m_ready, c * 2)
                pe.matmul(bank[6][:, :], ones[:, :], DG.rearrange("p a b -> p (a b)"), start=True, stop=True)\
                    .then_inc(rb, 1)

            def v_norms(c, first=False):
                pe.wait_ge(v_sq, c + 1)
                pe.wait_ge(t_sqrt, 1) if first else pe.wait_ge(vn_sq, c)
                for k in range(TPC):
                    last = pe.matmul(bank[2][:, k:k + 1], SQV[:, k * P:(k + 1) * P], ones[:, 0:1],
                                     start=True, stop=True)
                last.then_inc(n_mm, 1)

            def dots(c, first=False):
                pe.wait_ge(v_sq, c + 1)
                for u in range(2):
                    if not first:
                        pe.wait_ge(cos_done, c * 2 + (u - 1))
                    for i in range(2):
                        last = pe.matmul(bank[u][:, i * D:(i + 1) * D], VT[:, (2 * u + i) * P:(2 * u + i + 1) * P],
                                         TT[:, ds(c * CW + u * S, S)], start=True, stop=True)
                    last.then_inc(dot, 1)

            def transpose2(c, tail=False):
                pe.wait_ge(xl2, c + 1)
                for u in range(2):
                    if tail:
                        pe.wait_ge(x2t, c * 2 + (u - 1))
                    else:
                        pe.wait_ge(xt, c * 2 + (u + 5))
                    for k in range(KD):
                        for i in range(2):
                            last = pe.transpose(bank[3 + u][:, k * D + i * P:k * D + (i + 1) * P],
                                                XL2[:, 2 * u + i, k * P:(k + 1) * P], ident[:, :])
                    last.then_inc(t2, 1)

            def router(c):
                pe.wait_ge(x2t, c * 2 + 2)
                for i in range(TPC):
                    for k in range(KD):
                        last = pe.matmul(bank[7][:, ds(c * (TPC * E) + i * E, E)], X2T[:, k, i * P:(i + 1) * P],
                                         rw[:, k, :], start=(k == 0), stop=(k == KD - 1))
                last.then_inc(r_mm, 1)

            transpose1(0, True)
            values(0, True)
            row_norms(0, True)
            v_norms(0, True)
            dots(0, True)
            transpose1(1, after_t2=False)
            values(1)
            row_norms(1)
            v_norms(1)
            dots(1)
            transpose1(2, after_t2=False)
            transpose2(0)
            values(2)
            row_norms(2)
            router(0)
            v_norms(2)
            with pe.Fori(2, LAST) as c:
                dots(c)
                transpose1(c + 1)
                transpose2(c - 1)
                values(c + 1)
                row_norms(c + 1)
                router(c - 1)
                v_norms(c + 1)
            dots(LAST)
            transpose2(LAST - 1, tail=True)
            router(LAST - 1)
            transpose2(LAST, tail=True)
            router(LAST)

            pe.wait_ge(ohs_ready, 1)
            pe.matmul(bank[6][:, :], before[:, :], OHS.rearrange("p a b -> p (a b)"), start=True, stop=True)\
                .then_inc(rank, 1)
            pe.wait_ge(sig, 1)
            pe.matmul(bank[7][:, :], ones[:, :], OHS.rearrange("p a b -> p (a b)"), start=True, stop=True)\
                .then_inc(rank, 1)

            def hidden(n, u, j, first=False, load=None):
                a = j % 2
                if load is not None:
                    pe.wait_ge(ld_xtc[u], load)
                if not first:
                    pe.wait_ge(s_g, n - 1)
                for w in range(2):
                    acc = bank[2 * a + w]
                    for k in range(KD):
                        at = (w * KD + k) * SH + j * P
                        for m, (wx, xx) in enumerate(((0, 0), (0, 1), (1, 0))):
                            last = pe.matmul(acc[:, :], WS[:, wx, at:at + P], XTC[:, u, xx, k, :],
                                             start=(k == 0 and m == 0), stop=(k == KD - 1 and m == 2))
                last.then_inc(s_h, 1)

            def shared_rows(n, j, evacuated=None):
                a = j % 2
                pe.wait_ge(s_glo, n + 1)
                if evacuated is not None:
                    pe.wait_ge(s_base, evacuated)
                at = W3S + j * D
                for i in range(TPC):
                    acc = bank[4 + i // 2][:, (i % 2) * D:(i % 2 + 1) * D]
                    for m, (gx, wx) in enumerate(((0, 0), (0, 1), (1, 0))):
                        last = pe.matmul(acc, GS[:, a, gx, i * P:(i + 1) * P], WS[:, wx, at:at + D],
                                         start=(j == 0 and m == 0 and i % 2 == 0), stop=(j == J - 1 and m == 2),
                                         skip_group_check=True)
                last.then_inc(s_y, 1)

            def shared(i, first=False):
                def rows_of(k):
                    c = i * 2 + k // J
                    shared_rows(i * (2 * J) + k, k % J,
                                c if k % J == 0 and not (first and k == 0) else None)

                for k in range(2 * J):
                    hidden(i * (2 * J) + k, k // J, k % J, first and k < 2,
                           load=(i * 16 + 16) if k % J == 0 else None)
                    if k >= 1:
                        rows_of(k - 1)
                rows_of(2 * J - 1)

            pe.wait_ge(ws_lo, NC)
            pe.wait_ge(x2t, 2 * NC)
            pe.wait_ge(cos_done, 2 * NC)
            shared(0, True)
            with pe.Fori(1, NCA // 2) as i:
                shared(i)

            def experts(i):
                w = pe.value_load(blk_word[0:1, ds(i, 1)])
                return [(w >> (4 * k)) & (E - 1) for k in range(6)]

            def weights(e, at, n):
                return WR[:, :].rearrange("p (e n) -> p e n", e=E)[:, ds(e, 1), at:at + n]\
                    .rearrange("p a n -> p (a n)")

            def block_transpose(b, slot, count):
                pe.wait_ge(xg[slot], count)
                if not (isinstance(b, int) and b == 0):
                    pe.wait_ge(b_xlo, b)
                for k in range(KD):
                    last = pe.transpose(bank[2][:, k * P:(k + 1) * P], XG[:, slot, k * P:(k + 1) * P], ident[:, :])
                last.then_inc(b_tx, 1)

            def block_hidden(b, u, e, first=False):
                pe.wait_ge(b_xlo, b + 1)
                if not first:
                    pe.wait_ge(b_g, b - 1)
                for k in range(KD):
                    hi = weights(e, k * 2 * RH, 2 * RH)
                    lo = weights(e, WE + k * 2 * RH, 2 * RH)
                    for m, (xx, w) in enumerate(((0, hi), (0, lo), (1, hi))):
                        last = pe.matmul(bank[u][:, :], XTB[:, u, xx, k, :], w,
                                         start=(k == 0 and m == 0), stop=(k == KD - 1 and m == 2))
                last.then_inc(b_h, 1)

            def hidden_transpose(b, u, first=False):
                pe.wait_ge(b_g, b + 1)
                if not first:
                    pe.wait_ge(b_glo, b)
                for k in range(RH // P):
                    last = pe.transpose(bank[3][:, k * P:(k + 1) * P], G[:, u, k * P:(k + 1) * P], ident[:, :])
                last.then_inc(b_tg, 1)

            def block_rows(b, u, e, first=False):
                pe.wait_ge(b_glo, b + 1)
                if not first:
                    pe.wait_ge(b_yev, b)
                for k in range(RH // P):
                    hi = weights(e, W3E + k * D, D)
                    lo = weights(e, WE + W3E + k * D, D)
                    for m, (gx, w) in enumerate(((0, hi), (0, lo), (1, hi))):
                        last = pe.matmul(bank[4][:, 0:D], GT[:, u, gx, k, :], w,
                                         start=(k == 0 and m == 0), stop=(k == RH // P - 1 and m == 2))
                last.then_inc(b_y, 1)

            pe.wait_ge(routed_ok, 1)
            pe.wait_ge(w_lo, 2 * E)
            pe.wait_ge(s_glo, NSA)
            pe.wait_ge(s_base, NCA)
            block_transpose(0, 0, 16)
            block_transpose(1, 1, 16)
            es = experts(0)
            for b in range(4):
                block_hidden(b, b % 2, es[b + 2], b < 2)
                if b >= 1:
                    hidden_transpose(b - 1, (b - 1) % 2, b == 1)
                block_transpose(b + 2, (b + 2) % 4, 16 * ((b + 2) // 4 + 1))
                if b >= 2:
                    block_rows(b - 2, b % 2, es[b], b == 2)
            with pe.Fori(1, NBLK // 4 - 1) as i:
                es = experts(i)
                for k in range(4):
                    b = i * 4 + k
                    block_hidden(b, k % 2, es[k + 2])
                    hidden_transpose(b - 1, (k + 1) % 2)
                    block_transpose(b + 2, (k + 2) % 4, i * 16 + 16 * ((k + 2) // 4 + 1))
                    block_rows(b - 2, k % 2, es[k])
            es = experts(NBLK // 4 - 1)
            for k in range(4):
                b = NBLK - 4 + k
                block_hidden(b, b % 2, es[k + 2])
                hidden_transpose(b - 1, (b - 1) % 2)
                if b + 2 < NBLK:
                    block_transpose(b + 2, (b + 2) % 4, 16 * ((b + 2) // 4 + 1))
                block_rows(b - 2, b % 2, es[k])
            hidden_transpose(NBLK - 1, 1)
            block_rows(NBLK - 2, 0, es[4])
            block_rows(NBLK - 1, 1, es[5])

            pe.wait_ge(b_yev, NBLK)
            with pe.Fori(NCA // 2, NC // 2) as i:
                shared(i)


_INS = ["x", "ctx_t", "g_xattn", "g_ffn", "wv_t", "bv", "wt_t", "bt", "router_w", "expert_bias",
        "shared_w1", "shared_w2", "shared_w3", "routed_w1", "routed_w2", "routed_w3"]


def kernel(x, ctx_768, g_xattn, g_ffn, L0_xattn_Wv, L0_xattn_bv, L0_xattn_Wt, L0_xattn_bt, L0_ffn_router_w,
           L0_ffn_expert_bias, L0_ffn_shared_w1, L0_ffn_shared_w2, L0_ffn_shared_w3, L0_ffn_routed_w1,
           L0_ffn_routed_w2, L0_ffn_routed_w3):
    import numpy as np
    import concourse.bacc as bacc
    from concourse.bass_utils import run_bass_kernel_spmd

    ctx_768 = np.asarray(ctx_768)
    given = [x, ctx_768.transpose(2, 0, 1).reshape(ctx_768.shape[2], -1), g_xattn, g_ffn,
             np.asarray(L0_xattn_Wv).T, L0_xattn_bv, np.asarray(L0_xattn_Wt).T, L0_xattn_bt,
             L0_ffn_router_w, L0_ffn_expert_bias, L0_ffn_shared_w1, L0_ffn_shared_w2, L0_ffn_shared_w3,
             L0_ffn_routed_w1, L0_ffn_routed_w2, L0_ffn_routed_w3]
    nc = bacc.Bacc("TRN2", target_bir_lowering=False, num_devices=1)
    arrays, args = {}, []
    for name, a in zip(_INS, given):
        a = np.ascontiguousarray(a)
        arrays[f"in_{name}"] = a
        args.append(nc.dram_tensor(f"in_{name}", a.shape, mybir.dt.from_np(a.dtype), kind="ExternalInput").ap())
    args.append(nc.dram_tensor("out", tuple(x.shape), mybir.dt.float32, kind="ExternalOutput").ap())
    flamingo_block(nc, *args)
    done = run_bass_kernel_spmd(nc, [arrays], core_ids=[0])
    return done.results[0]["out"]
```

```python
import concourse.bass as bass
from concourse import mybir
from contextlib import ExitStack

P = 128


def flamingo_block(nc, x, ctx_t, g_xattn, g_ffn, wv_t, bv, wt_t, bt, router_w, expert_bias,
                   shared_w1, shared_w2, shared_w3, routed_w1, routed_w2, routed_w3, out):
    F32, F16, I32, U32 = mybir.dt.float32, mybir.dt.float16, mybir.dt.int32, mybir.dt.uint32
    ALU = mybir.AluOpType
    ACT = mybir.ActivationFunctionType
    AX = mybir.AxisListType
    ds = bass.ds

    B, S, D = x.shape
    TOK = B * S
    NT = TOK // P
    CW = 512
    TPC = CW // P
    NC = TOK // CW
    KD = D // P
    TD = ctx_t.shape[0]
    KT = TD // 2
    H = wv_t.shape[1]
    E = router_w.shape[1]
    SH = shared_w1.shape[2]
    J = SH // P
    RH = routed_w1.shape[2]
    NBLK = 2 * TOK // P + E
    WE = 2 * KD * RH + (RH // P) * D
    WH = WE // 2
    W3E = 2 * KD * RH
    WSH = 2 * KD * SH + J * D
    W3S = 2 * KD * SH
    WSCALE = 64.0
    LN_EPS = 1e-5
    INV_EPS = 1e8
    TINY = 1e-30

    x_tiles = x.rearrange("b s d -> (b s) d").rearrange("(t p) d -> p t d", p=P)
    out_tiles = out.rearrange("b s d -> (b s) d").rearrange("(t p) d -> p t d", p=P)

    xrow = nc.dram_tensor("xrow", (TOK, D), F32, kind="Internal").ap()
    xtd = nc.dram_tensor("xtd", (NC * P, 2 * KD * CW), F16, kind="Internal").ap()
    slot_token = nc.dram_tensor("slot_token", (P * NBLK, 1), I32, kind="Internal").ap()
    yrow = nc.dram_tensor("yrow", (NBLK * P, D), F32, kind="Internal").ap()
    xrow_tiles = xrow.rearrange("(t p) d -> p t d", p=P)

    ctx = ExitStack()
    with ctx:
        def sb(name, shape, dt):
            return ctx.enter_context(nc.sbuf_tensor(name, shape, dt))

        def sem(name):
            return ctx.enter_context(nc.semaphore(name))

        X = sb("X", [P, NT, D], F32)
        WR = sb("WR", [P, E * 2 * WE], F16)
        WS = sb("WS", [P, 2, WSH], F16)
        XTC = sb("XTC", [P, 2, 2, KD, CW], F16)
        GS = sb("GS", [P, 2, 2, CW], F16)
        SIL = sb("SIL", [P, 2, CW], F32)
        G = sb("G", [P, 2, CW], F32)
        STAGE = sb("STAGE", [P, 2, WE], F32)
        ROWS = sb("ROWS", [P, 8, D], F32)
        XG = ROWS[:, 0:4, :]
        YS = ROWS[:, 4:8, :]
        YG = ROWS[:, :, :].rearrange("p (t k) d -> p t k d", k=2)
        XTB = sb("XTB", [P, 2, 2, KD, P], F16)
        GT = sb("GT", [P, 2, 2, RH // P, P], F16)
        ident = sb("ident", [P, P], F32)
        before = sb("before", [P, P], F32)
        ones = sb("ones", [P, P], F32)
        wv = sb("wv", [P, KD, H], F32)
        wt = sb("wt", [KT, 2, H], F32)
        rw = sb("rw", [P, KD, E], F32)
        bvc = sb("bvc", [P, 1], F32)
        btc = sb("btc", [P, 1], F32)
        bias16 = sb("bias16", [P, E], F32)
        gates_in = sb("gates_in", [P, 2], F32)
        tg = sb("tg", [P, 2], F32)
        tgs = sb("tgs", [P, 1], F32)
        tbv = sb("tbv", [P, 1], F32)
        st = sb("st", [P, NT, 6], F32)
        mean1 = sb("mean1", [P, NT], F32)
        var1 = sb("var1", [P, NT], F32)
        rstd1 = sb("rstd1", [P, NT], F32)
        tmp1 = sb("tmp1", [P, NT], F32)
        tn = sb("tn", [P, NT], F32)
        rt = sb("rt", [P, NT], F32)
        vn = sb("vn", [P, TPC], F32)
        rv = sb("rv", [P, TPC], F32)
        st2 = sb("st2", [P, TPC, 6], F32)
        mv2 = sb("mv2", [P, TPC, 2], F32)
        ve2 = sb("ve2", [P, TPC], F32)
        sd2 = sb("sd2", [P, TPC], F32)
        rs2 = sb("rs2", [P, TPC], F32)
        posi = sb("posi", [P, 2, NT], I32)
        sloti = sb("sloti", [P, 2, NT], I32)
        gate = sb("gate", [P, 2, NT], F32)
        tokid = sb("tokid", [P, NT], I32)
        blk_word = sb("blk_word", [1, NBLK // 4], I32)
        row_iota = sb("row_iota", [P, 1], F32)
        pack = sb("pack", [P, NBLK // 4], F32)
        rev = sb("rev", [P, E], F32)
        idx = sb("idx", [P, NBLK], I32)
        zero_idx = sb("zero_idx", [P, NBLK], I32)
        ixs = sb("ixs", [P, 4, 2], I32)
        tks = sb("tks", [P, 4], I32)
        ixb = sb("ixb", [P, 4], I32)
        ixc = sb("ixc", [P, 4, 2], I32)

        arena_at = [0]

        def arena(shape):
            n = 2
            for s in shape:
                n *= s
            a = WR[:, arena_at[0]:arena_at[0] + n].bitcast(F32)
            arena_at[0] += n
            assert arena_at[0] <= E * 2 * WE
            if len(shape) == 2:
                a = a.rearrange("p (a b) -> p a b", a=shape[0])
            return a

        route_at = arena_at[0]
        CTX = arena([2, TOK])
        TT = arena([TOK])
        SHST = arena([WSH])
        SQT = arena([2, CW])
        XL = arena([TPC, D])
        XT = arena([KD, CW])
        VT = arena([CW])
        SQV = arena([CW])
        M = arena([TPC, D])
        DG = arena([TPC, P])
        stage_f = STAGE[:, :, :].rearrange("p a b -> p (a b)")
        XL2 = stage_f[:, 0:TPC * D].rearrange("p (a b) -> p a b", a=TPC)
        X2T = stage_f[:, TPC * D:TPC * D + KD * CW].rearrange("p (a b) -> p a b", a=KD)
        XHL = stage_f[:, TPC * D + KD * CW:TPC * D + 2 * KD * CW].bitcast(F16)\
            .rearrange("p (a k n) -> p a k n", a=2, k=KD)
        arena_at[0] = route_at
        SCS = arena([NT, E])
        SEL = arena([NT, E])
        EQ = arena([NT, E])
        RE = arena([NT, E])
        OH0 = arena([NT, E])
        OH1 = arena([NT, E])
        OHS = arena([NT, E])
        INCA = arena([NT // 2 + NT, E])
        INCB = arena([NT // 2 + NT, E])
        PA = arena([NT, E])
        PB = arena([NT, E])
        assert arena_at[0] <= 2 * 2 * TOK
        UNDER = -(-arena_at[0] // (2 * WE))
        OH = [OH0, OH1]
        m1 = sb("m1", [P, NT], F32)
        rm = sb("rm", [P, NT], F32)
        gsum = sb("gsum", [P, NT], F32)
        nf = sb("nf", [P, E], F32)
        ni = sb("ni", [P, E], I32)
        bi = sb("bi", [P, E], I32)
        bf = sb("bf", [P, E], F32)
        ea = sb("ea", [P, E // 2 + E], F32)
        eb = sb("eb", [P, E // 2 + E], F32)
        base_row = sb("base_row", [P, E], F32)
        lowi = sb("lowi", [P, 2, NT], I32)
        highi = sb("highi", [P, 2, NT], I32)
        ended = sb("ended", [P, E], F32)
        bef = sb("bef", [P, 1], F32)

        bank = [ctx.enter_context(nc.psum_tensor(f"bank{i}", [P, CW], F32)) for i in range(8)]

        HIDDEN = ((bank[0], bank[1]), (bank[2], bank[5]))
        SHARED_ROWS = (bank[3], bank[4])

        ld_text = sem("ld_text")
        ld_small = sem("ld_small")
        ld_ctx = [sem(f"ld_ctx{i}") for i in range(4)]
        ld_x = [sem(f"ld_x{i}") for i in range(4)]
        ld_shared = sem("ld_shared")
        ld_bias = sem("ld_bias")
        table_zeroed = sem("table_zeroed")
        pool_apart = sem("pool_apart")
        dve_apart = sem("dve_apart")
        c_mem = sem("c_mem")
        c_ready = sem("c_ready")
        ws_hi = sem("ws_hi")
        ws_lo = sem("ws_lo")
        tanh_done = sem("tanh_done")
        tgs_done = sem("tgs_done")
        t_mm = sem("t_mm")
        t_sq = sem("t_sq")
        t_norm = sem("t_norm")
        t_sqrt = sem("t_sqrt")
        rt_ready = sem("rt_ready")
        ve1_ready = sem("ve1_ready")
        sd1_ready = sem("sd1_ready")
        s1 = sem("s1")
        xln = sem("xln")
        t1 = sem("t1")
        xt = sem("xt")
        v_mm = sem("v_mm")
        v_sqr = sem("v_sqr")
        v_sq = sem("v_sq")
        dg = sem("dg")
        rb = sem("rb")
        n_mm = sem("n_mm")
        vn_sq = sem("vn_sq")
        rv_own = sem("rv_own")
        rv_ready = sem("rv_ready")
        m_ready = sem("m_ready")
        dot = sem("dot")
        added = sem("added")
        cos_done = sem("cos_done")
        s2 = sem("s2")
        s2_aggr = sem("s2_aggr")
        s2_rs = sem("s2_rs")
        ve2_ready = sem("ve2_ready")
        sd2_ready = sem("sd2_ready")
        xl2 = sem("xl2")
        t2 = sem("t2")
        x2t = sem("x2t")
        hl2 = sem("hl2")
        r_mm = sem("r_mm")
        st_rows = sem("st_rows")
        st_xt = sem("st_xt")
        sig = sem("sig")
        r = sem("r")
        ohs_ready = sem("ohs_ready")
        rank = sem("rank")
        slots_ok = sem("slots_ok")
        routed_ok = sem("routed_ok")
        pad_zero = sem("pad_zero")
        ix_copy = sem("ix_copy")
        scat = [sem(f"scat{i}") for i in range(4)]
        ld_idx = sem("ld_idx")
        ld_xtc = [sem(f"ld_xtc{i}") for i in range(2)]
        s_h = sem("s_h")
        s_sil = sem("s_sil")
        s_g = sem("s_g")
        s_ghi = sem("s_ghi")
        s_glo = sem("s_glo")
        s_y = sem("s_y")
        s_glo0 = sem("s_glo0")
        s_base = sem("s_base")
        products = sem("products")
        bef_ready = sem("bef_ready")
        word_mm = sem("word_mm")
        ld_stage = [sem(f"ld_stage{i}") for i in range(2)]
        w_hi = sem("w_hi")
        w_lo = sem("w_lo")
        xg = [sem(f"xg{i}") for i in range(4)]
        b_ix = sem("b_ix")
        b_tx = sem("b_tx")
        b_xhi = sem("b_xhi")
        b_xlo = sem("b_xlo")
        b_h = sem("b_h")
        b_sil = sem("b_sil")
        b_g = sem("b_g")
        b_tg = sem("b_tg")
        b_ghi = sem("b_ghi")
        b_glo = sem("b_glo")
        b_y = sem("b_y")
        b_yev = sem("b_yev")
        st_y = [sem(f"st_y{i}") for i in range(4)]
        c_ix = sem("c_ix")
        yg = [sem(f"yg{i}") for i in range(4)]
        cmb = sem("cmb")
        st_out = sem("st_out")

        NSMALL = 5 * 16
        WP = WSH // NC
        LAST = NC - 1
        NORM_TILES = ((0, NT // 4), (NT // 4, NT))
        NCA = NC // 2
        NSA = NCA * J
        NPOOL = J + 2
        CUTS = [0] * NPOOL + [2] * (2 * J - NPOOL) + [1, 1, 1, 2] * (J // 2)
        assert len(CUTS) == NSA and sum(CUTS) == 2 * E

        block = ctx.enter_context(nc.Block())

        @block.sync
        def _(sp):
            sp.dma_start(wt[:, :, :], wt_t.rearrange("(k p) h -> p k h", p=KT)).then_inc(ld_text, 16)
            sp.dma_start(btc[:, :], bt.rearrange("(p o) -> p o", o=1)).then_inc(ld_text, 16)
            ctx_k = ctx_t.rearrange("(k p) n -> p k n", p=KT)
            q = TOK // 4
            for i in range(4):
                sp.dma_start(CTX[0:KT, :, i * q:(i + 1) * q], ctx_k[:, :, i * q:(i + 1) * q]).then_inc(ld_ctx[i], 16)
                if i == 0:
                    sp.dma_start(bvc[:, :], bv.rearrange("(p o) -> p o", o=1)).then_inc(ld_small, 16)
                    sp.dma_start(gates_in[:, 0:1], g_xattn.partition_broadcast(P)).then_inc(ld_small, 16)
                    sp.dma_start(gates_in[:, 1:2], g_ffn.partition_broadcast(P)).then_inc(ld_small, 16)
                    sp.dma_start(wv[:, :, :], wv_t.rearrange("(k p) h -> p k h", p=P)).then_inc(ld_small, 16)
                    sp.dma_start(rw[:, :, :], router_w.rearrange("(k p) e -> p k e", p=P)).then_inc(ld_small, 16)
                    sp.dma_start(bias16[:, :], expert_bias.partition_broadcast(P)).then_inc(ld_bias, 16)
                sp.dma_start(X[:, i * (NT // 4):(i + 1) * (NT // 4), :],
                             x_tiles[:, i * (NT // 4):(i + 1) * (NT // 4), :]).then_inc(ld_x[i], 16)
            for w, at in ((shared_w1, 0), (shared_w2, KD * SH)):
                sp.dma_start(SHST[:, at:at + KD * SH].rearrange("p (k n) -> p k n", k=KD),
                             w[0].rearrange("(k p) n -> p k n", p=P)).then_inc(ld_shared, 16)
            sp.dma_start(SHST[:, W3S:WSH].rearrange("p (j n) -> p j n", j=J),
                         shared_w3[0].rearrange("(j p) n -> p j n", p=P)).then_inc(ld_shared, 16)
            sp.wait_ge(c_ready, 1)
            sp.dma_start(slot_token.rearrange("(p b) o -> p (b o)", p=P), zero_idx[:, :]).then_inc(table_zeroed, 16)

            def store_chunk(c):
                sp.wait_ge(xl2, c + 1)
                sp.dma_start(xrow_tiles[:, ds(c * TPC, TPC), :], XL2).then_inc(st_rows, 16)
                sp.wait_ge(hl2, c + 1)
                sp.dma_start(xtd[ds(c * P, P), :], XHL.rearrange("p a k n -> p (a k n)")).then_inc(st_xt, 16)

            with sp.Fori(0, 3) as c:
                store_chunk(c)
            sp.wait_ge(st_xt, 3 * 16)
            for u in range(2):
                sp.dma_start(XTC[:, u, :, :, :].rearrange("p a k n -> p (a k n)"),
                             xtd[u * P:(u + 1) * P, :]).then_inc(ld_xtc[u], 16)

            with sp.Fori(3, NC) as c:
                store_chunk(c)
            sp.wait_ge(st_rows, NC * 16)
            sp.wait_ge(st_xt, NC * 16)

            def stage(e, u):
                at = STAGE[:, u, 0:W3E].rearrange("p (k w n) -> p k w n", k=KD, w=2)
                for w, m in enumerate((routed_w1, routed_w2)):
                    sp.dma_start(at[:, :, w, :], m[ds(e, 1), :, :].rearrange("e (k p) n -> p (e k) n", p=P))\
                        .then_inc(ld_stage[u], 16)
                sp.dma_start(STAGE[:, u, W3E:WE].rearrange("p (k n) -> p k n", n=D),
                             routed_w3[ds(e, 1), :, :].rearrange("e (k p) n -> p (e k) n", p=P))\
                    .then_inc(ld_stage[u], 16)

            sp.wait_ge(r_mm, NC)
            for u in range(2):
                stage(UNDER + u, u)
            for first, last, expert in ((1, (E - UNDER) // 2, UNDER), ((E - UNDER) // 2, E // 2, UNDER - E)):
                with sp.Fori(first, last) as i:
                    for u in range(2):
                        sp.wait_ge(w_lo, i * 4 + (2 * u - 2))
                        stage(i * 2 + (u + expert), u)
            with sp.Fori(0, NBLK // 4) as i:
                for u in range(4):
                    sp.wait_ge(b_yev, i * 4 + (u + 1))
                    sp.dma_start(yrow[ds(i * (4 * P) + u * P, P), :], YS[:, u, :]).then_inc(st_y[u], 16)
            for u in range(2):
                sp.wait_ge(s_h, (NCA + 1 + u) * J)
                sp.dma_start(XTC[:, u, :, :, :].rearrange("p a k n -> p (a k n)"),
                             xtd[(NC - 2 + u) * P:(NC - 1 + u) * P, :]).then_inc(ld_xtc[u], 16)
            with sp.Fori(0, NC) as c:
                sp.wait_ge(s_base, c + 1)
                sp.wait_ge(cmb, c * (2 * TPC) + 2 * TPC)
                sp.dma_start(out_tiles[:, ds(c * TPC, TPC), :], X[:, ds(c * TPC, TPC), :]).then_inc(st_out, 16)
            sp.wait_ge(st_out, NC * 16)
            for u in range(4):
                sp.wait_ge(st_y[u], NBLK // 4 * 16)

        @block.gpsimd
        def _(pool):
            pool.memset(ident[:, :], 0.0).then_inc(c_mem, 1)
            pool.memset(before[:, :], 1.0).then_inc(c_mem, 1)
            pool.memset(ones[:, :], 1.0)
            pool.memset(zero_idx[:, :], 0)
            pool.iota(tokid[:, :], pattern=[[P, NT]], base=0, channel_multiplier=1)
            pool.wait_ge(c_mem, 2)
            pool.affine_select(out=ident[:, :], in_=ident[:, :], compare_op=ALU.not_equal, fill=1.0,
                               base=0, pattern=[[-1, P]], channel_multiplier=1)
            pool.affine_select(out=before[:, :], in_=before[:, :], compare_op=ALU.is_ge, fill=0.0,
                               base=-1, pattern=[[1, P]], channel_multiplier=-1).then_inc(c_ready, 1)
            pool.iota(row_iota[:, :], pattern=[[0, 1]], base=0, channel_multiplier=1,
                      allow_small_or_imprecise_dtypes=True)
            pool.memset(pack[:, :], 0.0).then_inc(c_mem, 1)
            for k in range(6):
                pool.wait_ge(c_mem, 3 + k)
                pool.affine_select(out=pack[:, :], in_=pack[:, :], compare_op=ALU.not_equal, fill=float(E ** k),
                                   base=2 - k, pattern=[[-4, NBLK // 4]], channel_multiplier=1).then_inc(c_mem, 1)
            pool.iota(rev[:, :], pattern=[[-1, E]], base=E, channel_multiplier=0,
                      allow_small_or_imprecise_dtypes=True).then_inc(c_ready, 1)
            def diagonal(c, first=False):
                if first:
                    pool.wait_ge(rt_ready, 1)
                else:
                    pool.wait_ge(rb, c)
                pool.tensor_tensor(DG, ident[:, :].unsqueeze(1).to_broadcast([P, TPC, P]),
                                   rt[:, ds(c * TPC, TPC)].unsqueeze(2).to_broadcast([P, TPC, P]),
                                   ALU.mult).then_inc(dg, 1)

            def cut(c):
                pool.wait_ge(x2t, c * 2 + 2)
                pool.sem_inc(pool_apart, 1)
                pool.tensor_tensor(XHL[:, 1], X2T, XHL[:, 0], ALU.subtract).then_inc(hl2, 1)

            def add_attention(c):
                for u in range(2):
                    pool.wait_ge(cos_done, c * 2 + (u + 1))
                    xs = X[:, ds(c * TPC + 2 * u, 2), :]
                    pool.tensor_tensor(xs, xs, M[:, 2 * u:2 * u + 2, :], ALU.add).then_inc(added, 1)

            diagonal(0, True)
            diagonal(1)
            add_attention(0)
            diagonal(2)
            with pool.Fori(1, NC - 2) as c:
                add_attention(c)
                cut(c - 1)
                diagonal(c + 2)
            add_attention(NC - 2)
            cut(NC - 3)
            add_attention(NC - 1)
            cut(NC - 2)
            cut(NC - 1)

            for n in range(NPOOL):
                pool.wait_ge(s_ghi, n + 1)
                pool.tensor_tensor(GS[:, n % 2, 1, :], G[:, n % 2, :], GS[:, n % 2, 0, :], ALU.subtract)\
                    .then_inc(s_glo0, 1)
                if n == 3:
                    pool.wait_ge(ohs_ready, 1)
                    pool.tensor_tensor(SEL, OH[0], SCS, ALU.mult)
                    pool.tensor_tensor(RE, OH[1], SCS, ALU.mult).then_inc(products, 1)

            pool.wait_ge(slots_ok, 1)
            pool.wait_ge(table_zeroed, 16)

            def scatter(i, u, first=False):
                t = i * 4 + u
                if not first:
                    pool.wait_ge(scat[u], i * 32)
                pool.sem_inc(pool_apart, 1)
                pool.tensor_copy(ixs[:, u, :], sloti[:, :, ds(t, 1)].rearrange("p a b -> p (a b)"))
                pool.tensor_copy(tks[:, u:u + 1], tokid[:, ds(t, 1)]).then_inc(ix_copy, 1)
                pool.wait_ge(ix_copy, t + 1)
                pool.sem_inc(pool_apart, 1)
                for k in range(2):
                    pool.indirect_dma_start(out=slot_token, in_=tks[:, u:u + 1], in_offset=None,
                                            out_offset=bass.IndirectOffsetOnAxis(
                                                ap=ixs[:, u, k:k + 1].bitcast(U32), axis=0))\
                        .then_inc(scat[u], 16)

            for u in range(4):
                scatter(0, u, True)
            with pool.Fori(1, NT // 4) as i:
                for u in range(4):
                    scatter(i, u)
            for u in range(4):
                pool.wait_ge(scat[u], NT // 4 * 32)
            pool.dma_start(idx[:, :], slot_token.rearrange("(p b) o -> p (b o)", p=P)).then_inc(ld_idx, 16)
            pool.wait_ge(ld_idx, 16)
            pool.wait_ge(st_rows, NC * 16)

            def fetch(i, u, first=False):
                b = i * 4 + u
                if not first:
                    pool.wait_ge(b_tx, i * 4 + (u - 3))
                pool.sem_inc(pool_apart, 1)
                pool.tensor_copy(ixb[:, u:u + 1], idx[:, ds(b, 1)]).then_inc(b_ix, 1)
                pool.wait_ge(b_ix, b + 1)
                pool.sem_inc(pool_apart, 1)
                pool.indirect_dma_start(out=XG[:, u, :], out_offset=None, in_=xrow,
                                        in_offset=bass.IndirectOffsetOnAxis(
                                            ap=ixb[:, u:u + 1].bitcast(U32), axis=0)).then_inc(xg[u], 16)

            for u in range(4):
                fetch(0, u, True)
            with pool.Fori(1, NBLK // 4) as i:
                for u in range(4):
                    fetch(i, u)

            pool.wait_ge(b_tx, NBLK)
            for u in range(4):
                pool.wait_ge(st_y[u], NBLK // 4 * 16)

            def bring(i, u, first=False):
                t = i * 4 + u
                if not first:
                    pool.wait_ge(cmb, i * 8 + (2 * u - 6))
                pool.sem_inc(pool_apart, 1)
                pool.tensor_copy(ixc[:, u, :], posi[:, :, ds(t, 1)].rearrange("p a b -> p (a b)")).then_inc(c_ix, 1)
                pool.wait_ge(c_ix, t + 1)
                pool.sem_inc(pool_apart, 1)
                for k in range(2):
                    pool.indirect_dma_start(out=YG[:, u, k, :], out_offset=None, in_=yrow,
                                            in_offset=bass.IndirectOffsetOnAxis(
                                                ap=ixc[:, u, k:k + 1].bitcast(U32), axis=0))\
                        .then_inc(yg[u], 16)

            for u in range(4):
                bring(0, u, True)
            with pool.Fori(1, NT // 4) as i:
                for u in range(4):
                    bring(i, u)

        @block.scalar
        def _(act):
            act.preload_act_table(ACT.Sqrt)
            act.wait_ge(ld_text, 32)
            def text(c):
                u = c % 2
                act.wait_ge(t_mm, c + 1)
                act.activation(TT[:, c * CW:(c + 1) * CW], bank[u][:, :], ACT.Identity, bias=btc[:, :])
                if c >= 2:
                    act.wait_ge(t_norm, c - 1)
                act.activation(SQT[:, u, :], bank[u][:, :], ACT.Square, bias=btc[:, :]).then_inc(t_sq, 1)

            def deviation1(i):
                tiles = slice(*NORM_TILES[i])
                act.wait_ge(ve1_ready, i + 1)
                act.activation(tmp1[:, tiles], var1[:, tiles], ACT.Sqrt).then_inc(sd1_ready, 1)

            def lead(c, first=False):
                for u in range(2):
                    act.wait_ge(t1, c * 2 + (u + 1))
                    if u == 0 and not first:
                        act.wait_ge(v_mm, c)
                    act.activation(XT[:, :, u * D:(u + 1) * D],
                                   bank[3 + u][:, :].rearrange("p (k n) -> p k n", k=KD), ACT.Copy).then_inc(xt, 1)

            def lead_v(c, first=False):
                act.wait_ge(v_mm, c + 1)
                if not first:
                    act.wait_ge(n_mm, c)
                act.activation(SQV, bank[5][:, :], ACT.Square, bias=bvc[:, :]).then_inc(v_sqr, 1)
                if not first:
                    act.wait_ge(dot, c * 2)
                act.activation(VT, bank[5][:, :], ACT.Identity, bias=tbv[:, :], scale=tg[:, 0:1]).then_inc(v_sq, 1)

            def lead_norm(c, first=False):
                act.wait_ge(n_mm, c + 1)
                if not first:
                    act.wait_ge(rv_ready, c)
                act.activation(vn[:, :], bank[2][:, 0:TPC], ACT.Sqrt).then_inc(vn_sq, 1)

            def scales(c, first=False):
                act.wait_ge(rv_ready, c + 1)
                act.wait_ge(rb, c + 1)
                for u in range(2):
                    if not first:
                        act.wait_ge(added, c * 2 + (u - 1))
                    for i in range(2):
                        last = act.activation(M[:, 2 * u + i, :], bank[6][:, u * D:(u + 1) * D], ACT.Copy,
                                              scale=rv[:, 2 * u + i:2 * u + i + 1])
                    last.then_inc(m_ready, 1)

            def lag(c, first=False):
                for u in range(2):
                    act.wait_ge(t2, c * 2 + (u + 1))
                    if u == 0 and not first:
                        act.wait_ge(r_mm, c)
                        act.wait_ge(hl2, c)
                        act.wait_ge(st_xt, c * 16)
                    half = bank[3 + u][:, :].rearrange("p (k n) -> p k n", k=KD)
                    act.activation(X2T[:, :, u * D:(u + 1) * D], half, ACT.Copy)
                    act.activation(XHL[:, 0, :, u * D:(u + 1) * D], half, ACT.Copy).then_inc(x2t, 1)

            def weights_hi(c):
                act.activation(WS[:, 0, ds(c * WP, WP)], SHST[:, ds(c * WP, WP)], ACT.Copy, scale=WSCALE)\
                    .then_inc(ws_hi, 1)

            def deviation(c):
                act.wait_ge(ve2_ready, c + 1)
                act.activation(sd2[:, :], ve2[:, :], ACT.Sqrt).then_inc(sd2_ready, 1)

            text(0)
            act.wait_ge(ld_small, NSMALL)
            act.activation(tg[:, :], gates_in[:, :], ACT.Tanh).then_inc(tanh_done, 1)
            text(1)
            deviation1(0)
            text(2)
            text(3)
            lead(0, True)
            text(4)
            text(5)
            act.wait_ge(tgs_done, 1)
            lead_v(0, True)
            text(6)
            deviation1(1)
            text(7)
            act.wait_ge(t_norm, NC)
            act.activation(tn[:, :], bank[2][:, 0:NT], ACT.Sqrt).then_inc(t_sqrt, 1)
            lead_norm(0, True)
            lead(1)
            scales(0, True)
            lead_v(1)
            lead_norm(1)
            deviation(0)
            act.wait_ge(ld_shared, 48)
            weights_hi(0)
            weights_hi(1)
            lead(2)
            scales(1)
            lag(0, True)
            lead_v(2)
            lead_norm(2)
            deviation(1)
            weights_hi(2)
            with act.Fori(2, LAST) as c:
                lead(c + 1)
                scales(c)
                lag(c - 1)
                lead_v(c + 1)
                lead_norm(c + 1)
                deviation(c)
                weights_hi(c + 1)
            scales(LAST)
            lag(LAST - 1)
            deviation(LAST)

            def silu(n, j, first=False):
                a = j % 2
                act.wait_ge(s_h, n + 1)
                if not first:
                    act.wait_ge(s_g, n - 1)
                act.activation(SIL[:, a, :], HIDDEN[a][0][:, :], ACT.Silu, scale=1.0 / WSCALE).then_inc(s_sil, 1)

            def hidden_hi(n, j, first=False):
                a = j % 2
                act.wait_ge(s_g, n + 1)
                if not first:
                    act.wait_ge(s_y, n - 1)
                act.activation(GS[:, a, 0, :], G[:, a, :], ACT.Copy).then_inc(s_ghi, 1)

            def routed_hi(m, h):
                e = (m + UNDER) % E
                if h == 0:
                    act.wait_ge(ld_stage[m % 2], (m // 2 + 1) * 48)
                act.activation(WR[:, e * (2 * WE) + h * WH:e * (2 * WE) + (h + 1) * WH],
                               STAGE[:, m % 2, h * WH:(h + 1) * WH], ACT.Copy, scale=WSCALE).then_inc(w_hi, 1)

            act.preload_act_table(ACT.Silu)
            silu(0, 0, True)
            lag(LAST)
            hidden_hi(0, 0, True)
            silu(1, 1, True)
            hidden_hi(1, 1, True)
            act.preload_act_table(ACT.Sigmoid)
            act.wait_ge(r_mm, NC)
            act.activation(SCS.rearrange("p a b -> p (a b)"), bank[7][:, :], ACT.Sigmoid).then_inc(sig, 1)
            act.preload_act_table(ACT.Silu)
            half = 0
            for n in range(2, NSA):
                silu(n, n % J)
                hidden_hi(n, n % J)
                for p in range(half, half + CUTS[n]):
                    if p == 2 * (E - UNDER):
                        act.wait_ge(routed_ok, 1)
                    routed_hi(p // 2, p % 2)
                half += CUTS[n]
                if n % J == J - 1:
                    c = n // J
                    act.dma_start(XTC[:, c % 2, :, :, :].rearrange("p a k n -> p (a k n)"),
                                  xtd[(c + 2) * P:(c + 3) * P, :]).then_inc(ld_xtc[c % 2], 16)

            def x_hi(b, u, first=False):
                act.wait_ge(b_tx, b + 1)
                if not first:
                    act.wait_ge(b_h, b - 1)
                act.activation(XTB[:, u, 0], bank[2][:, 0:KD * P].rearrange("p (k n) -> p k n", k=KD), ACT.Copy)\
                    .then_inc(b_xhi, 1)

            def r_silu(b, u, first=False):
                act.wait_ge(b_h, b + 1)
                if not first:
                    act.wait_ge(b_g, b - 1)
                act.activation(SIL[:, u, 0:RH], bank[u][:, 0:RH], ACT.Silu, scale=1.0 / WSCALE).then_inc(b_sil, 1)

            def g_hi(b, u, first=False):
                act.wait_ge(b_tg, b + 1)
                if not first:
                    act.wait_ge(b_y, b - 1)
                act.activation(GT[:, u, 0], bank[3][:, 0:RH].rearrange("p (k n) -> p k n", k=RH // P), ACT.Copy)\
                    .then_inc(b_ghi, 1)

            act.wait_ge(s_g, NSA)
            x_hi(0, 0, True)
            x_hi(1, 1, True)
            for b in range(4):
                r_silu(b, b % 2, b < 2)
                if b >= 1:
                    g_hi(b - 1, (b - 1) % 2, b - 1 < 2)
                x_hi(b + 2, b % 2)
            with act.Fori(1, NBLK // 4 - 1) as i:
                for k in range(4):
                    b = i * 4 + k
                    r_silu(b, k % 2)
                    g_hi(b - 1, (k + 1) % 2)
                    x_hi(b + 2, k % 2)
            for b in range(NBLK - 4, NBLK):
                r_silu(b, b % 2)
                g_hi(b - 1, (b - 1) % 2)
                if b + 2 < NBLK:
                    x_hi(b + 2, b % 2)
            g_hi(NBLK - 1, 1)

            act.wait_ge(b_g, NBLK)
            with act.Fori(NCA // 2, NC // 2) as i:
                for k in range(2 * J):
                    silu(i * (2 * J) + k, k % J)
                    hidden_hi(i * (2 * J) + k, k % J)

        @block.vector
        def _(dve):
            own1 = [0]

            def link1(ins):
                own1[0] += 1
                ins.then_inc(s1, 1)
                dve.wait_ge(s1, own1[0])

            def statistics(g):
                dve.wait_ge(ld_x[g], 16)
                for t in range(g * (NT // 4), (g + 1) * (NT // 4)):
                    last = dve.bn_stats(st[:, t, :], X[:, t, :])
                link1(last)

            def variances(i):
                tiles = slice(*NORM_TILES[i])
                dve.tensor_tensor(mean1[:, tiles], st[:, tiles, 1], st[:, tiles, 4], ALU.add)
                dve.tensor_tensor(gsum[:, tiles], st[:, tiles, 1], st[:, tiles, 4], ALU.subtract)
                link1(dve.tensor_tensor(var1[:, tiles], st[:, tiles, 2], st[:, tiles, 5], ALU.add))
                dve.tensor_scalar(mean1[:, tiles], mean1[:, tiles], 0.5, None, ALU.mult)
                dve.tensor_scalar(gsum[:, tiles], gsum[:, tiles], 0.5, None, ALU.mult)
                link1(dve.tensor_scalar(var1[:, tiles], var1[:, tiles], 1.0 / D, LN_EPS, ALU.mult, ALU.add))
                link1(dve.tensor_tensor(rstd1[:, tiles], gsum[:, tiles], gsum[:, tiles], ALU.mult))
                dve.tensor_tensor(var1[:, tiles], var1[:, tiles], rstd1[:, tiles], ALU.add).then_inc(ve1_ready, 1)

            def inverse_deviations(i):
                tiles = slice(*NORM_TILES[i])
                dve.wait_ge(sd1_ready, i + 1)
                link1(dve.reciprocal(rstd1[:, tiles], tmp1[:, tiles]))

            def normalise(c, first=False):
                if not first:
                    dve.wait_ge(t1, c * 2)
                for k in range(TPC):
                    t = c * TPC + k
                    last = dve.tensor_scalar(XL[:, k, :], X[:, ds(t, 1), :].rearrange("p a n -> p (a n)"),
                                             mean1[:, ds(t, 1)], rstd1[:, ds(t, 1)], ALU.subtract, ALU.mult)
                last.then_inc(xln, 1)

            def inverse_norm(c, first=False):
                dve.wait_ge(vn_sq, c + 1)
                if not first:
                    dve.wait_ge(m_ready, c * 2)
                dve.tensor_scalar(vn[:, :], vn[:, :], TINY, None, ALU.max).then_inc(rv_own, 1)
                dve.wait_ge(rv_own, c + 1)
                dve.reciprocal(rv[:, :], vn[:, :]).then_inc(rv_ready, 1)

            def attend(c):
                for u in range(2):
                    dve.wait_ge(dot, c * 2 + (u + 1))
                    dve.wait_ge(m_ready, c * 2 + (u + 1))
                    for i in range(2):
                        last = dve.scalar_tensor_tensor(out=M[:, 2 * u + i, :], in0=M[:, 2 * u + i, :], scalar=INV_EPS,
                                                        in1=bank[u][:, i * D:(i + 1) * D],
                                                        op0=ALU.min, op1=ALU.mult)
                    last.then_inc(cos_done, 1)

            def statistics2(c):
                for u in range(2):
                    dve.wait_ge(added, c * 2 + (u + 1))
                    dve.sem_inc(dve_apart, 1)
                    for i in range(2):
                        last = dve.bn_stats(st2[:, 2 * u + i, :],
                                            X[:, ds(c * TPC + (2 * u + i), 1), :].rearrange("p a n -> p (a n)"))
                last.then_inc(s2, 1)
                dve.wait_ge(s2, c + 1)
                dve.sem_inc(dve_apart, 1)
                for i in range(TPC):
                    last = dve.bn_aggr(mv2[:, i, :], st2[:, i, :])
                last.then_inc(s2_aggr, 1)
                dve.wait_ge(s2_aggr, c + 1)
                dve.tensor_scalar(ve2[:, :], mv2[:, :, 1], LN_EPS, None, ALU.add).then_inc(ve2_ready, 1)

            def normalise2(c, first=False):
                dve.wait_ge(sd2_ready, c + 1)
                dve.reciprocal(rs2[:, :], sd2[:, :]).then_inc(s2_rs, 1)
                dve.wait_ge(s2_rs, c + 1)
                if not first:
                    dve.wait_ge(t2, c * 2)
                    dve.wait_ge(st_rows, c * 16)
                for k in range(TPC):
                    last = dve.tensor_scalar(XL2[:, k, :],
                                             X[:, ds(c * TPC + k, 1), :].rearrange("p a n -> p (a n)"),
                                             mv2[:, k, 0:1], rs2[:, k:k + 1], ALU.subtract, ALU.mult)
                last.then_inc(xl2, 1)

            def weights_lo(c):
                dve.wait_ge(ws_hi, c + 1)
                dve.scalar_tensor_tensor(out=WS[:, 1, ds(c * WP, WP)], in0=SHST[:, ds(c * WP, WP)], scalar=WSCALE,
                                         in1=WS[:, 0, ds(c * WP, WP)], op0=ALU.mult, op1=ALU.subtract)\
                    .then_inc(ws_lo, 1)

            statistics(0)
            variances(0)
            statistics(1)
            dve.wait_ge(tanh_done, 1)
            dve.tensor_scalar(tbv[:, :], bvc[:, :], tg[:, 0:1], None, ALU.mult)
            dve.tensor_scalar(tgs[:, :], tg[:, 1:2], 1.0 / WSCALE, None, ALU.mult).then_inc(tgs_done, 1)
            inverse_deviations(0)
            normalise(0, True)
            statistics(2)
            statistics(3)
            variances(1)
            normalise(1)
            inverse_deviations(1)
            dve.wait_ge(t_sqrt, 1)
            link1(dve.tensor_scalar(tn[:, :], tn[:, :], TINY, None, ALU.max))
            dve.reciprocal(rt[:, :], tn[:, :]).then_inc(rt_ready, 1)
            inverse_norm(0, True)
            attend(0)
            normalise(2)
            statistics2(0)
            normalise2(0, True)
            inverse_norm(1)
            weights_lo(0)
            with dve.Fori(1, LAST - 1) as c:
                attend(c)
                normalise(c + 2)
                weights_lo(c)
                statistics2(c)
                normalise2(c)
                inverse_norm(c + 1)
            attend(LAST - 1)
            weights_lo(LAST - 1)
            statistics2(LAST - 1)
            normalise2(LAST - 1)
            inverse_norm(LAST)
            attend(LAST)
            weights_lo(LAST)
            statistics2(LAST)
            normalise2(LAST)

            own = [0]

            def link(ins):
                own[0] += 1
                ins.then_inc(r, 1)
                dve.wait_ge(r, own[0])

            def over_tiles(a):
                return a.unsqueeze(1).to_broadcast([P, NT, E])

            def over_experts(a):
                return a.unsqueeze(2).to_broadcast([P, NT, E])

            PADT = NT // 2
            PADE = E // 2

            def rows_flat(a):
                return a.rearrange("p a b -> p (a b)")

            def prepare():
                dve.memset(INCA[:, 0:PADT, :], 0.0)
                dve.memset(INCB[:, 0:PADT, :], 0.0)
                dve.memset(ea[:, 0:PADE], 0.0)
                dve.memset(eb[:, 0:PADE], 0.0)

            def selection_scores():
                dve.wait_ge(ld_bias, 16)
                dve.wait_ge(c_ready, 2)
                dve.wait_ge(sig, 1)
                link(dve.tensor_tensor(SEL, SCS, over_tiles(bias16[:, :]), ALU.add))

            def choose(k):
                link(dve.tensor_reduce(m1[:, :], SEL, AX.X, ALU.max))
                link(dve.tensor_tensor(EQ, SEL, over_experts(m1[:, :]), ALU.is_equal))

            def choose_lowest(k):
                link(dve.tensor_tensor(RE, EQ, over_tiles(rev[:, :]), ALU.mult))
                link(dve.tensor_reduce(rm[:, :], RE, AX.X, ALU.max))
                link(dve.tensor_tensor(OH[k], over_experts(rm[:, :]), over_tiles(rev[:, :]), ALU.is_equal))

            def exclude_first():
                link(dve.scalar_tensor_tensor(out=SEL, in0=OH[0], scalar=-1e30, in1=SEL,
                                              op0=ALU.mult, op1=ALU.add))

            def gates():
                dve.wait_ge(products, 1)
                for k, chosen in enumerate((SEL, RE)):
                    link(dve.tensor_reduce(gsum[:, :], chosen, AX.X, ALU.add))
                    link(dve.tensor_scalar(gate[:, k, :], gsum[:, :], tgs[:, :], None, ALU.mult))

            def take_totals():
                dve.wait_ge(rank, 2)
                link(dve.tensor_copy(rows_flat(INCA[:, PADT:PADT + NT, :]), bank[7][:, :]))

            def sum_tiles(src, dst, step):
                link(dve.tensor_tensor(dst[:, PADT:PADT + NT, :], src[:, PADT:PADT + NT, :],
                                       src[:, PADT - step:PADT - step + NT, :], ALU.add))

            def sum_experts(inc):
                link(dve.tensor_scalar(ni[:, :], inc[:, PADT + NT - 1, :], float(P - 1), None, ALU.add))
                link(dve.tensor_scalar(bi[:, :], ni[:, :], 7, None, ALU.arith_shift_right))
                dve.tensor_copy(bf[:, :], bi[:, :])
                link(dve.tensor_copy(ea[:, PADE:PADE + E], bi[:, :]))
                es, ed = ea, eb
                step = 1
                while step < E:
                    link(dve.tensor_tensor(ed[:, PADE:PADE + E], es[:, PADE:PADE + E],
                                           es[:, PADE - step:PADE - step + E], ALU.add))
                    es, ed = ed, es
                    step *= 2
                ends = es[:, PADE:PADE + E]
                link(dve.tensor_tensor(nf[:, :], ends, bf[:, :], ALU.subtract))
                link(dve.tensor_scalar(base_row[:, :], nf[:, :], float(P), None, ALU.mult))
                return ends

            def slots_of_all(inc):
                link(dve.tensor_tensor(rows_flat(PA), rows_flat(inc[:, PADT:PADT + NT, :]), bank[7][:, :],
                                       ALU.subtract))
                link(dve.tensor_tensor(PB, PA, over_tiles(base_row[:, :]), ALU.add))
                link(dve.tensor_tensor(rows_flat(PA), rows_flat(PB), bank[6][:, :], ALU.add))

            def slots_of_choice(k):
                link(dve.tensor_tensor(EQ, OH[k], PA, ALU.mult))
                link(dve.tensor_reduce(gsum[:, :], EQ, AX.X, ALU.add))
                link(dve.tensor_copy(posi[:, k, :], gsum[:, :]))

            def table_slots():
                dve.tensor_scalar(lowi[:, :, :], posi[:, :, :], P - 1, None, ALU.bitwise_and)
                link(dve.tensor_scalar(highi[:, :, :], posi[:, :, :], 7, None, ALU.arith_shift_right))
                dve.scalar_tensor_tensor(out=sloti[:, :, :], in0=lowi[:, :, :], scalar=float(NBLK),
                                         in1=highi[:, :, :], op0=ALU.mult, op1=ALU.add).then_inc(slots_ok, 1)

            def block_experts(ends):
                link(dve.tensor_scalar(ended[:, :], ends, row_iota[:, :], None, ALU.is_le))
                link(dve.tensor_reduce(bef[:, :], ended[:, :], AX.X, ALU.add))
                dve.tensor_scalar(bef[:, :], bef[:, :], float(E - 1), None, ALU.min).then_inc(bef_ready, 1)

            def block_words():
                dve.wait_ge(word_mm, 1)
                dve.tensor_copy(blk_word[:, :], bank[6][0:1, 0:NBLK // 4]).then_inc(routed_ok, 1)

            def add_shared(c, combined=None):
                dve.wait_ge(s_y, c * J + J)
                if combined is not None:
                    dve.wait_ge(cmb, combined)
                for k in range(TPC):
                    xs = X[:, ds(c * TPC + k, 1), :].rearrange("p a n -> p (a n)")
                    last = dve.scalar_tensor_tensor(out=xs, in0=SHARED_ROWS[k // 2][:, (k % 2) * D:(k % 2 + 1) * D],
                                                    scalar=tgs[:, :], in1=xs, op0=ALU.mult, op1=ALU.add)
                last.then_inc(s_base, 1)

            def add_routed(t, slot, count, chunks):
                dve.wait_ge(yg[slot], count)
                dve.wait_ge(s_base, chunks)
                xs = X[:, ds(t, 1), :].rearrange("p a n -> p (a n)")
                for k in range(2):
                    if k == 1:
                        dve.wait_ge(cmb, t * 2 + 1)
                    dve.scalar_tensor_tensor(out=xs, in0=YG[:, slot, k, :], scalar=gate[:, k, ds(t, 1)],
                                             in1=xs, op0=ALU.mult, op1=ALU.add).then_inc(cmb, 1)

            def gate_hidden(n, j, first=False, pool=None):
                a = j % 2
                dve.wait_ge(s_sil, n + 1)
                if not first:
                    dve.wait_ge(s_ghi, n - 1)
                if pool is not None:
                    dve.wait_ge(s_glo0, pool)
                dve.scalar_tensor_tensor(out=G[:, a, :], in0=HIDDEN[a][1][:, :], scalar=1.0 / WSCALE,
                                         in1=SIL[:, a, :], op0=ALU.mult, op1=ALU.mult).then_inc(s_g, 1)

            def hidden_lo(n, j):
                a = j % 2
                dve.wait_ge(s_ghi, n + 1)
                dve.tensor_tensor(GS[:, a, 1, :], G[:, a, :], GS[:, a, 0, :], ALU.subtract).then_inc(s_glo, 1)

            def routed_lo(m, h):
                at = (m + UNDER) % E * (2 * WE) + h * WH
                dve.wait_ge(w_hi, m * 2 + (h + 1))
                dve.scalar_tensor_tensor(out=WR[:, at + WE:at + WE + WH], in0=STAGE[:, m % 2, h * WH:(h + 1) * WH],
                                         scalar=WSCALE, in1=WR[:, at:at + WH], op0=ALU.mult, op1=ALU.subtract)\
                    .then_inc(w_lo, 1)

            prepare()
            gate_hidden(0, 0, True)
            gate_hidden(1, 1, True)
            selection_scores()
            choose(0)
            gate_hidden(2, 0, pool=1)
            choose_lowest(0)
            exclude_first()
            gate_hidden(3, 1, pool=2)
            choose(1)
            choose_lowest(1)
            dve.tensor_tensor(OHS, OH[0], OH[1], ALU.add).then_inc(ohs_ready, 1)
            gate_hidden(4, 0, pool=3)
            gate_hidden(5, 1, pool=4)
            take_totals()
            sum_tiles(INCA, INCB, 1)
            sum_tiles(INCB, INCA, 2)
            sum_tiles(INCA, INCB, 4)
            gate_hidden(6, 0, pool=5)
            sum_tiles(INCB, INCA, 8)
            sum_tiles(INCA, INCB, 16)
            ends = sum_experts(INCB)
            gate_hidden(7, 1, pool=6)
            slots_of_all(INCB)
            block_experts(ends)
            gate_hidden(8, 0, pool=7)
            add_shared(0)
            slots_of_choice(0)
            slots_of_choice(1)
            table_slots()
            gate_hidden(9, 1, pool=8)
            gates()
            block_words()
            half = 0
            for n in range(NPOOL, NSA):
                gate_hidden(n, n % J, pool=n - 1 if n < NPOOL + 2 else None)
                if n % J == 0:
                    add_shared(n // J - 1)
                hidden_lo(n, n % J)
                for p in range(half, half + CUTS[n]):
                    routed_lo(p // 2, p % 2)
                half += CUTS[n]
            add_shared(NCA - 1)

            def x_lo(b, u):
                dve.wait_ge(b_xhi, b + 1)
                dve.tensor_tensor(XTB[:, u, 1], bank[2][:, 0:KD * P].rearrange("p (k n) -> p k n", k=KD),
                                  XTB[:, u, 0], ALU.subtract).then_inc(b_xlo, 1)

            def gated(b, u, first=False):
                dve.wait_ge(b_sil, b + 1)
                if not first:
                    dve.wait_ge(b_tg, b - 1)
                dve.scalar_tensor_tensor(out=G[:, u, 0:RH], in0=bank[u][:, RH:2 * RH], scalar=1.0 / WSCALE,
                                         in1=SIL[:, u, 0:RH], op0=ALU.mult, op1=ALU.mult).then_inc(b_g, 1)

            def g_lo(b, u):
                dve.wait_ge(b_ghi, b + 1)
                dve.tensor_tensor(GT[:, u, 1], bank[3][:, 0:RH].rearrange("p (k n) -> p k n", k=RH // P),
                                  GT[:, u, 0], ALU.subtract).then_inc(b_glo, 1)

            def rows(b, i, u, first=False):
                dve.wait_ge(b_y, b + 1)
                if not first:
                    dve.wait_ge(st_y[u], i * 16)
                dve.tensor_copy(YS[:, u, :], bank[4][:, 0:D]).then_inc(b_yev, 1)

            dve.wait_ge(s_y, NSA)
            x_lo(0, 0)
            x_lo(1, 1)
            for b in range(4):
                gated(b, b % 2, b < 2)
                if b >= 1:
                    g_lo(b - 1, (b - 1) % 2)
                x_lo(b + 2, b % 2)
                if b >= 2:
                    rows(b - 2, 0, b - 2, True)
            gated(4, 0)
            g_lo(3, 1)
            x_lo(6, 0)
            rows(2, 0, 2, True)
            gated(5, 1)
            g_lo(4, 0)
            x_lo(7, 1)
            rows(3, 0, 3, True)
            with dve.Fori(1, NBLK // 4 - 1) as i:
                for k in range(4):
                    b = i * 4 + (k + 2)
                    gated(b, k % 2)
                    g_lo(b - 1, (k + 1) % 2)
                    x_lo(b + 2, k % 2)
                    rows(b - 2, i, k)
            for b in range(NBLK - 2, NBLK):
                gated(b, b % 2)
                g_lo(b - 1, (b - 1) % 2)
                rows(b - 2, (b - 2) // 4, (b - 2) % 4)
            g_lo(NBLK - 1, 1)
            rows(NBLK - 2, NBLK // 4 - 1, 2)
            rows(NBLK - 1, NBLK // 4 - 1, 3)

            tiles_of_step = [0, 0, 0, 0, 1, 2, 1, 2, 0, 1, 2, 1, 2, 1, 2, 1]
            assert len(tiles_of_step) == 2 * J and sum(tiles_of_step) == NT // 2

            def two_chunks(i, first=False):
                done = 0
                for k in range(2 * J):
                    gate_hidden(i * (2 * J) + k, k % J)
                    if k % J == 0 and not (first and k == 0):
                        add_shared(i * 2 + (k // J - 1), combined=i * (4 * J) + (2 * done - 2 * NSA))
                    for q in range(done, done + tiles_of_step[k]):
                        add_routed(i * (2 * J) + (q - NSA), q % 4, i * (4 * 32) + (q // 4 + 1 - NSA // 4) * 32,
                                   i * 2 + k // J)
                    done += tiles_of_step[k]
                    hidden_lo(i * (2 * J) + k, k % J)

            two_chunks(NCA // 2, first=True)
            with dve.Fori(NCA // 2 + 1, NC // 2) as i:
                two_chunks(i)
            add_shared(LAST, combined=2 * NT)

        @block.tensor
        def _(pe):
            pe.wait_ge(ld_text, 32)
            pe.wait_ge(c_ready, 1)

            def t_norms(c):
                u = c % 2
                pe.wait_ge(t_sq, c + 1)
                for k in range(TPC):
                    last = pe.matmul(bank[2][:, c * TPC + k:c * TPC + k + 1], SQT[:, u, k * P:(k + 1) * P],
                                     ones[:, 0:1], start=True, stop=True)
                last.then_inc(t_norm, 1)

            def text(c):
                u = c % 2
                if u == 0:
                    pe.wait_ge(ld_ctx[c // 2], 16)
                if c >= 2:
                    pe.wait_ge(t_sq, c - 1)
                for k in range(2):
                    last = pe.matmul(bank[u][:, :], wt[:, k, :], CTX[0:KT, k, c * CW:(c + 1) * CW],
                                     start=(k == 0), stop=(k == 1))
                last.then_inc(t_mm, 1)
                if c >= 1:
                    t_norms(c - 1)

            def transpose1(c, first=False, after_t2=True):
                pe.wait_ge(xln, c + 1)
                for u in range(2):
                    if not first:
                        if after_t2:
                            pe.wait_ge(x2t, c * 2 + (u - 5))
                        else:
                            pe.wait_ge(xt, c * 2 + (u - 1))
                    for k in range(KD):
                        for i in range(2):
                            last = pe.transpose(bank[3 + u][:, k * D + i * P:k * D + (i + 1) * P],
                                                XL[:, 2 * u + i, k * P:(k + 1) * P], ident[:, :])
                    last.then_inc(t1, 1)

            def values(c, first=False):
                pe.wait_ge(xt, c * 2 + 2)
                if not first:
                    pe.wait_ge(v_sq, c)
                for k in range(KD):
                    last = pe.matmul(bank[5][:, :], wv[:, k, :], XT[:, k, :], start=(k == 0), stop=(k == KD - 1))
                last.then_inc(v_mm, 1)

            def row_norms(c, first=False):
                pe.wait_ge(dg, c + 1)
                if not first:
                    pe.wait_ge(m_ready, c * 2)
                pe.matmul(bank[6][:, :], ones[:, :], DG.rearrange("p a b -> p (a b)"), start=True, stop=True)\
                    .then_inc(rb, 1)

            def v_norms(c, first=False):
                pe.wait_ge(v_sqr, c + 1)
                pe.wait_ge(t_sqrt, 1) if first else pe.wait_ge(vn_sq, c)
                for k in range(TPC):
                    last = pe.matmul(bank[2][:, k:k + 1], SQV[:, k * P:(k + 1) * P], ones[:, 0:1],
                                     start=True, stop=True)
                last.then_inc(n_mm, 1)

            def dots(c, first=False):
                pe.wait_ge(v_sq, c + 1)
                for u in range(2):
                    if not first:
                        pe.wait_ge(cos_done, c * 2 + (u - 1))
                    for i in range(2):
                        last = pe.matmul(bank[u][:, i * D:(i + 1) * D], VT[:, (2 * u + i) * P:(2 * u + i + 1) * P],
                                         TT[:, ds(c * CW + u * S, S)], start=True, stop=True)
                    last.then_inc(dot, 1)

            def transpose2(c, tail=False):
                pe.wait_ge(xl2, c + 1)
                for u in range(2):
                    if tail:
                        pe.wait_ge(x2t, c * 2 + (u - 1))
                    else:
                        pe.wait_ge(xt, c * 2 + (u + 5))
                    for k in range(KD):
                        for i in range(2):
                            last = pe.transpose(bank[3 + u][:, k * D + i * P:k * D + (i + 1) * P],
                                                XL2[:, 2 * u + i, k * P:(k + 1) * P], ident[:, :])
                    last.then_inc(t2, 1)

            def router(c):
                pe.wait_ge(x2t, c * 2 + 2)
                for i in range(TPC):
                    for k in range(KD):
                        last = pe.matmul(bank[7][:, ds(c * (TPC * E) + i * E, E)], X2T[:, k, i * P:(i + 1) * P],
                                         rw[:, k, :], start=(k == 0), stop=(k == KD - 1))
                last.then_inc(r_mm, 1)

            for c in range(4):
                text(c)
            pe.wait_ge(ld_small, NSMALL)
            transpose1(0, True)
            text(4)
            text(5)
            values(0, True)
            text(6)
            text(7)
            t_norms(LAST)
            v_norms(0, True)
            dots(0, True)
            transpose1(1, after_t2=False)
            row_norms(0, True)
            values(1)
            row_norms(1)
            v_norms(1)
            transpose1(2, after_t2=False)
            dots(1)
            transpose2(0)
            values(2)
            row_norms(2)
            v_norms(2)
            router(0)
            with pe.Fori(2, LAST) as c:
                transpose1(c + 1)
                dots(c)
                transpose2(c - 1)
                values(c + 1)
                row_norms(c + 1)
                v_norms(c + 1)
                router(c - 1)
            dots(LAST)
            transpose2(LAST - 1, tail=True)

            def ranks():
                pe.wait_ge(ohs_ready, 1)
                pe.matmul(bank[6][:, :], before[:, :], OHS.rearrange("p a b -> p (a b)"), start=True, stop=True)\
                    .then_inc(rank, 1)
                pe.wait_ge(sig, 1)
                pe.matmul(bank[7][:, :], ones[:, :], OHS.rearrange("p a b -> p (a b)"), start=True, stop=True)\
                    .then_inc(rank, 1)

            def words():
                pe.wait_ge(bef_ready, 1)
                pe.matmul(bank[6][0:1, 0:NBLK // 4], bef[0:NBLK, :], pack[0:NBLK, :], start=True, stop=True)\
                    .then_inc(word_mm, 1)

            def hidden(n, u, j, first=False, load=None):
                a = j % 2
                if load is not None:
                    pe.wait_ge(ld_xtc[u], load)
                if not first:
                    pe.wait_ge(s_g, n - 1)
                for w in range(2):
                    acc = HIDDEN[a][w]
                    for k in range(KD):
                        at = (w * KD + k) * SH + j * P
                        for m, (wx, xx) in enumerate(((0, 0), (0, 1), (1, 0))):
                            last = pe.matmul(acc[:, :], WS[:, wx, at:at + P], XTC[:, u, xx, k, :],
                                             start=(k == 0 and m == 0), stop=(k == KD - 1 and m == 2))
                last.then_inc(s_h, 1)

            def shared_rows(n, j, evacuated=None):
                a = j % 2
                if isinstance(n, int) and n < NPOOL:
                    pe.wait_ge(s_glo0, n + 1)
                else:
                    pe.wait_ge(s_glo, n + (1 - NPOOL))
                if evacuated is not None:
                    pe.wait_ge(s_base, evacuated)
                at = W3S + j * D
                for i in range(TPC):
                    acc = SHARED_ROWS[i // 2][:, (i % 2) * D:(i % 2 + 1) * D]
                    for m, (gx, wx) in enumerate(((0, 0), (0, 1), (1, 0))):
                        last = pe.matmul(acc, GS[:, a, gx, i * P:(i + 1) * P], WS[:, wx, at:at + D],
                                         start=(j == 0 and m == 0 and i % 2 == 0), stop=(j == J - 1 and m == 2),
                                         skip_group_check=True)
                last.then_inc(s_y, 1)

            def two_chunks(i, first=False, behind=True):
                for k in range(2 * J):
                    if not (first and k < 2):
                        hidden(i * (2 * J) + k, k // J, k % J, load=(i * 16 + 16) if k % J == 0 else None)
                    if first and k == 5:
                        ranks()
                    if first and k == 9:
                        words()
                    if k >= 1 or behind:
                        shared_rows(i * (2 * J) + (k - 1), (k - 1) % J,
                                    i * 2 + k // J if k % J == 1 and not (first and k == 1) else None)

            pe.wait_ge(ws_lo, NC)
            pe.wait_ge(cos_done, 2 * NC)
            hidden(0, 0, 0, first=True, load=16)
            router(LAST - 1)
            transpose2(LAST, tail=True)
            hidden(1, 0, 1, first=True)
            router(LAST)
            pe.wait_ge(x2t, 2 * NC)
            two_chunks(0, first=True, behind=False)
            with pe.Fori(1, NCA // 2) as i:
                two_chunks(i)
            shared_rows(NSA - 1, J - 1)

            def experts(i):
                w = pe.value_load(blk_word[0:1, ds(i, 1)])
                return [(w >> (4 * k)) & (E - 1) for k in range(6)]

            def weights(e, at, n):
                return WR[:, :].rearrange("p (e n) -> p e n", e=E)[:, ds(e, 1), at:at + n]\
                    .rearrange("p a n -> p (a n)")

            def block_transpose(b, slot, count):
                pe.wait_ge(xg[slot], count)
                if not (isinstance(b, int) and b == 0):
                    pe.wait_ge(b_xlo, b)
                for k in range(KD):
                    last = pe.transpose(bank[2][:, k * P:(k + 1) * P], XG[:, slot, k * P:(k + 1) * P], ident[:, :])
                last.then_inc(b_tx, 1)

            def block_hidden(b, u, e, first=False):
                pe.wait_ge(b_xlo, b + 1)
                if not first:
                    pe.wait_ge(b_g, b - 1)
                for k in range(KD):
                    hi = weights(e, k * 2 * RH, 2 * RH)
                    lo = weights(e, WE + k * 2 * RH, 2 * RH)
                    for m, (xx, w) in enumerate(((0, hi), (0, lo), (1, hi))):
                        last = pe.matmul(bank[u][:, :], XTB[:, u, xx, k, :], w,
                                         start=(k == 0 and m == 0), stop=(k == KD - 1 and m == 2))
                last.then_inc(b_h, 1)

            def hidden_transpose(b, u, first=False):
                pe.wait_ge(b_g, b + 1)
                if not first:
                    pe.wait_ge(b_glo, b)
                for k in range(RH // P):
                    last = pe.transpose(bank[3][:, k * P:(k + 1) * P], G[:, u, k * P:(k + 1) * P], ident[:, :])
                last.then_inc(b_tg, 1)

            def block_rows(b, u, e, first=False):
                pe.wait_ge(b_glo, b + 1)
                if not first:
                    pe.wait_ge(b_yev, b)
                for k in range(RH // P):
                    hi = weights(e, W3E + k * D, D)
                    lo = weights(e, WE + W3E + k * D, D)
                    for m, (gx, w) in enumerate(((0, hi), (0, lo), (1, hi))):
                        last = pe.matmul(bank[4][:, 0:D], GT[:, u, gx, k, :], w,
                                         start=(k == 0 and m == 0), stop=(k == RH // P - 1 and m == 2))
                last.then_inc(b_y, 1)

            pe.wait_ge(routed_ok, 1)
            pe.wait_ge(w_lo, 2 * E)
            pe.wait_ge(s_glo, NSA - NPOOL)
            pe.wait_ge(s_base, NCA)
            block_transpose(0, 0, 16)
            block_transpose(1, 1, 16)
            es = experts(0)
            for b in range(4):
                block_hidden(b, b % 2, es[b + 2], b < 2)
                if b >= 1:
                    hidden_transpose(b - 1, (b - 1) % 2, b == 1)
                block_transpose(b + 2, (b + 2) % 4, 16 * ((b + 2) // 4 + 1))
                if b >= 2:
                    block_rows(b - 2, b % 2, es[b], b == 2)
            with pe.Fori(0, NBLK // 8 - 1) as i:
                for h in range(2):
                    es = experts(i * 2 + (h + 1))
                    for k in range(4):
                        b = i * 8 + (4 + 4 * h + k)
                        block_hidden(b, k % 2, es[k + 2])
                        hidden_transpose(b - 1, (k + 1) % 2)
                        block_transpose(b + 2, (k + 2) % 4, i * 32 + 16 * ((k + 2) // 4 + h + 2))
                        block_rows(b - 2, k % 2, es[k])
            es = experts(NBLK // 4 - 1)
            for k in range(4):
                b = NBLK - 4 + k
                block_hidden(b, b % 2, es[k + 2])
                hidden_transpose(b - 1, (b - 1) % 2)
                if b + 2 < NBLK:
                    block_transpose(b + 2, (b + 2) % 4, 16 * ((b + 2) // 4 + 1))
                block_rows(b - 2, b % 2, es[k])
            hidden_transpose(NBLK - 1, 1)
            block_rows(NBLK - 2, 0, es[4])
            block_rows(NBLK - 1, 1, es[5])

            pe.wait_ge(b_yev, NBLK)
            two_chunks(NCA // 2, behind=False)
            with pe.Fori(NCA // 2 + 1, NC // 2) as i:
                two_chunks(i)
            shared_rows(NC * J - 1, J - 1)


_INS = ["x", "ctx_t", "g_xattn", "g_ffn", "wv_t", "bv", "wt_t", "bt", "router_w", "expert_bias",
        "shared_w1", "shared_w2", "shared_w3", "routed_w1", "routed_w2", "routed_w3"]


def kernel(x, ctx_768, g_xattn, g_ffn, L0_xattn_Wv, L0_xattn_bv, L0_xattn_Wt, L0_xattn_bt, L0_ffn_router_w,
           L0_ffn_expert_bias, L0_ffn_shared_w1, L0_ffn_shared_w2, L0_ffn_shared_w3, L0_ffn_routed_w1,
           L0_ffn_routed_w2, L0_ffn_routed_w3):
    import numpy as np
    import concourse.bacc as bacc
    from concourse.bass_utils import run_bass_kernel_spmd

    ctx_768 = np.asarray(ctx_768)
    given = [x, ctx_768.transpose(2, 0, 1).reshape(ctx_768.shape[2], -1), g_xattn, g_ffn,
             np.asarray(L0_xattn_Wv).T, L0_xattn_bv, np.asarray(L0_xattn_Wt).T, L0_xattn_bt,
             L0_ffn_router_w, L0_ffn_expert_bias, L0_ffn_shared_w1, L0_ffn_shared_w2, L0_ffn_shared_w3,
             L0_ffn_routed_w1, L0_ffn_routed_w2, L0_ffn_routed_w3]
    nc = bacc.Bacc("TRN2", target_bir_lowering=False, num_devices=1)
    arrays, args = {}, []
    for name, a in zip(_INS, given):
        a = np.ascontiguousarray(a)
        arrays[f"in_{name}"] = a
        args.append(nc.dram_tensor(f"in_{name}", a.shape, mybir.dt.from_np(a.dtype), kind="ExternalInput").ap())
    args.append(nc.dram_tensor("out", tuple(x.shape), mybir.dt.float32, kind="ExternalOutput").ap())
    flamingo_block(nc, *args)
    done = run_bass_kernel_spmd(nc, [arrays], core_ids=[0])
    return done.results[0]["out"]
```

```python
import concourse.bass as bass
from concourse import mybir
from contextlib import ExitStack

P = 128


def flamingo_block(nc, x, ctx_t, g_xattn, g_ffn, wv_t, bv, wt_t, bt, router_w, expert_bias,
                   shared_w1, shared_w2, shared_w3, routed_w1, routed_w2, routed_w3, out):
    F32, F16, I32, U32 = mybir.dt.float32, mybir.dt.float16, mybir.dt.int32, mybir.dt.uint32
    ALU = mybir.AluOpType
    ACT = mybir.ActivationFunctionType
    AX = mybir.AxisListType
    ds = bass.ds

    B, S, D = x.shape
    TOK = B * S
    NT = TOK // P
    CW = 512
    TPC = CW // P
    NC = TOK // CW
    KD = D // P
    TD = ctx_t.shape[0]
    KT = TD // 2
    H = wv_t.shape[1]
    E = router_w.shape[1]
    SH = shared_w1.shape[2]
    J = SH // P
    RH = routed_w1.shape[2]
    NRUN = (2 * TOK + E * (P - 1)) // P
    NBLK = -(-NRUN // 8) * 8
    WE = 2 * KD * RH + (RH // P) * D
    WH = WE // 2
    W3E = 2 * KD * RH
    WSH = 2 * KD * SH + J * D
    W3S = 2 * KD * SH
    WSCALE = 64.0
    LN_EPS = 1e-5
    INV_EPS = 1e8
    TINY = 1e-30

    x_tiles = x.rearrange("b s d -> (b s) d").rearrange("(t p) d -> p t d", p=P)
    out_tiles = out.rearrange("b s d -> (b s) d").rearrange("(t p) d -> p t d", p=P)

    xrow = nc.dram_tensor("xrow", (TOK, D), F32, kind="Internal").ap()
    xtd = nc.dram_tensor("xtd", (NC * P, 2 * KD * CW), F16, kind="Internal").ap()
    slot_token = nc.dram_tensor("slot_token", (P * NBLK, 1), I32, kind="Internal").ap()
    yrow = nc.dram_tensor("yrow", (NRUN * P, D), F32, kind="Internal").ap()
    xrow_tiles = xrow.rearrange("(t p) d -> p t d", p=P)

    ctx = ExitStack()
    with ctx:
        def sb(name, shape, dt):
            return ctx.enter_context(nc.sbuf_tensor(name, shape, dt))

        def sem(name):
            return ctx.enter_context(nc.semaphore(name))

        X = sb("X", [P, NT, D], F32)
        WR = sb("WR", [P, E * 2 * WE], F16)
        WS = sb("WS", [P, 2, WSH], F16)
        XTC = sb("XTC", [P, 2, 2, KD, CW], F16)
        GS = sb("GS", [P, 2, 2, CW], F16)
        SIL = sb("SIL", [P, 2, CW], F32)
        G = sb("G", [P, 2, CW], F32)
        STAGE = sb("STAGE", [P, 2, WE], F32)
        ROWS = sb("ROWS", [P, 8, D], F32)
        XG = ROWS[:, 0:4, :]
        YS = ROWS[:, 4:8, :]
        YG = ROWS[:, :, :].rearrange("p (t k) d -> p t k d", k=2)
        XTB = sb("XTB", [P, 2, 2, KD, P], F16)
        GT = sb("GT", [P, 2, 2, RH // P, P], F16)
        ident = sb("ident", [P, P], F32)
        before = sb("before", [P, P], F32)
        ones = sb("ones", [P, P], F32)
        wv = sb("wv", [P, KD, H], F32)
        wt = sb("wt", [KT, 2, H], F32)
        rw = sb("rw", [P, KD, E], F32)
        bvc = sb("bvc", [P, 1], F32)
        btc = sb("btc", [P, 1], F32)
        bias16 = sb("bias16", [P, E], F32)
        gates_in = sb("gates_in", [P, 2], F32)
        tg = sb("tg", [P, 2], F32)
        tgs = sb("tgs", [P, 1], F32)
        tbv = sb("tbv", [P, 1], F32)
        st = sb("st", [P, NT, 6], F32)
        mean1 = sb("mean1", [P, NT], F32)
        var1 = sb("var1", [P, NT], F32)
        rstd1 = sb("rstd1", [P, NT], F32)
        tmp1 = sb("tmp1", [P, NT], F32)
        tn = sb("tn", [P, NT], F32)
        rt = sb("rt", [P, NT], F32)
        vn = sb("vn", [P, TPC], F32)
        rv = sb("rv", [P, TPC], F32)
        st2 = sb("st2", [P, TPC, 6], F32)
        mv2 = sb("mv2", [P, TPC, 2], F32)
        ve2 = sb("ve2", [P, TPC], F32)
        sd2 = sb("sd2", [P, TPC], F32)
        rs2 = sb("rs2", [P, TPC], F32)
        posi = sb("posi", [P, 2, NT], I32)
        sloti = sb("sloti", [P, 2, NT], I32)
        gate = sb("gate", [P, 2, NT], F32)
        tokid = sb("tokid", [P, NT], I32)
        blk_word = sb("blk_word", [1, NBLK // 4], I32)
        row_iota = sb("row_iota", [P, 1], F32)
        pack = sb("pack", [P, NBLK // 4], F32)
        rev = sb("rev", [P, E], F32)
        idx = sb("idx", [P, NBLK], I32)
        zero_idx = sb("zero_idx", [P, NBLK], I32)
        ixs = sb("ixs", [P, 2, 2, 4], I32)
        tks = sb("tks", [P, 2, 4], I32)
        ixb = sb("ixb", [P, 4], I32)
        ixc = sb("ixc", [P, 4, 2], I32)

        arena_at = [0]

        def arena(shape):
            n = 2
            for s in shape:
                n *= s
            a = WR[:, arena_at[0]:arena_at[0] + n].bitcast(F32)
            arena_at[0] += n
            assert arena_at[0] <= E * 2 * WE
            if len(shape) == 2:
                a = a.rearrange("p (a b) -> p a b", a=shape[0])
            return a

        route_at = arena_at[0]
        CTX = arena([2, TOK])
        TT = arena([TOK])
        SHST = arena([WSH])
        SQT = arena([2, CW])
        XL = arena([TPC, D])
        XT = arena([KD, CW])
        VT = arena([CW])
        SQV = arena([CW])
        M = arena([TPC, D])
        DG = arena([TPC, P])
        stage_f = STAGE[:, :, :].rearrange("p a b -> p (a b)")
        XL2 = stage_f[:, 0:TPC * D].rearrange("p (a b) -> p a b", a=TPC)
        X2T = stage_f[:, TPC * D:TPC * D + KD * CW].rearrange("p (a b) -> p a b", a=KD)
        XHL = stage_f[:, TPC * D + KD * CW:TPC * D + 2 * KD * CW].bitcast(F16)\
            .rearrange("p (a k n) -> p a k n", a=2, k=KD)
        arena_at[0] = route_at
        SCS = arena([NT, E])
        SEL = arena([NT, E])
        EQ = arena([NT, E])
        RE = arena([NT, E])
        OH0 = arena([NT, E])
        OH1 = arena([NT, E])
        OHS = arena([NT, E])
        INCA = arena([NT // 2 + NT, E])
        INCB = arena([NT // 2 + NT, E])
        PA = arena([NT, E])
        PB = arena([NT, E])
        assert arena_at[0] <= 2 * 2 * TOK
        UNDER = -(-arena_at[0] // (2 * WE))
        OH = [OH0, OH1]
        m1 = sb("m1", [P, NT], F32)
        rm = sb("rm", [P, NT], F32)
        gsum = sb("gsum", [P, NT], F32)
        nf = sb("nf", [P, E], F32)
        ni = sb("ni", [P, E], I32)
        bi = sb("bi", [P, E], I32)
        bf = sb("bf", [P, E], F32)
        ea = sb("ea", [P, E // 2 + E], F32)
        eb = sb("eb", [P, E // 2 + E], F32)
        base_row = sb("base_row", [P, E], F32)
        lowi = sb("lowi", [P, 2, NT], I32)
        highi = sb("highi", [P, 2, NT], I32)
        ended = sb("ended", [P, E], F32)
        bef = sb("bef", [P, 1], F32)

        bank = [ctx.enter_context(nc.psum_tensor(f"bank{i}", [P, CW], F32)) for i in range(8)]

        HIDDEN = ((bank[2], bank[5]), (bank[0], bank[1]))
        SHARED_ROWS = (bank[3], bank[4])

        ld_text = sem("ld_text")
        ld_small = sem("ld_small")
        ld_ctx = [sem(f"ld_ctx{i}") for i in range(4)]
        ld_x = [sem(f"ld_x{i}") for i in range(4)]
        ld_shared = sem("ld_shared")
        ld_bias = sem("ld_bias")
        table_zeroed = sem("table_zeroed")
        pool_apart = sem("pool_apart")
        dve_apart = sem("dve_apart")
        c_mem = sem("c_mem")
        c_ready = sem("c_ready")
        ws_hi = sem("ws_hi")
        ws_lo = sem("ws_lo")
        tanh_done = sem("tanh_done")
        tgs_done = sem("tgs_done")
        t_mm = sem("t_mm")
        t_sq = sem("t_sq")
        t_norm = sem("t_norm")
        t_sqrt = sem("t_sqrt")
        rt_ready = sem("rt_ready")
        ve1_ready = sem("ve1_ready")
        sd1_ready = sem("sd1_ready")
        s1 = sem("s1")
        xln = sem("xln")
        t1 = sem("t1")
        xt = sem("xt")
        v_mm = sem("v_mm")
        v_sqr = sem("v_sqr")
        v_sq = sem("v_sq")
        dg = sem("dg")
        rb = sem("rb")
        n_mm = sem("n_mm")
        vn_sq = sem("vn_sq")
        rv_own = sem("rv_own")
        rv_ready = sem("rv_ready")
        m_ready = sem("m_ready")
        dot = sem("dot")
        added = sem("added")
        cos_done = sem("cos_done")
        s2 = sem("s2")
        s2_aggr = sem("s2_aggr")
        s2_rs = sem("s2_rs")
        ve2_ready = sem("ve2_ready")
        sd2_ready = sem("sd2_ready")
        xl2 = sem("xl2")
        t2 = sem("t2")
        x2f = sem("x2f")
        x2t = sem("x2t")
        hl2 = sem("hl2")
        r_mm = sem("r_mm")
        st_rows = sem("st_rows")
        st_xt = sem("st_xt")
        sig = sem("sig")
        r = sem("r")
        ohs_ready = sem("ohs_ready")
        rank = sem("rank")
        slots_ok = sem("slots_ok")
        routed_ok = sem("routed_ok")
        ix_copy = sem("ix_copy")
        scat = [sem(f"scat{i}") for i in range(2)]
        ld_idx = sem("ld_idx")
        ld_xtc = [sem(f"ld_xtc{i}") for i in range(2)]
        s_h = sem("s_h")
        s_sil = sem("s_sil")
        s_g = sem("s_g")
        s_ghi = sem("s_ghi")
        s_glo = sem("s_glo")
        s_y = sem("s_y")
        s_glo0 = sem("s_glo0")
        s_base = sem("s_base")
        products = sem("products")
        bef_ready = sem("bef_ready")
        word_mm = sem("word_mm")
        ld_stage = [sem(f"ld_stage{i}") for i in range(2)]
        w_hi = sem("w_hi")
        w_lo = sem("w_lo")
        xg = [sem(f"xg{i}") for i in range(4)]
        b_ix = sem("b_ix")
        b_tx = sem("b_tx")
        b_xhi = sem("b_xhi")
        b_xlo = sem("b_xlo")
        b_h = sem("b_h")
        b_sil = sem("b_sil")
        b_g = sem("b_g")
        b_tg = sem("b_tg")
        b_ghi = sem("b_ghi")
        b_glo = sem("b_glo")
        b_y = sem("b_y")
        b_yev = sem("b_yev")
        st_y = [sem(f"st_y{i}") for i in range(4)]
        c_ix = sem("c_ix")
        yg = [sem(f"yg{i}") for i in range(4)]
        cmb = sem("cmb")
        st_out = sem("st_out")

        NSMALL = 5 * 16
        WP = WSH // NC
        LAST = NC - 1
        HW = CW // 2
        NORM_TILES = ((0, NT // 4), (NT // 4, NT))
        NCA = NC // 2
        NSA = NCA * J
        POOL_FROM, POOL_TO = 2, J + 1

        def blocks_in_slot(u):
            return (NRUN - u + 3) // 4

        CUTS = [0] * (J + 2) + [2] * (J - 2) + [2, 1, 1, 1] * (J // 2)
        assert len(CUTS) == NSA and sum(CUTS) == 2 * E

        block = ctx.enter_context(nc.Block())

        @block.sync
        def _(sp):
            sp.dma_start(wt[:, :, :], wt_t.rearrange("(k p) h -> p k h", p=KT)).then_inc(ld_text, 16)
            sp.dma_start(btc[:, :], bt.rearrange("(p o) -> p o", o=1)).then_inc(ld_text, 16)
            ctx_k = ctx_t.rearrange("(k p) n -> p k n", p=KT)
            q = TOK // 4
            for i in range(4):
                sp.dma_start(CTX[0:KT, :, i * q:(i + 1) * q], ctx_k[:, :, i * q:(i + 1) * q]).then_inc(ld_ctx[i], 16)
                if i == 0:
                    sp.dma_start(bvc[:, :], bv.rearrange("(p o) -> p o", o=1)).then_inc(ld_small, 16)
                    sp.dma_start(gates_in[:, 0:1], g_xattn.partition_broadcast(P)).then_inc(ld_small, 16)
                    sp.dma_start(gates_in[:, 1:2], g_ffn.partition_broadcast(P)).then_inc(ld_small, 16)
                    sp.dma_start(wv[:, :, :], wv_t.rearrange("(k p) h -> p k h", p=P)).then_inc(ld_small, 16)
                    sp.dma_start(rw[:, :, :], router_w.rearrange("(k p) e -> p k e", p=P)).then_inc(ld_small, 16)
                    sp.dma_start(bias16[:, :], expert_bias.partition_broadcast(P)).then_inc(ld_bias, 16)
                sp.dma_start(X[:, i * (NT // 4):(i + 1) * (NT // 4), :],
                             x_tiles[:, i * (NT // 4):(i + 1) * (NT // 4), :]).then_inc(ld_x[i], 16)
            for w, at in ((shared_w1, 0), (shared_w2, KD * SH)):
                sp.dma_start(SHST[:, at:at + KD * SH].rearrange("p (k n) -> p k n", k=KD),
                             w[0].rearrange("(k p) n -> p k n", p=P)).then_inc(ld_shared, 16)
            sp.dma_start(SHST[:, W3S:WSH].rearrange("p (j n) -> p j n", j=J),
                         shared_w3[0].rearrange("(j p) n -> p j n", p=P)).then_inc(ld_shared, 16)
            sp.wait_ge(c_ready, 1)
            sp.dma_start(slot_token.rearrange("(p b) o -> p (b o)", p=P), zero_idx[:, :]).then_inc(table_zeroed, 16)

            def store_chunk(c):
                sp.wait_ge(xl2, c + 1)
                sp.dma_start(xrow_tiles[:, ds(c * TPC, TPC), :], XL2).then_inc(st_rows, 16)
                sp.wait_ge(hl2, c + 1)
                sp.dma_start(xtd[ds(c * P, P), :], XHL.rearrange("p a k n -> p (a k n)")).then_inc(st_xt, 16)

            with sp.Fori(0, 3) as c:
                store_chunk(c)
            sp.wait_ge(st_xt, 3 * 16)
            for u in range(2):
                sp.dma_start(XTC[:, u, :, :, :].rearrange("p a k n -> p (a k n)"),
                             xtd[u * P:(u + 1) * P, :]).then_inc(ld_xtc[u], 16)

            with sp.Fori(3, NC) as c:
                store_chunk(c)
            sp.wait_ge(st_rows, NC * 16)
            sp.wait_ge(st_xt, NC * 16)

            def stage(e, u):
                at = STAGE[:, u, 0:W3E].rearrange("p (k w n) -> p k w n", k=KD, w=2)
                for w, m in enumerate((routed_w1, routed_w2)):
                    sp.dma_start(at[:, :, w, :], m[ds(e, 1), :, :].rearrange("e (k p) n -> p (e k) n", p=P))\
                        .then_inc(ld_stage[u], 16)
                sp.dma_start(STAGE[:, u, W3E:WE].rearrange("p (k n) -> p k n", n=D),
                             routed_w3[ds(e, 1), :, :].rearrange("e (k p) n -> p (e k) n", p=P))\
                    .then_inc(ld_stage[u], 16)

            sp.wait_ge(r_mm, NC)
            for u in range(2):
                stage(UNDER + u, u)
            for first, last, expert in ((1, (E - UNDER) // 2, UNDER), ((E - UNDER) // 2, E // 2, UNDER - E)):
                with sp.Fori(first, last) as i:
                    for u in range(2):
                        sp.wait_ge(w_lo, i * 4 + (2 * u - 2))
                        stage(i * 2 + (u + expert), u)
            def store_block(i, u):
                sp.wait_ge(b_yev, i * 4 + (u + 1))
                sp.dma_start(yrow[ds(i * (4 * P) + u * P, P), :], YS[:, u, :]).then_inc(st_y[u], 16)

            with sp.Fori(0, NBLK // 4 - 1) as i:
                for u in range(4):
                    store_block(i, u)
            for b in range(NBLK - 4, NRUN):
                store_block(b // 4, b % 4)
            for u in range(2):
                sp.wait_ge(s_h, (NCA + 1 + u) * J)
                sp.dma_start(XTC[:, u, :, :, :].rearrange("p a k n -> p (a k n)"),
                             xtd[(NC - 2 + u) * P:(NC - 1 + u) * P, :]).then_inc(ld_xtc[u], 16)
            with sp.Fori(0, LAST) as c:
                sp.wait_ge(s_base, c + 1)
                sp.wait_ge(cmb, c * (2 * TPC) + 2 * TPC)
                sp.dma_start(out_tiles[:, ds(c * TPC, TPC), :], X[:, ds(c * TPC, TPC), :]).then_inc(st_out, 16)
            for h in range(2):
                sp.wait_ge(s_base, LAST + 1 + h)
                t = LAST * TPC + 2 * h
                sp.dma_start(out_tiles[:, t:t + 2, :], X[:, t:t + 2, :]).then_inc(st_out, 16)
            sp.wait_ge(st_out, (NC + 1) * 16)
            for u in range(4):
                sp.wait_ge(st_y[u], blocks_in_slot(u) * 16)

        @block.gpsimd
        def _(pool):
            pool.memset(ident[:, :], 0.0).then_inc(c_mem, 1)
            pool.memset(before[:, :], 1.0).then_inc(c_mem, 1)
            pool.memset(ones[:, :], 1.0)
            pool.memset(zero_idx[:, :], 0)
            pool.iota(tokid[:, :], pattern=[[P, NT]], base=0, channel_multiplier=1)
            pool.wait_ge(c_mem, 2)
            pool.affine_select(out=ident[:, :], in_=ident[:, :], compare_op=ALU.not_equal, fill=1.0,
                               base=0, pattern=[[-1, P]], channel_multiplier=1)
            pool.affine_select(out=before[:, :], in_=before[:, :], compare_op=ALU.is_ge, fill=0.0,
                               base=-1, pattern=[[1, P]], channel_multiplier=-1).then_inc(c_ready, 1)
            pool.iota(row_iota[:, :], pattern=[[0, 1]], base=0, channel_multiplier=1,
                      allow_small_or_imprecise_dtypes=True)
            pool.memset(pack[:, :], 0.0).then_inc(c_mem, 1)
            for k in range(6):
                pool.wait_ge(c_mem, 3 + k)
                pool.affine_select(out=pack[:, :], in_=pack[:, :], compare_op=ALU.not_equal, fill=float(E ** k),
                                   base=2 - k, pattern=[[-4, NBLK // 4]], channel_multiplier=1).then_inc(c_mem, 1)
            pool.iota(rev[:, :], pattern=[[-1, E]], base=E, channel_multiplier=0,
                      allow_small_or_imprecise_dtypes=True).then_inc(c_ready, 1)

            def diagonal(c, first=False):
                if first:
                    pool.wait_ge(rt_ready, 1)
                else:
                    pool.wait_ge(rb, c)
                pool.tensor_tensor(DG, ident[:, :].unsqueeze(1).to_broadcast([P, TPC, P]),
                                   rt[:, ds(c * TPC, TPC)].unsqueeze(2).to_broadcast([P, TPC, P]),
                                   ALU.mult).then_inc(dg, 1)

            def cut(c):
                pool.wait_ge(x2t, c * 2 + 2)
                pool.sem_inc(pool_apart, 1)
                pool.tensor_tensor(XHL[:, 1], X2T, XHL[:, 0], ALU.subtract).then_inc(hl2, 1)

            def add_attention(c):
                for u in range(2):
                    pool.wait_ge(cos_done, c * 2 + (u + 1))
                    xs = X[:, ds(c * TPC + 2 * u, 2), :]
                    pool.tensor_tensor(xs, xs, M[:, 2 * u:2 * u + 2, :], ALU.add).then_inc(added, 1)

            diagonal(0, True)
            diagonal(1)
            add_attention(0)
            diagonal(2)
            with pool.Fori(1, NC - 2) as c:
                add_attention(c)
                cut(c - 1)
                diagonal(c + 2)
            add_attention(NC - 2)
            cut(NC - 3)
            add_attention(NC - 1)
            cut(NC - 2)
            cut(NC - 1)

            for n in range(POOL_FROM, POOL_TO):
                pool.wait_ge(s_ghi, n + 1)
                pool.tensor_tensor(GS[:, n % 2, 1, :], G[:, n % 2, :], GS[:, n % 2, 0, :], ALU.subtract)\
                    .then_inc(s_glo0, 1)
                if n == 3:
                    pool.wait_ge(ohs_ready, 1)
                    pool.tensor_tensor(SEL, OH[0], SCS, ALU.mult)
                    pool.tensor_tensor(RE, OH[1], SCS, ALU.mult).then_inc(products, 1)

            pool.wait_ge(slots_ok, 1)
            pool.wait_ge(table_zeroed, 16)

            def scatter(i, u, first=False):
                t = i * 8 + 4 * u
                if not first:
                    pool.wait_ge(scat[u], i * (8 * 16))
                pool.sem_inc(pool_apart, 1)
                pool.tensor_copy(ixs[:, u], sloti[:, :, ds(t, 4)])
                pool.tensor_copy(tks[:, u, :], tokid[:, ds(t, 4)]).then_inc(ix_copy, 1)
                pool.wait_ge(ix_copy, i * 2 + (u + 1))
                pool.sem_inc(pool_apart, 1)
                for n in range(4):
                    for k in range(2):
                        pool.indirect_dma_start(out=slot_token, in_=tks[:, u, n:n + 1], in_offset=None,
                                                out_offset=bass.IndirectOffsetOnAxis(
                                                    ap=ixs[:, u, k, n:n + 1].bitcast(U32), axis=0))\
                            .then_inc(scat[u], 16)

            for u in range(2):
                scatter(0, u, True)
            with pool.Fori(1, NT // 8) as i:
                for u in range(2):
                    scatter(i, u)
            for u in range(2):
                pool.wait_ge(scat[u], NT // 8 * 8 * 16)
            pool.dma_start(idx[:, :], slot_token.rearrange("(p b) o -> p (b o)", p=P)).then_inc(ld_idx, 16)
            pool.wait_ge(ld_idx, 16)
            pool.wait_ge(st_rows, NC * 16)

            def fetch(i, u, first=False):
                b = i * 4 + u
                if not first:
                    pool.wait_ge(b_tx, i * 4 + (u - 3))
                pool.sem_inc(pool_apart, 1)
                pool.tensor_copy(ixb[:, u:u + 1], idx[:, ds(b, 1)]).then_inc(b_ix, 1)
                pool.wait_ge(b_ix, b + 1)
                pool.sem_inc(pool_apart, 1)
                pool.indirect_dma_start(out=XG[:, u, :], out_offset=None, in_=xrow,
                                        in_offset=bass.IndirectOffsetOnAxis(
                                            ap=ixb[:, u:u + 1].bitcast(U32), axis=0)).then_inc(xg[u], 16)

            for u in range(4):
                fetch(0, u, True)
            with pool.Fori(1, NBLK // 4 - 1) as i:
                for u in range(4):
                    fetch(i, u)
            for b in range(NBLK - 4, NRUN):
                fetch(b // 4, b % 4)

            pool.wait_ge(b_tx, NRUN)
            for u in range(4):
                pool.wait_ge(st_y[u], blocks_in_slot(u) * 16)

            def bring(i, u, first=False):
                t = i * 4 + u
                if not first:
                    pool.wait_ge(cmb, i * 8 + (2 * u - 6))
                pool.sem_inc(pool_apart, 1)
                pool.tensor_copy(ixc[:, u, :], posi[:, :, ds(t, 1)].rearrange("p a b -> p (a b)")).then_inc(c_ix, 1)
                pool.wait_ge(c_ix, t + 1)
                pool.sem_inc(pool_apart, 1)
                for k in range(2):
                    pool.indirect_dma_start(out=YG[:, u, k, :], out_offset=None, in_=yrow,
                                            in_offset=bass.IndirectOffsetOnAxis(
                                                ap=ixc[:, u, k:k + 1].bitcast(U32), axis=0))\
                        .then_inc(yg[u], 16)

            for u in range(4):
                bring(0, u, True)
            with pool.Fori(1, NT // 4) as i:
                for u in range(4):
                    bring(i, u)

        @block.scalar
        def _(act):
            act.preload_act_table(ACT.Sqrt)
            act.wait_ge(ld_text, 32)
            def text(c):
                u = c % 2
                act.wait_ge(t_mm, c + 1)
                act.activation(TT[:, c * CW:(c + 1) * CW], bank[u][:, :], ACT.Identity, bias=btc[:, :])
                if c >= 2:
                    act.wait_ge(t_norm, c - 1)
                act.activation(SQT[:, u, :], bank[u][:, :], ACT.Square, bias=btc[:, :]).then_inc(t_sq, 1)

            def deviation1(i):
                tiles = slice(*NORM_TILES[i])
                act.wait_ge(ve1_ready, i + 1)
                act.activation(tmp1[:, tiles], var1[:, tiles], ACT.Sqrt).then_inc(sd1_ready, 1)

            def lead(c, first=False):
                for u in range(2):
                    act.wait_ge(t1, c * 2 + (u + 1))
                    if u == 0 and not first:
                        act.wait_ge(v_mm, c)
                    act.activation(XT[:, :, u * D:(u + 1) * D],
                                   bank[3 + u][:, :].rearrange("p (k n) -> p k n", k=KD), ACT.Copy).then_inc(xt, 1)

            def lead_v(c, first=False):
                act.wait_ge(v_mm, c + 1)
                if not first:
                    act.wait_ge(n_mm, c)
                act.activation(SQV, bank[5][:, :], ACT.Square, bias=bvc[:, :]).then_inc(v_sqr, 1)
                if not first:
                    act.wait_ge(dot, c * 2)
                act.activation(VT, bank[5][:, :], ACT.Identity, bias=tbv[:, :], scale=tg[:, 0:1]).then_inc(v_sq, 1)

            def lead_norm(c, first=False):
                act.wait_ge(n_mm, c + 1)
                if not first:
                    act.wait_ge(rv_ready, c)
                act.activation(vn[:, :], bank[2][:, 0:TPC], ACT.Sqrt).then_inc(vn_sq, 1)

            def scales(c, first=False):
                act.wait_ge(rv_ready, c + 1)
                act.wait_ge(rb, c + 1)
                for u in range(2):
                    if not first:
                        act.wait_ge(added, c * 2 + (u - 1))
                    for i in range(2):
                        last = act.activation(M[:, 2 * u + i, :], bank[6][:, u * D:(u + 1) * D], ACT.Copy,
                                              scale=rv[:, 2 * u + i:2 * u + i + 1])
                    last.then_inc(m_ready, 1)

            def lag(c, first=False):
                for u in range(2):
                    act.wait_ge(t2, c * 2 + (u + 1))
                    if u == 0 and not first:
                        act.wait_ge(r_mm, c)
                        act.wait_ge(hl2, c)
                        act.wait_ge(st_xt, c * 16)
                    half = bank[3 + u][:, :].rearrange("p (k n) -> p k n", k=KD)
                    act.activation(X2T[:, :, u * D:(u + 1) * D], half, ACT.Copy).then_inc(x2f, 1)
                    act.activation(XHL[:, 0, :, u * D:(u + 1) * D], half, ACT.Copy).then_inc(x2t, 1)

            def weights_hi(c):
                act.activation(WS[:, 0, ds(c * WP, WP)], SHST[:, ds(c * WP, WP)], ACT.Copy, scale=WSCALE)\
                    .then_inc(ws_hi, 1)

            def deviation(c):
                act.wait_ge(ve2_ready, c + 1)
                act.activation(sd2[:, :], ve2[:, :], ACT.Sqrt).then_inc(sd2_ready, 1)

            text(0)
            act.wait_ge(ld_small, NSMALL)
            act.activation(tg[:, :], gates_in[:, :], ACT.Tanh).then_inc(tanh_done, 1)
            text(1)
            deviation1(0)
            text(2)
            text(3)
            text(4)
            lead(0, True)
            text(5)
            act.wait_ge(tgs_done, 1)
            lead_v(0, True)
            text(6)
            deviation1(1)
            text(7)
            lead(1)
            act.wait_ge(t_norm, NC)
            act.activation(tn[:, :], bank[2][:, 0:NT], ACT.Sqrt).then_inc(t_sqrt, 1)
            lead_norm(0, True)
            scales(0, True)
            lead_v(1)
            lead_norm(1)
            lead(2)
            deviation(0)
            act.wait_ge(ld_shared, 48)
            weights_hi(0)
            weights_hi(1)
            scales(1)
            lag(0, True)
            lead_v(2)
            lead_norm(2)
            deviation(1)
            weights_hi(2)
            with act.Fori(2, LAST) as c:
                lead(c + 1)
                scales(c)
                lag(c - 1)
                lead_v(c + 1)
                lead_norm(c + 1)
                deviation(c)
                weights_hi(c + 1)
            scales(LAST)
            lag(LAST - 1)
            deviation(LAST)

            def silu(n, j, first=False):
                a = j % 2
                act.wait_ge(s_h, n + 1)
                if not first:
                    act.wait_ge(s_g, n - 1)
                act.activation(SIL[:, a, :], HIDDEN[a][0][:, :], ACT.Silu, scale=1.0 / WSCALE).then_inc(s_sil, 1)

            def hidden_hi(n, j, first=False):
                a = j % 2
                act.wait_ge(s_g, n + 1)
                if not first:
                    act.wait_ge(s_y, n - 1)
                act.activation(GS[:, a, 0, :], G[:, a, :], ACT.Copy).then_inc(s_ghi, 1)

            def routed_hi(m, h):
                e = (m + UNDER) % E
                if h == 0:
                    act.wait_ge(ld_stage[m % 2], (m // 2 + 1) * 48)
                act.activation(WR[:, e * (2 * WE) + h * WH:e * (2 * WE) + (h + 1) * WH],
                               STAGE[:, m % 2, h * WH:(h + 1) * WH], ACT.Copy, scale=WSCALE).then_inc(w_hi, 1)

            act.preload_act_table(ACT.Silu)
            silu(0, 0, True)
            hidden_hi(0, 0, True)
            lag(LAST)
            silu(1, 1, True)
            hidden_hi(1, 1, True)
            act.preload_act_table(ACT.Sigmoid)
            act.wait_ge(r_mm, NC)
            act.activation(SCS.rearrange("p a b -> p (a b)"), bank[7][:, :], ACT.Sigmoid).then_inc(sig, 1)
            act.preload_act_table(ACT.Silu)
            half = 0
            for n in range(2, NSA):
                silu(n, n % J)
                hidden_hi(n, n % J)
                for p in range(half, half + CUTS[n]):
                    if p == 2 * (E - UNDER):
                        act.wait_ge(routed_ok, 1)
                    routed_hi(p // 2, p % 2)
                half += CUTS[n]
                if n % J == J - 1:
                    c = n // J
                    act.dma_start(XTC[:, c % 2, :, :, :].rearrange("p a k n -> p (a k n)"),
                                  xtd[(c + 2) * P:(c + 3) * P, :]).then_inc(ld_xtc[c % 2], 16)

            def x_hi(b, u, first=False):
                act.wait_ge(b_tx, b + 1)
                if not first:
                    act.wait_ge(b_h, b - 1)
                act.activation(XTB[:, u, 0], bank[2][:, 0:KD * P].rearrange("p (k n) -> p k n", k=KD), ACT.Copy)\
                    .then_inc(b_xhi, 1)

            def r_silu(b, u, first=False):
                act.wait_ge(b_h, b + 1)
                if not first:
                    act.wait_ge(b_g, b - 1)
                act.activation(SIL[:, u, 0:RH], bank[u][:, 0:RH], ACT.Silu, scale=1.0 / WSCALE).then_inc(b_sil, 1)

            def g_hi(b, u, first=False):
                act.wait_ge(b_tg, b + 1)
                if not first:
                    act.wait_ge(b_y, b - 1)
                act.activation(GT[:, u, 0], bank[3][:, 0:RH].rearrange("p (k n) -> p k n", k=RH // P), ACT.Copy)\
                    .then_inc(b_ghi, 1)

            act.wait_ge(s_g, NSA)
            x_hi(0, 0, True)
            x_hi(1, 1, True)
            for b in range(4):
                r_silu(b, b % 2, b < 2)
                if b >= 1:
                    g_hi(b - 1, (b - 1) % 2, b - 1 < 2)
                x_hi(b + 2, b % 2)
            with act.Fori(1, NBLK // 4 - 1) as i:
                for k in range(4):
                    b = i * 4 + k
                    r_silu(b, k % 2)
                    g_hi(b - 1, (k + 1) % 2)
                    x_hi(b + 2, k % 2)
            for b in range(NBLK - 4, NRUN):
                r_silu(b, b % 2)
                g_hi(b - 1, (b - 1) % 2)
                if b + 2 < NRUN:
                    x_hi(b + 2, b % 2)
            g_hi(NRUN - 1, (NRUN - 1) % 2)

            act.wait_ge(b_g, NRUN)
            with act.Fori(NCA // 2, NC // 2 - 1) as i:
                for k in range(2 * J):
                    silu(i * (2 * J) + k, k % J)
                    hidden_hi(i * (2 * J) + k, k % J)
            for n in range((NC - 2) * J, NC * J - 1):
                silu(n, n % J)
                hidden_hi(n, n % J)
            n, a = NC * J - 1, (J - 1) % 2
            act.wait_ge(s_h, n + 1)
            act.wait_ge(s_g, n - 1)
            for h in range(2):
                part = slice(h * HW, (h + 1) * HW)
                act.activation(SIL[:, a, part], HIDDEN[a][0][:, part], ACT.Silu, scale=1.0 / WSCALE).then_inc(s_sil, 1)
            act.wait_ge(s_y, n - 1)
            for h in range(2):
                part = slice(h * HW, (h + 1) * HW)
                act.wait_ge(s_g, n + 1 + h)
                act.activation(GS[:, a, 0, part], G[:, a, part], ACT.Copy).then_inc(s_ghi, 1)

        @block.vector
        def _(dve):
            own1 = [0]

            def link1(ins):
                own1[0] += 1
                ins.then_inc(s1, 1)
                dve.wait_ge(s1, own1[0])

            def statistics(g):
                dve.wait_ge(ld_x[g], 16)
                for t in range(g * (NT // 4), (g + 1) * (NT // 4)):
                    last = dve.bn_stats(st[:, t, :], X[:, t, :])
                link1(last)

            def variances(i):
                tiles = slice(*NORM_TILES[i])
                dve.tensor_tensor(mean1[:, tiles], st[:, tiles, 1], st[:, tiles, 4], ALU.add)
                dve.tensor_tensor(gsum[:, tiles], st[:, tiles, 1], st[:, tiles, 4], ALU.subtract)
                link1(dve.tensor_tensor(var1[:, tiles], st[:, tiles, 2], st[:, tiles, 5], ALU.add))
                dve.tensor_scalar(mean1[:, tiles], mean1[:, tiles], 0.5, None, ALU.mult)
                dve.tensor_scalar(gsum[:, tiles], gsum[:, tiles], 0.5, None, ALU.mult)
                link1(dve.tensor_scalar(var1[:, tiles], var1[:, tiles], 1.0 / D, LN_EPS, ALU.mult, ALU.add))
                link1(dve.tensor_tensor(rstd1[:, tiles], gsum[:, tiles], gsum[:, tiles], ALU.mult))
                dve.tensor_tensor(var1[:, tiles], var1[:, tiles], rstd1[:, tiles], ALU.add).then_inc(ve1_ready, 1)

            def inverse_deviations(i):
                tiles = slice(*NORM_TILES[i])
                dve.wait_ge(sd1_ready, i + 1)
                link1(dve.reciprocal(rstd1[:, tiles], tmp1[:, tiles]))

            def normalise(c, first=False):
                if not first:
                    dve.wait_ge(t1, c * 2)
                for k in range(TPC):
                    t = c * TPC + k
                    last = dve.tensor_scalar(XL[:, k, :], X[:, ds(t, 1), :].rearrange("p a n -> p (a n)"),
                                             mean1[:, ds(t, 1)], rstd1[:, ds(t, 1)], ALU.subtract, ALU.mult)
                last.then_inc(xln, 1)

            def inverse_norm(c, first=False):
                dve.wait_ge(vn_sq, c + 1)
                if not first:
                    dve.wait_ge(m_ready, c * 2)
                dve.tensor_scalar(vn[:, :], vn[:, :], TINY, None, ALU.max).then_inc(rv_own, 1)
                dve.wait_ge(rv_own, c + 1)
                dve.reciprocal(rv[:, :], vn[:, :]).then_inc(rv_ready, 1)

            def attend(c):
                for u in range(2):
                    dve.wait_ge(dot, c * 2 + (u + 1))
                    dve.wait_ge(m_ready, c * 2 + (u + 1))
                    for i in range(2):
                        last = dve.scalar_tensor_tensor(out=M[:, 2 * u + i, :], in0=M[:, 2 * u + i, :], scalar=INV_EPS,
                                                        in1=bank[u][:, i * D:(i + 1) * D],
                                                        op0=ALU.min, op1=ALU.mult)
                    last.then_inc(cos_done, 1)

            def statistics2(c):
                for u in range(2):
                    dve.wait_ge(added, c * 2 + (u + 1))
                    dve.sem_inc(dve_apart, 1)
                    for i in range(2):
                        last = dve.bn_stats(st2[:, 2 * u + i, :],
                                            X[:, ds(c * TPC + (2 * u + i), 1), :].rearrange("p a n -> p (a n)"))
                last.then_inc(s2, 1)
                dve.wait_ge(s2, c + 1)
                dve.sem_inc(dve_apart, 1)
                for i in range(TPC):
                    last = dve.bn_aggr(mv2[:, i, :], st2[:, i, :])
                last.then_inc(s2_aggr, 1)
                dve.wait_ge(s2_aggr, c + 1)
                dve.tensor_scalar(ve2[:, :], mv2[:, :, 1], LN_EPS, None, ALU.add).then_inc(ve2_ready, 1)

            def normalise2(c, first=False):
                dve.wait_ge(sd2_ready, c + 1)
                dve.reciprocal(rs2[:, :], sd2[:, :]).then_inc(s2_rs, 1)
                dve.wait_ge(s2_rs, c + 1)
                if not first:
                    dve.wait_ge(t2, c * 2)
                    dve.wait_ge(st_rows, c * 16)
                for k in range(TPC):
                    last = dve.tensor_scalar(XL2[:, k, :],
                                             X[:, ds(c * TPC + k, 1), :].rearrange("p a n -> p (a n)"),
                                             mv2[:, k, 0:1], rs2[:, k:k + 1], ALU.subtract, ALU.mult)
                last.then_inc(xl2, 1)

            def weights_lo(c):
                dve.wait_ge(ws_hi, c + 1)
                dve.scalar_tensor_tensor(out=WS[:, 1, ds(c * WP, WP)], in0=SHST[:, ds(c * WP, WP)], scalar=WSCALE,
                                         in1=WS[:, 0, ds(c * WP, WP)], op0=ALU.mult, op1=ALU.subtract)\
                    .then_inc(ws_lo, 1)

            statistics(0)
            variances(0)
            statistics(1)
            dve.wait_ge(tanh_done, 1)
            dve.tensor_scalar(tbv[:, :], bvc[:, :], tg[:, 0:1], None, ALU.mult)
            dve.tensor_scalar(tgs[:, :], tg[:, 1:2], 1.0 / WSCALE, None, ALU.mult).then_inc(tgs_done, 1)
            inverse_deviations(0)
            normalise(0, True)
            statistics(2)
            statistics(3)
            variances(1)
            normalise(1)
            inverse_deviations(1)
            dve.wait_ge(t_sqrt, 1)
            link1(dve.tensor_scalar(tn[:, :], tn[:, :], TINY, None, ALU.max))
            dve.reciprocal(rt[:, :], tn[:, :]).then_inc(rt_ready, 1)
            inverse_norm(0, True)
            attend(0)
            normalise(2)
            statistics2(0)
            inverse_norm(1)
            normalise2(0, True)
            weights_lo(0)
            with dve.Fori(1, LAST - 1) as c:
                attend(c)
                normalise(c + 2)
                weights_lo(c)
                statistics2(c)
                inverse_norm(c + 1)
                normalise2(c)
            weights_lo(LAST - 1)
            attend(LAST - 1)
            statistics2(LAST - 1)
            inverse_norm(LAST)
            normalise2(LAST - 1)
            weights_lo(LAST)
            attend(LAST)
            statistics2(LAST)
            normalise2(LAST)

            own = [0]

            def link(ins):
                own[0] += 1
                ins.then_inc(r, 1)
                dve.wait_ge(r, own[0])

            def over_tiles(a):
                return a.unsqueeze(1).to_broadcast([P, NT, E])

            def over_experts(a):
                return a.unsqueeze(2).to_broadcast([P, NT, E])

            PADT = NT // 2
            PADE = E // 2

            def rows_flat(a):
                return a.rearrange("p a b -> p (a b)")

            def prepare():
                dve.memset(INCA[:, 0:PADT, :], 0.0)
                dve.memset(INCB[:, 0:PADT, :], 0.0)
                dve.memset(ea[:, 0:PADE], 0.0)
                dve.memset(eb[:, 0:PADE], 0.0)

            def selection_scores():
                dve.wait_ge(ld_bias, 16)
                dve.wait_ge(c_ready, 2)
                dve.wait_ge(sig, 1)
                link(dve.tensor_tensor(SEL, SCS, over_tiles(bias16[:, :]), ALU.add))

            def choose():
                link(dve.tensor_reduce(m1[:, :], SEL, AX.X, ALU.max))
                link(dve.tensor_tensor(EQ, SEL, over_experts(m1[:, :]), ALU.is_equal))

            def choose_lowest(k):
                link(dve.tensor_tensor(RE, EQ, over_tiles(rev[:, :]), ALU.mult))
                link(dve.tensor_reduce(rm[:, :], RE, AX.X, ALU.max))
                link(dve.tensor_tensor(OH[k], over_experts(rm[:, :]), over_tiles(rev[:, :]), ALU.is_equal))

            def exclude_first():
                link(dve.scalar_tensor_tensor(out=SEL, in0=OH[0], scalar=-1e30, in1=SEL,
                                              op0=ALU.mult, op1=ALU.add))

            def gates():
                dve.wait_ge(products, 1)
                for k, chosen in enumerate((SEL, RE)):
                    link(dve.tensor_reduce(gsum[:, :], chosen, AX.X, ALU.add))
                    link(dve.tensor_scalar(gate[:, k, :], gsum[:, :], tgs[:, :], None, ALU.mult))

            def take_totals():
                dve.wait_ge(rank, 2)
                link(dve.tensor_copy(rows_flat(INCA[:, PADT:PADT + NT, :]), bank[7][:, :]))

            def sum_tiles(src, dst, step):
                link(dve.tensor_tensor(dst[:, PADT:PADT + NT, :], src[:, PADT:PADT + NT, :],
                                       src[:, PADT - step:PADT - step + NT, :], ALU.add))

            def sum_experts(inc):
                link(dve.tensor_scalar(ni[:, :], inc[:, PADT + NT - 1, :], float(P - 1), None, ALU.add))
                link(dve.tensor_scalar(bi[:, :], ni[:, :], 7, None, ALU.arith_shift_right))
                dve.tensor_copy(bf[:, :], bi[:, :])
                link(dve.tensor_copy(ea[:, PADE:PADE + E], bi[:, :]))
                es, ed = ea, eb
                step = 1
                while step < E:
                    link(dve.tensor_tensor(ed[:, PADE:PADE + E], es[:, PADE:PADE + E],
                                           es[:, PADE - step:PADE - step + E], ALU.add))
                    es, ed = ed, es
                    step *= 2
                ends = es[:, PADE:PADE + E]
                link(dve.tensor_tensor(nf[:, :], ends, bf[:, :], ALU.subtract))
                link(dve.tensor_scalar(base_row[:, :], nf[:, :], float(P), None, ALU.mult))
                return ends

            def slots_of_all(inc):
                link(dve.tensor_tensor(rows_flat(PA), rows_flat(inc[:, PADT:PADT + NT, :]), bank[7][:, :],
                                       ALU.subtract))
                link(dve.tensor_tensor(PB, PA, over_tiles(base_row[:, :]), ALU.add))
                link(dve.tensor_tensor(rows_flat(PA), rows_flat(PB), bank[6][:, :], ALU.add))

            def slots_of_choice(k):
                link(dve.tensor_tensor(EQ, OH[k], PA, ALU.mult))
                link(dve.tensor_reduce(gsum[:, :], EQ, AX.X, ALU.add))
                link(dve.tensor_copy(posi[:, k, :], gsum[:, :]))

            def table_slots():
                dve.tensor_scalar(lowi[:, :, :], posi[:, :, :], P - 1, None, ALU.bitwise_and)
                link(dve.tensor_scalar(highi[:, :, :], posi[:, :, :], 7, None, ALU.arith_shift_right))
                dve.scalar_tensor_tensor(out=sloti[:, :, :], in0=lowi[:, :, :], scalar=float(NBLK),
                                         in1=highi[:, :, :], op0=ALU.mult, op1=ALU.add).then_inc(slots_ok, 1)

            def block_experts(ends):
                link(dve.tensor_scalar(ended[:, :], ends, row_iota[:, :], None, ALU.is_le))
                link(dve.tensor_reduce(bef[:, :], ended[:, :], AX.X, ALU.add))
                dve.tensor_scalar(bef[:, :], bef[:, :], float(E - 1), None, ALU.min).then_inc(bef_ready, 1)

            def block_words():
                dve.wait_ge(word_mm, 1)
                dve.tensor_copy(blk_word[:, :], bank[6][0:1, 0:NBLK // 4]).then_inc(routed_ok, 1)

            def add_shared(c, combined=None):
                dve.wait_ge(s_y, c * J + J)
                if combined is not None:
                    dve.wait_ge(cmb, combined)
                for k in range(TPC):
                    xs = X[:, ds(c * TPC + k, 1), :].rearrange("p a n -> p (a n)")
                    last = dve.scalar_tensor_tensor(out=xs, in0=SHARED_ROWS[k // 2][:, (k % 2) * D:(k % 2 + 1) * D],
                                                    scalar=tgs[:, :], in1=xs, op0=ALU.mult, op1=ALU.add)
                last.then_inc(s_base, 1)

            def add_routed(t, slot, count, chunks):
                dve.wait_ge(yg[slot], count)
                dve.wait_ge(s_base, chunks)
                xs = X[:, ds(t, 1), :].rearrange("p a n -> p (a n)")
                for k in range(2):
                    if k == 1:
                        dve.wait_ge(cmb, t * 2 + 1)
                    dve.scalar_tensor_tensor(out=xs, in0=YG[:, slot, k, :], scalar=gate[:, k, ds(t, 1)],
                                             in1=xs, op0=ALU.mult, op1=ALU.add).then_inc(cmb, 1)

            def gate_hidden(n, j, first=False, pool=None):
                a = j % 2
                dve.wait_ge(s_sil, n + 1)
                if not first:
                    dve.wait_ge(s_ghi, n - 1)
                if pool is not None:
                    dve.wait_ge(s_glo0, pool)
                dve.scalar_tensor_tensor(out=G[:, a, :], in0=HIDDEN[a][1][:, :], scalar=1.0 / WSCALE,
                                         in1=SIL[:, a, :], op0=ALU.mult, op1=ALU.mult).then_inc(s_g, 1)

            def hidden_lo(n, j):
                a = j % 2
                dve.wait_ge(s_ghi, n + 1)
                dve.tensor_tensor(GS[:, a, 1, :], G[:, a, :], GS[:, a, 0, :], ALU.subtract).then_inc(s_glo, 1)

            def routed_lo(m, h):
                at = (m + UNDER) % E * (2 * WE) + h * WH
                dve.wait_ge(w_hi, m * 2 + (h + 1))
                dve.scalar_tensor_tensor(out=WR[:, at + WE:at + WE + WH], in0=STAGE[:, m % 2, h * WH:(h + 1) * WH],
                                         scalar=WSCALE, in1=WR[:, at:at + WH], op0=ALU.mult, op1=ALU.subtract)\
                    .then_inc(w_lo, 1)

            prepare()
            gate_hidden(0, 0, True)
            hidden_lo(0, 0)
            gate_hidden(1, 1, True)
            hidden_lo(1, 1)
            selection_scores()
            choose()
            gate_hidden(2, 0)
            choose_lowest(0)
            exclude_first()
            gate_hidden(3, 1)
            choose()
            choose_lowest(1)
            dve.tensor_tensor(OHS, OH[0], OH[1], ALU.add).then_inc(ohs_ready, 1)
            gate_hidden(4, 0, pool=1)
            gate_hidden(5, 1, pool=2)
            take_totals()
            sum_tiles(INCA, INCB, 1)
            sum_tiles(INCB, INCA, 2)
            sum_tiles(INCA, INCB, 4)
            gate_hidden(6, 0, pool=3)
            sum_tiles(INCB, INCA, 8)
            sum_tiles(INCA, INCB, 16)
            ends = sum_experts(INCB)
            gate_hidden(7, 1, pool=4)
            slots_of_all(INCB)
            block_experts(ends)
            gate_hidden(8, 0, pool=5)
            add_shared(0)
            slots_of_choice(0)
            slots_of_choice(1)
            table_slots()
            gate_hidden(9, 1, pool=6)
            hidden_lo(9, 1)
            gates()
            block_words()
            half = 0
            for n in range(POOL_TO + 1, NSA):
                gate_hidden(n, n % J, pool=n - 1 - POOL_FROM if n < POOL_TO + 2 else None)
                if n % J == 0:
                    add_shared(n // J - 1)
                hidden_lo(n, n % J)
                for p in range(half, half + CUTS[n]):
                    routed_lo(p // 2, p % 2)
                half += CUTS[n]

            def x_lo(b, u):
                dve.wait_ge(b_xhi, b + 1)
                dve.tensor_tensor(XTB[:, u, 1], bank[2][:, 0:KD * P].rearrange("p (k n) -> p k n", k=KD),
                                  XTB[:, u, 0], ALU.subtract).then_inc(b_xlo, 1)

            def gated(b, u, first=False):
                dve.wait_ge(b_sil, b + 1)
                if not first:
                    dve.wait_ge(b_tg, b - 1)
                dve.scalar_tensor_tensor(out=G[:, u, 0:RH], in0=bank[u][:, RH:2 * RH], scalar=1.0 / WSCALE,
                                         in1=SIL[:, u, 0:RH], op0=ALU.mult, op1=ALU.mult).then_inc(b_g, 1)

            def g_lo(b, u):
                dve.wait_ge(b_ghi, b + 1)
                dve.tensor_tensor(GT[:, u, 1], bank[3][:, 0:RH].rearrange("p (k n) -> p k n", k=RH // P),
                                  GT[:, u, 0], ALU.subtract).then_inc(b_glo, 1)

            def rows(b, i, u, first=False):
                dve.wait_ge(b_y, b + 1)
                if not first:
                    dve.wait_ge(st_y[u], i * 16)
                dve.tensor_copy(YS[:, u, :], bank[4][:, 0:D]).then_inc(b_yev, 1)

            x_lo(0, 0)
            x_lo(1, 1)
            add_shared(NCA - 1)
            for b in range(4):
                gated(b, b % 2, b < 2)
                if b >= 1:
                    g_lo(b - 1, (b - 1) % 2)
                x_lo(b + 2, b % 2)
                if b >= 2:
                    rows(b - 2, 0, b - 2, True)
            gated(4, 0)
            g_lo(3, 1)
            x_lo(6, 0)
            rows(2, 0, 2, True)
            gated(5, 1)
            g_lo(4, 0)
            x_lo(7, 1)
            rows(3, 0, 3, True)
            with dve.Fori(1, NBLK // 4 - 2) as i:
                for k in range(4):
                    b = i * 4 + (k + 2)
                    gated(b, k % 2)
                    g_lo(b - 1, (k + 1) % 2)
                    x_lo(b + 2, k % 2)
                    rows(b - 2, i, k)
            for b in range(NBLK - 6, NRUN):
                gated(b, b % 2)
                g_lo(b - 1, (b - 1) % 2)
                if b + 2 < NRUN:
                    x_lo(b + 2, b % 2)
                rows(b - 2, (b - 2) // 4, (b - 2) % 4)
            g_lo(NRUN - 1, (NRUN - 1) % 2)
            rows(NRUN - 2, (NRUN - 2) // 4, (NRUN - 2) % 4)
            dve.wait_ge(b_tg, NRUN)
            gate_hidden(NSA, 0)
            hidden_lo(NSA, 0)
            rows(NRUN - 1, (NRUN - 1) // 4, (NRUN - 1) % 4)

            tiles_of_step = [0, 0, 0, 0, 2, 1, 2, 1, 0, 2, 1, 2, 1, 2, 2, 0]
            assert len(tiles_of_step) == 2 * J and sum(tiles_of_step) == NT // 2

            def two_chunks(i, first=False, last=False):
                done = 0
                for k in range(1 if first else 0, 2 * J - 1 if last else 2 * J):
                    gate_hidden(i * (2 * J) + k, k % J)
                    if k % J == 0:
                        add_shared(i * 2 + (k // J - 1), combined=i * (4 * J) + (2 * done - 2 * NSA))
                    for q in range(done, done + tiles_of_step[k]):
                        add_routed(i * (2 * J) + (q - NSA), q % 4, i * (4 * 32) + (q // 4 + 1 - NSA // 4) * 32,
                                   i * 2 + k // J)
                    done += tiles_of_step[k]
                    hidden_lo(i * (2 * J) + k, k % J)

            two_chunks(NCA // 2, first=True)
            two_chunks(NC // 2 - 1, last=True)
            n, a = NC * J - 1, (J - 1) % 2
            dve.wait_ge(s_ghi, n - 1)
            for h in range(2):
                part = slice(h * HW, (h + 1) * HW)
                dve.wait_ge(s_sil, n + 1 + h)
                dve.scalar_tensor_tensor(out=G[:, a, part], in0=HIDDEN[a][1][:, part], scalar=1.0 / WSCALE,
                                         in1=SIL[:, a, part], op0=ALU.mult, op1=ALU.mult).then_inc(s_g, 1)
            for h in range(2):
                part = slice(h * HW, (h + 1) * HW)
                dve.wait_ge(s_ghi, n + 1 + h)
                dve.tensor_tensor(GS[:, a, 1, part], G[:, a, part], GS[:, a, 0, part], ALU.subtract).then_inc(s_glo, 1)
            dve.wait_ge(cmb, 2 * NT)
            for h in range(2):
                dve.wait_ge(s_y, n + 1 + h)
                for k in (2 * h, 2 * h + 1):
                    xs = X[:, LAST * TPC + k, :]
                    last = dve.scalar_tensor_tensor(out=xs, in0=SHARED_ROWS[h][:, (k % 2) * D:(k % 2 + 1) * D],
                                                    scalar=tgs[:, :], in1=xs, op0=ALU.mult, op1=ALU.add)
                last.then_inc(s_base, 1)

        @block.tensor
        def _(pe):
            pe.wait_ge(ld_text, 32)
            pe.wait_ge(c_ready, 1)

            def t_norms(c):
                u = c % 2
                pe.wait_ge(t_sq, c + 1)
                for k in range(TPC):
                    last = pe.matmul(bank[2][:, c * TPC + k:c * TPC + k + 1], SQT[:, u, k * P:(k + 1) * P],
                                     ones[:, 0:1], start=True, stop=True)
                last.then_inc(t_norm, 1)

            def text(c):
                u = c % 2
                if u == 0:
                    pe.wait_ge(ld_ctx[c // 2], 16)
                if c >= 2:
                    pe.wait_ge(t_sq, c - 1)
                for k in range(2):
                    last = pe.matmul(bank[u][:, :], wt[:, k, :], CTX[0:KT, k, c * CW:(c + 1) * CW],
                                     start=(k == 0), stop=(k == 1))
                last.then_inc(t_mm, 1)
                if c >= 1:
                    t_norms(c - 1)

            def transpose1(c, first=False, after_t2=True):
                pe.wait_ge(xln, c + 1)
                for u in range(2):
                    if not first:
                        if after_t2:
                            pe.wait_ge(x2t, c * 2 + (u - 5))
                        else:
                            pe.wait_ge(xt, c * 2 + (u - 1))
                    for k in range(KD):
                        for i in range(2):
                            last = pe.transpose(bank[3 + u][:, k * D + i * P:k * D + (i + 1) * P],
                                                XL[:, 2 * u + i, k * P:(k + 1) * P], ident[:, :])
                    last.then_inc(t1, 1)

            def values(c, first=False):
                pe.wait_ge(xt, c * 2 + 2)
                if not first:
                    pe.wait_ge(v_sq, c)
                for k in range(KD):
                    last = pe.matmul(bank[5][:, :], wv[:, k, :], XT[:, k, :], start=(k == 0), stop=(k == KD - 1))
                last.then_inc(v_mm, 1)

            def row_norms(c, first=False):
                pe.wait_ge(dg, c + 1)
                if not first:
                    pe.wait_ge(m_ready, c * 2)
                pe.matmul(bank[6][:, :], ones[:, :], DG.rearrange("p a b -> p (a b)"), start=True, stop=True)\
                    .then_inc(rb, 1)

            def v_norms(c, first=False):
                pe.wait_ge(v_sqr, c + 1)
                if first:
                    pe.wait_ge(t_sqrt, 1)
                else:
                    pe.wait_ge(vn_sq, c)
                for k in range(TPC):
                    last = pe.matmul(bank[2][:, k:k + 1], SQV[:, k * P:(k + 1) * P], ones[:, 0:1],
                                     start=True, stop=True)
                last.then_inc(n_mm, 1)

            def dots(c, first=False):
                pe.wait_ge(v_sq, c + 1)
                for u in range(2):
                    if not first:
                        pe.wait_ge(cos_done, c * 2 + (u - 1))
                    for i in range(2):
                        last = pe.matmul(bank[u][:, i * D:(i + 1) * D], VT[:, (2 * u + i) * P:(2 * u + i + 1) * P],
                                         TT[:, ds(c * CW + u * S, S)], start=True, stop=True)
                    last.then_inc(dot, 1)

            def transpose2(c, tail=False):
                pe.wait_ge(xl2, c + 1)
                for u in range(2):
                    if tail:
                        pe.wait_ge(x2t, c * 2 + (u - 1))
                    else:
                        pe.wait_ge(xt, c * 2 + (u + 5))
                    for k in range(KD):
                        for i in range(2):
                            last = pe.transpose(bank[3 + u][:, k * D + i * P:k * D + (i + 1) * P],
                                                XL2[:, 2 * u + i, k * P:(k + 1) * P], ident[:, :])
                    last.then_inc(t2, 1)

            def router(c, u):
                pe.wait_ge(x2f, c * 2 + (u + 1))
                for i in (2 * u, 2 * u + 1):
                    for k in range(KD):
                        last = pe.matmul(bank[7][:, ds(c * (TPC * E) + i * E, E)], X2T[:, k, i * P:(i + 1) * P],
                                         rw[:, k, :], start=(k == 0), stop=(k == KD - 1))
                if u == 1:
                    last.then_inc(r_mm, 1)

            for c in range(5):
                text(c)
            pe.wait_ge(ld_small, NSMALL)
            transpose1(0, True)
            text(5)
            values(0, True)
            text(6)
            text(7)
            transpose1(1, after_t2=False)
            t_norms(LAST)
            dots(0, True)
            v_norms(0, True)
            row_norms(0, True)
            values(1)
            row_norms(1)
            v_norms(1)
            transpose1(2, after_t2=False)
            dots(1)
            values(2)
            transpose2(0)
            router(0, 0)
            row_norms(2)
            v_norms(2)
            with pe.Fori(2, LAST) as c:
                transpose1(c + 1)
                router(c - 2, 1)
                dots(c)
                transpose2(c - 1)
                values(c + 1)
                router(c - 1, 0)
                row_norms(c + 1)
                v_norms(c + 1)
            dots(LAST)
            router(LAST - 2, 1)
            transpose2(LAST - 1, tail=True)

            def ranks():
                pe.wait_ge(ohs_ready, 1)
                pe.matmul(bank[6][:, :], before[:, :], OHS.rearrange("p a b -> p (a b)"), start=True, stop=True)\
                    .then_inc(rank, 1)
                pe.wait_ge(sig, 1)
                pe.matmul(bank[7][:, :], ones[:, :], OHS.rearrange("p a b -> p (a b)"), start=True, stop=True)\
                    .then_inc(rank, 1)

            def words():
                pe.wait_ge(bef_ready, 1)
                pe.matmul(bank[6][0:1, 0:NBLK // 4], bef[0:NBLK, :], pack[0:NBLK, :], start=True, stop=True)\
                    .then_inc(word_mm, 1)

            def hidden(n, u, j, first=False, load=None, products=(0, 1)):
                a = j % 2
                if load is not None:
                    pe.wait_ge(ld_xtc[u], load)
                if not first:
                    pe.wait_ge(s_g, n - 1)
                for w in products:
                    acc = HIDDEN[a][w]
                    for k in range(KD):
                        at = (w * KD + k) * SH + j * P
                        for m, (wx, xx) in enumerate(((0, 0), (0, 1), (1, 0))):
                            last = pe.matmul(acc[:, :], WS[:, wx, at:at + P], XTC[:, u, xx, k, :],
                                             start=(k == 0 and m == 0), stop=(k == KD - 1 and m == 2))
                if 1 in products:
                    last.then_inc(s_h, 1)

            def shared_rows(n, j, evacuated=None, half=None):
                a = j % 2
                if isinstance(n, int) and POOL_FROM <= n < POOL_TO:
                    pe.wait_ge(s_glo0, n + 1 - POOL_FROM)
                elif isinstance(n, int) and n < POOL_FROM:
                    pe.wait_ge(s_glo, n + 1)
                else:
                    pe.wait_ge(s_glo, n + (1 - (POOL_TO - POOL_FROM) + (half or 0)))
                if evacuated is not None:
                    pe.wait_ge(s_base, evacuated)
                at = W3S + j * D
                for i in range(TPC) if half is None else (2 * half, 2 * half + 1):
                    acc = SHARED_ROWS[i // 2][:, (i % 2) * D:(i % 2 + 1) * D]
                    for m, (gx, wx) in enumerate(((0, 0), (0, 1), (1, 0))):
                        last = pe.matmul(acc, GS[:, a, gx, i * P:(i + 1) * P], WS[:, wx, at:at + D],
                                         start=(j == 0 and m == 0 and i % 2 == 0), stop=(j == J - 1 and m == 2),
                                         skip_group_check=True)
                last.then_inc(s_y, 1)

            def two_chunks(i, start=0, with_routing=False):
                for k in range(start, 2 * J):
                    hidden(i * (2 * J) + k, k // J, k % J, load=(i * 16 + 16) if k % J == 0 else None)
                    if with_routing and k == 5:
                        ranks()
                    if with_routing and k == 9:
                        words()
                    shared_rows(i * (2 * J) + (k - 1), (k - 1) % J, i * 2 + k // J if k % J == 1 else None)

            pe.wait_ge(ws_lo, NC)
            pe.wait_ge(v_sq, NC)
            pe.wait_ge(vn_sq, NC)
            hidden(0, 0, 0, first=True, load=16)
            for u in range(2):
                router(LAST - 1, u)
            pe.wait_ge(cos_done, 2 * NC)
            hidden(1, 0, 1, first=True, products=(0,))
            transpose2(LAST, tail=True)
            hidden(1, 0, 1, first=True, products=(1,))
            hidden(2, 0, 2)
            for u in range(2):
                router(LAST, u)
            pe.wait_ge(x2t, 2 * NC)
            shared_rows(0, 0)
            shared_rows(1, 1)
            two_chunks(0, start=3, with_routing=True)
            with pe.Fori(1, NCA // 2) as i:
                two_chunks(i)
            def experts(i):
                w = pe.value_load(blk_word[0:1, ds(i, 1)])
                return [(w >> (4 * k)) & (E - 1) for k in range(6)]

            def weights(e, at, n):
                return WR[:, :].rearrange("p (e n) -> p e n", e=E)[:, ds(e, 1), at:at + n]\
                    .rearrange("p a n -> p (a n)")

            def block_transpose(b, slot, count):
                pe.wait_ge(xg[slot], count)
                if not (isinstance(b, int) and b == 0):
                    pe.wait_ge(b_xlo, b)
                for k in range(KD):
                    last = pe.transpose(bank[2][:, k * P:(k + 1) * P], XG[:, slot, k * P:(k + 1) * P], ident[:, :])
                last.then_inc(b_tx, 1)

            def block_hidden(b, u, e, first=False):
                pe.wait_ge(b_xlo, b + 1)
                if not first:
                    pe.wait_ge(b_g, b - 1)
                for k in range(KD):
                    hi = weights(e, k * 2 * RH, 2 * RH)
                    lo = weights(e, WE + k * 2 * RH, 2 * RH)
                    for m, (xx, w) in enumerate(((0, hi), (0, lo), (1, hi))):
                        last = pe.matmul(bank[u][:, :], XTB[:, u, xx, k, :], w,
                                         start=(k == 0 and m == 0), stop=(k == KD - 1 and m == 2))
                last.then_inc(b_h, 1)

            def hidden_transpose(b, u, first=False):
                pe.wait_ge(b_g, b + 1)
                if not first:
                    pe.wait_ge(b_glo, b)
                for k in range(RH // P):
                    last = pe.transpose(bank[3][:, k * P:(k + 1) * P], G[:, u, k * P:(k + 1) * P], ident[:, :])
                last.then_inc(b_tg, 1)

            def block_rows(b, u, e, first=False):
                pe.wait_ge(b_glo, b + 1)
                if not first:
                    pe.wait_ge(b_yev, b)
                for k in range(RH // P):
                    hi = weights(e, W3E + k * D, D)
                    lo = weights(e, WE + W3E + k * D, D)
                    for m, (gx, w) in enumerate(((0, hi), (0, lo), (1, hi))):
                        last = pe.matmul(bank[4][:, 0:D], GT[:, u, gx, k, :], w,
                                         start=(k == 0 and m == 0), stop=(k == RH // P - 1 and m == 2))
                last.then_inc(b_y, 1)

            pe.wait_ge(s_g, NSA)
            block_transpose(0, 0, 16)
            shared_rows(NSA - 1, J - 1)
            block_transpose(1, 1, 16)
            pe.wait_ge(routed_ok, 1)
            pe.wait_ge(w_lo, 2 * E)
            es = experts(0)
            for b in range(4):
                block_hidden(b, b % 2, es[b + 2], b < 2)
                if b == 1:
                    pe.wait_ge(s_base, NCA)
                if b >= 1:
                    hidden_transpose(b - 1, (b - 1) % 2, b == 1)
                block_transpose(b + 2, (b + 2) % 4, 16 * ((b + 2) // 4 + 1))
                if b >= 2:
                    block_rows(b - 2, b % 2, es[b], b == 2)
            with pe.Fori(0, NBLK // 8 - 1) as i:
                for h in range(2):
                    es = experts(i * 2 + (h + 1))
                    for k in range(4):
                        b = i * 8 + (4 + 4 * h + k)
                        block_hidden(b, k % 2, es[k + 2])
                        hidden_transpose(b - 1, (k + 1) % 2)
                        block_transpose(b + 2, (k + 2) % 4, i * 32 + 16 * ((k + 2) // 4 + h + 2))
                        block_rows(b - 2, k % 2, es[k])
            es = experts(NBLK // 4 - 1)
            for k in range(NRUN - (NBLK - 4)):
                b = NBLK - 4 + k
                block_hidden(b, b % 2, es[k + 2])
                hidden_transpose(b - 1, (b - 1) % 2)
                if b + 2 < NRUN:
                    block_transpose(b + 2, (b + 2) % 4, 16 * ((b + 2) // 4 + 1))
                block_rows(b - 2, b % 2, es[k])
            hidden(NSA, 0, 0, load=NCA // 2 * 16 + 16)
            hidden_transpose(NRUN - 1, (NRUN - 1) % 2)
            block_rows(NRUN - 2, (NRUN - 2) % 2, es[NRUN - 2 - (NBLK - 6)])
            hidden(NSA + 1, 0, 1)
            block_rows(NRUN - 1, (NRUN - 1) % 2, es[NRUN - 1 - (NBLK - 6)])

            pe.wait_ge(b_yev, NRUN)
            shared_rows(NSA, 0)
            two_chunks(NCA // 2, start=2)
            two_chunks(NC // 2 - 1)
            for h in range(2):
                shared_rows(NC * J - 1, J - 1, half=h)


_INS = ["x", "ctx_t", "g_xattn", "g_ffn", "wv_t", "bv", "wt_t", "bt", "router_w", "expert_bias",
        "shared_w1", "shared_w2", "shared_w3", "routed_w1", "routed_w2", "routed_w3"]


def kernel(x, ctx_768, g_xattn, g_ffn, L0_xattn_Wv, L0_xattn_bv, L0_xattn_Wt, L0_xattn_bt, L0_ffn_router_w,
           L0_ffn_expert_bias, L0_ffn_shared_w1, L0_ffn_shared_w2, L0_ffn_shared_w3, L0_ffn_routed_w1,
           L0_ffn_routed_w2, L0_ffn_routed_w3):
    import numpy as np
    import concourse.bacc as bacc
    from concourse.bass_utils import run_bass_kernel_spmd

    ctx_768 = np.asarray(ctx_768)
    given = [x, ctx_768.transpose(2, 0, 1).reshape(ctx_768.shape[2], -1), g_xattn, g_ffn,
             np.asarray(L0_xattn_Wv).T, L0_xattn_bv, np.asarray(L0_xattn_Wt).T, L0_xattn_bt,
             L0_ffn_router_w, L0_ffn_expert_bias, L0_ffn_shared_w1, L0_ffn_shared_w2, L0_ffn_shared_w3,
             L0_ffn_routed_w1, L0_ffn_routed_w2, L0_ffn_routed_w3]
    nc = bacc.Bacc("TRN2", target_bir_lowering=False, num_devices=1)
    arrays, args = {}, []
    for name, a in zip(_INS, given):
        a = np.ascontiguousarray(a)
        arrays[f"in_{name}"] = a
        args.append(nc.dram_tensor(f"in_{name}", a.shape, mybir.dt.from_np(a.dtype), kind="ExternalInput").ap())
    args.append(nc.dram_tensor("out", tuple(x.shape), mybir.dt.float32, kind="ExternalOutput").ap())
    flamingo_block(nc, *args)
    done = run_bass_kernel_spmd(nc, [arrays], core_ids=[0])
    return done.results[0]["out"]
```
